# Optimizing a Trainium2 kernel written in Bass

```python
import numpy as np
import jax
import jax.numpy as jnp

def _softmax(x, axis=-1):
    return jax.nn.softmax(x, axis=axis)

def _gelu(x):
    return jax.nn.gelu(x, approximate=True)

def _silu(x):
    return jax.nn.silu(x)

def _sigmoid(x):
    return jax.nn.sigmoid(x)

def _layernorm(x, axis=-1, eps=1e-05):
    m = jnp.mean(x, axis=axis, keepdims=True)
    v = jnp.var(x, axis=axis, keepdims=True)
    return (x - m) / jnp.sqrt(v + eps)

def _scatter_add(tgt, idx, src, axis=0):
    return tgt.at[idx].add(src)

def _segment_sum(src, seg, n):
    return jax.ops.segment_sum(src, seg, n)
kernel_name = 'mk_cond_seq_d4_seqx_r8_0c1cfa'

def setup_inputs(seed: int=0):
    np.random.seed(seed)
    _w = jnp.asarray

    def _rec_inputs():
        import jax
        import jax.numpy as jnp
        _rk = jax.random.key(seed)
        x = -0.0003929 + 0.9999 * jax.random.normal(jax.random.fold_in(_rk, 1), (2, 512, 128), jnp.float32)
        _lenS = 512 - jax.random.randint(jax.random.fold_in(_rk, 7), (2,), 0, max(1, 512 // 4) + 1, jnp.int32)
        _lenS2 = 512 - jax.random.randint(jax.random.fold_in(_rk, 8), (2,), 0, max(1, 512 // 4) + 1, jnp.int32)
        cond_1024 = 0.0061147 + 1.02565 * jax.random.normal(jax.random.fold_in(_rk, 11), (2, 128), jnp.float32)
        fside_1x1xSxS_0 = 3.76506e-05 + 0.0999991 * jax.random.normal(jax.random.fold_in(_rk, 12), (1, 1, 512, 512), jnp.float32)
        return (x, cond_1024, fside_1x1xSxS_0)
    x, cond_1024, fside_1x1xSxS_0 = _rec_inputs()

    def _L0_cond_setup():
        import jax, jax.numpy as jnp
        import numpy as np
        H = 16
        EPS = 1e-05

        def layer_norm(x, g, b):
            mu = jnp.mean(x, axis=-1, keepdims=True)
            var = jnp.var(x, axis=-1, keepdims=True)
            return (x - mu) * jax.lax.rsqrt(var + EPS) * g + b
        key = jax.random.key(seed)
        ks = jax.random.split(key, 8)
        B, T, D, TE = (4, 512, 128, 128)
        s = 0.02
        return {'x': jax.random.normal(ks[0], (B, T, D), jnp.float32), 'emb': jax.random.normal(ks[1], (B, 1, TE), jnp.float32), 'gate_msa': jax.random.normal(ks[2], (B, 1, D), jnp.float32), 'norm_g': jnp.ones((D,), jnp.float32), 'norm_b': jnp.zeros((D,), jnp.float32), 'Wq': jax.random.normal(ks[3], (D, D), jnp.float32) * s, 'bq': jnp.zeros((D,), jnp.float32), 'Wk': jax.random.normal(ks[4], (D, D), jnp.float32) * s, 'bk': jnp.zeros((D,), jnp.float32), 'Wv': jax.random.normal(ks[5], (D, D), jnp.float32) * s, 'bv': jnp.zeros((D,), jnp.float32), 'emb_W': jax.random.normal(ks[6], (TE, 2 * D), jnp.float32) * s, 'emb_b': jnp.zeros((2 * D,), jnp.float32), 'sn_g': jnp.ones((D,), jnp.float32), 'sn_b': jnp.zeros((D,), jnp.float32), 'out_W': jax.random.normal(ks[7], (D, D), jnp.float32) * s, 'out_b': jnp.zeros((D,), jnp.float32)}
    _L0_cond_all = _L0_cond_setup()
    _L0_cond_in = {k: v for k, v in _L0_cond_all.items() if k in ('norm_g', 'norm_b', 'Wq', 'bq', 'Wk', 'bk', 'Wv', 'bv', 'emb_W', 'emb_b', 'sn_g', 'sn_b', 'out_W', 'out_b')}
    del _L0_cond_all

    def _L1_cond_setup():
        import jax, jax.numpy as jnp
        import numpy as np
        DIM = 128
        FF_MULT = 2
        EPS = 1e-06

        def _ln(x):
            mu = jnp.mean(x, axis=-1, keepdims=True)
            var = jnp.mean(jnp.square(x - mu), axis=-1, keepdims=True)
            return (x - mu) * jax.lax.rsqrt(var + EPS)
        key = jax.random.key(seed)
        ks = jax.random.split(key, 12)
        b, n, d = (4, 256, DIM)
        h = FF_MULT * d
        s = lambda fan_in: 1.0 / np.sqrt(fan_in)
        return {'x': jax.random.normal(ks[0], (b, n, d), jnp.float32), 't': jax.random.normal(ks[1], (b, d), jnp.float32), 'ada_w': jax.random.normal(ks[2], (d, 6 * d), jnp.float32) * s(d), 'ada_b': jnp.zeros((6 * d,), jnp.float32), 'ssm_w1': jax.random.normal(ks[3], (d, d), jnp.float32) * s(d), 'ssm_b1': jnp.zeros((d,), jnp.float32), 'ssm_w2': jax.random.normal(ks[4], (d, d), jnp.float32) * s(d), 'ssm_b2': jnp.zeros((d,), jnp.float32), 'ff_w1': jax.random.normal(ks[5], (d, h), jnp.float32) * s(d), 'ff_b1': jnp.zeros((h,), jnp.float32), 'ff_w2': jax.random.normal(ks[6], (h, d), jnp.float32) * s(h), 'ff_b2': jnp.zeros((d,), jnp.float32)}
    _L1_cond_all = _L1_cond_setup()
    _L1_cond_in = {k: v for k, v in _L1_cond_all.items() if k in ('ada_w', 'ada_b', 'ssm_w1', 'ssm_b1', 'ssm_w2', 'ssm_b2', 'ff_w1', 'ff_b1', 'ff_w2', 'ff_b2')}
    del _L1_cond_all

    def _L2_cond_setup():
        import jax, jax.numpy as jnp
        import numpy as np
        DIM = 128
        HEADS = 16
        HEAD_DIM = DIM // HEADS
        MLP = 4 * DIM
        EPS = 1e-05

        def layer_norm(x, g, b):
            mu = jnp.mean(x, axis=-1, keepdims=True)
            var = jnp.var(x, axis=-1, keepdims=True)
            return (x - mu) * jax.lax.rsqrt(var + EPS) * g + b

        def rope_cos_sin(n, d):
            inv_freq = 1.0 / 10000.0 ** (jnp.arange(0, d, 2, dtype=jnp.float32) / d)
            t = jnp.arange(n, dtype=jnp.float32)
            freqs = jnp.outer(t, inv_freq)
            emb = jnp.concatenate([freqs, freqs], -1)
            return (jnp.cos(emb), jnp.sin(emb))

        def rotate_half(x):
            x1, x2 = (x[..., ::2], x[..., 1::2])
            return jnp.concatenate([-x2, x1], axis=-1)
        key = jax.random.key(seed)
        ks = jax.random.split(key, 16)
        B, N = (2, 256)
        s = lambda fan_in: 1.0 / np.sqrt(fan_in)
        inp = {'x': jax.random.normal(ks[0], (B, N, DIM), jnp.float32), 't_emb': jax.random.normal(ks[1], (B, DIM), jnp.float32), 'norm1_g': jnp.ones((DIM,), jnp.float32), 'norm1_b': jnp.zeros((DIM,), jnp.float32), 'Wq': jax.random.normal(ks[2], (DIM, DIM), jnp.float32) * s(DIM), 'Wk': jax.random.normal(ks[3], (DIM, DIM), jnp.float32) * s(DIM), 'Wv': jax.random.normal(ks[4], (DIM, DIM), jnp.float32) * s(DIM), 'Wo': jax.random.normal(ks[5], (DIM, DIM), jnp.float32) * s(DIM), 'norm2_g': jnp.ones((DIM,), jnp.float32), 'norm2_b': jnp.zeros((DIM,), jnp.float32), 'W1': jax.random.normal(ks[6], (DIM, MLP), jnp.float32) * s(DIM), 'W2': jax.random.normal(ks[7], (MLP, DIM), jnp.float32) * s(MLP), 'ada_W': jax.random.normal(ks[8], (DIM, 6 * DIM), jnp.float32) * s(DIM), 'ada_b': jnp.zeros((6 * DIM,), jnp.float32)}
        return inp
    _L2_cond_all = _L2_cond_setup()
    _L2_cond_in = {k: v for k, v in _L2_cond_all.items() if k in ('norm1_g', 'norm1_b', 'Wq', 'Wk', 'Wv', 'Wo', 'norm2_g', 'norm2_b', 'W1', 'W2', 'ada_W', 'ada_b')}
    del _L2_cond_all

    def _L3_cond_setup():
        import jax, jax.numpy as jnp
        import numpy as np
        C = 128
        H = 16
        DH = C // H
        DFF = 4 * C
        D = 128
        B = 2
        L = 256
        MAX_SCALE_MUL = float(np.log(100.0))
        EPS = 1e-06

        def _ln(x):
            m = jnp.mean(x, axis=-1, keepdims=True)
            xc = x - m
            var = jnp.mean(xc * xc, axis=-1, keepdims=True)
            return xc * jax.lax.rsqrt(var + EPS)

        def _attention(x, attn_bias, qkv_w, q_bias, v_bias, scale_mul, proj_w, proj_b):
            b, l, c = x.shape
            bias = jnp.concatenate([q_bias, jnp.zeros_like(q_bias), v_bias])
            qkv = x @ qkv_w.T + bias
            qkv = qkv.reshape(b, l, 3, H, DH).transpose(2, 0, 3, 1, 4)
            q, k, v = (qkv[0], qkv[1], qkv[2])
            sm = jnp.exp(jnp.minimum(scale_mul, MAX_SCALE_MUL))
            q = q * jax.lax.rsqrt(jnp.sum(q * q, -1, keepdims=True).clip(1e-24)) * sm
            k = k * jax.lax.rsqrt(jnp.sum(k * k, -1, keepdims=True).clip(1e-24))
            attn = jnp.einsum('bhqd,bhkd->bhqk', q, k) + attn_bias
            attn = jax.nn.softmax(attn, axis=-1)
            out = jnp.einsum('bhqk,bhkd->bhqd', attn, v)
            out = out.transpose(0, 2, 1, 3).reshape(b, l, c)
            return out @ proj_w.T + proj_b
        key = jax.random.key(seed)
        ks = jax.random.split(key, 16)
        s = 0.02
        return {'x': jax.random.normal(ks[0], (B, L, C), jnp.float32), 'cond_BD': jax.random.normal(ks[1], (B, D), jnp.float32), 'attn_bias': jax.random.normal(ks[2], (1, 1, L, L), jnp.float32) * 0.1, 'qkv_w': jax.random.normal(ks[3], (3 * C, C), jnp.float32) * s, 'q_bias': jnp.zeros((C,), jnp.float32), 'v_bias': jnp.zeros((C,), jnp.float32), 'scale_mul': jnp.full((1, H, 1, 1), np.log(4.0), jnp.float32), 'proj_w': jax.random.normal(ks[4], (C, C), jnp.float32) * s, 'proj_b': jnp.zeros((C,), jnp.float32), 'fc1_w': jax.random.normal(ks[5], (DFF, C), jnp.float32) * s, 'fc1_b': jnp.zeros((DFF,), jnp.float32), 'fc2_w': jax.random.normal(ks[6], (C, DFF), jnp.float32) * s, 'fc2_b': jnp.zeros((C,), jnp.float32), 'ada_w': jax.random.normal(ks[7], (6 * C, D), jnp.float32) * s, 'ada_b': jnp.zeros((6 * C,), jnp.float32)}
    _L3_cond_all = _L3_cond_setup()
    _L3_cond_in = {k: v for k, v in _L3_cond_all.items() if k in ('qkv_w', 'q_bias', 'v_bias', 'scale_mul', 'proj_w', 'proj_b', 'fc1_w', 'fc1_b', 'fc2_w', 'fc2_b', 'ada_w', 'ada_b')}
    del _L3_cond_all
    return {'x': x, 'cond_1024': cond_1024, 'fside_1x1xSxS_0': fside_1x1xSxS_0, 'L0_cond_norm_g': _L0_cond_in['norm_g'], 'L0_cond_norm_b': _L0_cond_in['norm_b'], 'L0_cond_Wq': _L0_cond_in['Wq'], 'L0_cond_bq': _L0_cond_in['bq'], 'L0_cond_Wk': _L0_cond_in['Wk'], 'L0_cond_bk': _L0_cond_in['bk'], 'L0_cond_Wv': _L0_cond_in['Wv'], 'L0_cond_bv': _L0_cond_in['bv'], 'L0_cond_emb_W': _L0_cond_in['emb_W'], 'L0_cond_emb_b': _L0_cond_in['emb_b'], 'L0_cond_sn_g': _L0_cond_in['sn_g'], 'L0_cond_sn_b': _L0_cond_in['sn_b'], 'L0_cond_out_W': _L0_cond_in['out_W'], 'L0_cond_out_b': _L0_cond_in['out_b'], 'L1_cond_ada_w': _L1_cond_in['ada_w'], 'L1_cond_ada_b': _L1_cond_in['ada_b'], 'L1_cond_ssm_w1': _L1_cond_in['ssm_w1'], 'L1_cond_ssm_b1': _L1_cond_in['ssm_b1'], 'L1_cond_ssm_w2': _L1_cond_in['ssm_w2'], 'L1_cond_ssm_b2': _L1_cond_in['ssm_b2'], 'L1_cond_ff_w1': _L1_cond_in['ff_w1'], 'L1_cond_ff_b1': _L1_cond_in['ff_b1'], 'L1_cond_ff_w2': _L1_cond_in['ff_w2'], 'L1_cond_ff_b2': _L1_cond_in['ff_b2'], 'L2_cond_norm1_g': _L2_cond_in['norm1_g'], 'L2_cond_norm1_b': _L2_cond_in['norm1_b'], 'L2_cond_Wq': _L2_cond_in['Wq'], 'L2_cond_Wk': _L2_cond_in['Wk'], 'L2_cond_Wv': _L2_cond_in['Wv'], 'L2_cond_Wo': _L2_cond_in['Wo'], 'L2_cond_norm2_g': _L2_cond_in['norm2_g'], 'L2_cond_norm2_b': _L2_cond_in['norm2_b'], 'L2_cond_W1': _L2_cond_in['W1'], 'L2_cond_W2': _L2_cond_in['W2'], 'L2_cond_ada_W': _L2_cond_in['ada_W'], 'L2_cond_ada_b': _L2_cond_in['ada_b'], 'L3_cond_qkv_w': _L3_cond_in['qkv_w'], 'L3_cond_q_bias': _L3_cond_in['q_bias'], 'L3_cond_v_bias': _L3_cond_in['v_bias'], 'L3_cond_scale_mul': _L3_cond_in['scale_mul'], 'L3_cond_proj_w': _L3_cond_in['proj_w'], 'L3_cond_proj_b': _L3_cond_in['proj_b'], 'L3_cond_fc1_w': _L3_cond_in['fc1_w'], 'L3_cond_fc1_b': _L3_cond_in['fc1_b'], 'L3_cond_fc2_w': _L3_cond_in['fc2_w'], 'L3_cond_fc2_b': _L3_cond_in['fc2_b'], 'L3_cond_ada_w': _L3_cond_in['ada_w'], 'L3_cond_ada_b': _L3_cond_in['ada_b']}

def reference(x, cond_1024, fside_1x1xSxS_0, L0_cond_norm_g, L0_cond_norm_b, L0_cond_Wq, L0_cond_bq, L0_cond_Wk, L0_cond_bk, L0_cond_Wv, L0_cond_bv, L0_cond_emb_W, L0_cond_emb_b, L0_cond_sn_g, L0_cond_sn_b, L0_cond_out_W, L0_cond_out_b, L1_cond_ada_w, L1_cond_ada_b, L1_cond_ssm_w1, L1_cond_ssm_b1, L1_cond_ssm_w2, L1_cond_ssm_b2, L1_cond_ff_w1, L1_cond_ff_b1, L1_cond_ff_w2, L1_cond_ff_b2, L2_cond_norm1_g, L2_cond_norm1_b, L2_cond_Wq, L2_cond_Wk, L2_cond_Wv, L2_cond_Wo, L2_cond_norm2_g, L2_cond_norm2_b, L2_cond_W1, L2_cond_W2, L2_cond_ada_W, L2_cond_ada_b, L3_cond_qkv_w, L3_cond_q_bias, L3_cond_v_bias, L3_cond_scale_mul, L3_cond_proj_w, L3_cond_proj_b, L3_cond_fc1_w, L3_cond_fc1_b, L3_cond_fc2_w, L3_cond_fc2_b, L3_cond_ada_w, L3_cond_ada_b):
    import jax
    import jax.numpy as jnp

    def _L0_cond_ref(x, emb, gate_msa, norm_g, norm_b, Wq, bq, Wk, bk, Wv, bv, emb_W, emb_b, sn_g, sn_b, out_W, out_b):
        import jax, jax.numpy as jnp
        import numpy as np
        H = 16
        EPS = 1e-05

        def layer_norm(x, g, b):
            mu = jnp.mean(x, axis=-1, keepdims=True)
            var = jnp.var(x, axis=-1, keepdims=True)
            return (x - mu) * jax.lax.rsqrt(var + EPS) * g + b
        B, T, D = x.shape
        dh = D // H
        xn = layer_norm(x, norm_g, norm_b)
        q = (xn @ Wq + bq).reshape(B, T, H, dh)
        k = (xn @ Wk + bk).reshape(B, T, H, dh)
        v = (xn @ Wv + bv).reshape(B, T, H, dh)
        q = jax.nn.softmax(q, axis=-1)
        k = jax.nn.softmax(k, axis=1)
        ctx = jnp.einsum('bnhd,bnhl->bhdl', k, v)
        y = jnp.einsum('bnhd,bhdl->bnhl', q, ctx).reshape(B, T, D)
        emb_out = jax.nn.silu(emb) @ emb_W + emb_b
        scale, shift = jnp.split(emb_out, 2, axis=-1)
        h = layer_norm(y, sn_g, sn_b) * (1.0 + scale) + shift
        h = jax.nn.silu(h) @ out_W + out_b
        return x + gate_msa * h

    def _L1_cond_ref(x, t, ada_w, ada_b, ssm_w1, ssm_b1, ssm_w2, ssm_b2, ff_w1, ff_b1, ff_w2, ff_b2):
        import jax, jax.numpy as jnp
        import numpy as np
        DIM = 128
        FF_MULT = 2
        EPS = 1e-06

        def _ln(x):
            mu = jnp.mean(x, axis=-1, keepdims=True)
            var = jnp.mean(jnp.square(x - mu), axis=-1, keepdims=True)
            return (x - mu) * jax.lax.rsqrt(var + EPS)
        emb = jnp.dot(jax.nn.silu(t), ada_w) + ada_b
        shift_msa, scale_msa, gate_msa, shift_mlp, scale_mlp, gate_mlp = jnp.split(emb, 6, axis=-1)
        norm = _ln(x) * (1.0 + scale_msa[:, None]) + shift_msa[:, None]
        h = jax.nn.gelu(jnp.dot(norm, ssm_w1) + ssm_b1, approximate=False)
        ssm_out = jnp.dot(h, ssm_w2) + ssm_b2
        x = x + gate_msa[:, None] * ssm_out
        norm2 = _ln(x) * (1.0 + scale_mlp[:, None]) + shift_mlp[:, None]
        hf = jax.nn.gelu(jnp.dot(norm2, ff_w1) + ff_b1, approximate=True)
        ff_out = jnp.dot(hf, ff_w2) + ff_b2
        x = x + gate_mlp[:, None] * ff_out
        return x

    def _L2_cond_ref(x, t_emb, norm1_g, norm1_b, Wq, Wk, Wv, Wo, norm2_g, norm2_b, W1, W2, ada_W, ada_b):
        import jax, jax.numpy as jnp
        import numpy as np
        DIM = 128
        HEADS = 16
        HEAD_DIM = DIM // HEADS
        MLP = 4 * DIM
        EPS = 1e-05

        def layer_norm(x, g, b):
            mu = jnp.mean(x, axis=-1, keepdims=True)
            var = jnp.var(x, axis=-1, keepdims=True)
            return (x - mu) * jax.lax.rsqrt(var + EPS) * g + b

        def rope_cos_sin(n, d):
            inv_freq = 1.0 / 10000.0 ** (jnp.arange(0, d, 2, dtype=jnp.float32) / d)
            t = jnp.arange(n, dtype=jnp.float32)
            freqs = jnp.outer(t, inv_freq)
            emb = jnp.concatenate([freqs, freqs], -1)
            return (jnp.cos(emb), jnp.sin(emb))

        def rotate_half(x):
            x1, x2 = (x[..., ::2], x[..., 1::2])
            return jnp.concatenate([-x2, x1], axis=-1)
        B, N, C = x.shape
        H, D = (HEADS, HEAD_DIM)
        scale = D ** (-0.5)
        mod = jax.nn.silu(t_emb) @ ada_W + ada_b
        shift_msa, scale_msa, gate_msa, shift_mlp, scale_mlp, gate_mlp = jnp.split(mod, 6, axis=-1)
        xn = layer_norm(x, norm1_g, norm1_b) * (1 + scale_msa[:, None, :]) + shift_msa[:, None, :]
        q = (xn @ Wq).reshape(B, N, H, D).transpose(0, 2, 1, 3)
        k = (xn @ Wk).reshape(B, N, H, D).transpose(0, 2, 1, 3)
        v = (xn @ Wv).reshape(B, N, H, D).transpose(0, 2, 1, 3)
        cos, sin = rope_cos_sin(N, D)
        q = q * cos + rotate_half(q) * sin
        k = k * cos + rotate_half(k) * sin
        attn = jnp.einsum('bhnd,bhmd->bhnm', q, k) * scale
        attn = jax.nn.softmax(attn, axis=-1)
        out = jnp.einsum('bhnm,bhmd->bhnd', attn, v)
        out = out.transpose(0, 2, 1, 3).reshape(B, N, C) @ Wo
        x = x + gate_msa[:, None, :] * out
        xn = layer_norm(x, norm2_g, norm2_b) * (1 + scale_mlp[:, None, :]) + shift_mlp[:, None, :]
        mlp = jax.nn.gelu(xn @ W1, approximate=False) @ W2
        x = x + gate_mlp[:, None, :] * mlp
        return x

    def _L3_cond_ref(x, cond_BD, attn_bias, qkv_w, q_bias, v_bias, scale_mul, proj_w, proj_b, fc1_w, fc1_b, fc2_w, fc2_b, ada_w, ada_b):
        import jax, jax.numpy as jnp
        import numpy as np
        C = 128
        H = 16
        DH = C // H
        DFF = 4 * C
        D = 128
        B = 2
        L = 256
        MAX_SCALE_MUL = float(np.log(100.0))
        EPS = 1e-06

        def _ln(x):
            m = jnp.mean(x, axis=-1, keepdims=True)
            xc = x - m
            var = jnp.mean(xc * xc, axis=-1, keepdims=True)
            return xc * jax.lax.rsqrt(var + EPS)

        def _attention(x, attn_bias, qkv_w, q_bias, v_bias, scale_mul, proj_w, proj_b):
            b, l, c = x.shape
            bias = jnp.concatenate([q_bias, jnp.zeros_like(q_bias), v_bias])
            qkv = x @ qkv_w.T + bias
            qkv = qkv.reshape(b, l, 3, H, DH).transpose(2, 0, 3, 1, 4)
            q, k, v = (qkv[0], qkv[1], qkv[2])
            sm = jnp.exp(jnp.minimum(scale_mul, MAX_SCALE_MUL))
            q = q * jax.lax.rsqrt(jnp.sum(q * q, -1, keepdims=True).clip(1e-24)) * sm
            k = k * jax.lax.rsqrt(jnp.sum(k * k, -1, keepdims=True).clip(1e-24))
            attn = jnp.einsum('bhqd,bhkd->bhqk', q, k) + attn_bias
            attn = jax.nn.softmax(attn, axis=-1)
            out = jnp.einsum('bhqk,bhkd->bhqd', attn, v)
            out = out.transpose(0, 2, 1, 3).reshape(b, l, c)
            return out @ proj_w.T + proj_b
        ada = jax.nn.silu(cond_BD) @ ada_w.T + ada_b
        ada = ada.reshape(-1, 1, 6, C)
        g1, g2, s1, s2, sh1, sh2 = [ada[:, :, i, :] for i in range(6)]
        h = _ln(x) * (s1 + 1.0) + sh1
        x = x + _attention(h, attn_bias, qkv_w, q_bias, v_bias, scale_mul, proj_w, proj_b) * g1
        h = _ln(x) * (s2 + 1.0) + sh2
        h = jax.nn.gelu(h @ fc1_w.T + fc1_b, approximate=True) @ fc2_w.T + fc2_b
        x = x + h * g2
        return x
    x = _L0_cond_ref(x, cond_1024[:, None, :], cond_1024[:, None, :], L0_cond_norm_g, L0_cond_norm_b, L0_cond_Wq, L0_cond_bq, L0_cond_Wk, L0_cond_bk, L0_cond_Wv, L0_cond_bv, L0_cond_emb_W, L0_cond_emb_b, L0_cond_sn_g, L0_cond_sn_b, L0_cond_out_W, L0_cond_out_b)
    x = _L1_cond_ref(x, cond_1024, L1_cond_ada_w, L1_cond_ada_b, L1_cond_ssm_w1, L1_cond_ssm_b1, L1_cond_ssm_w2, L1_cond_ssm_b2, L1_cond_ff_w1, L1_cond_ff_b1, L1_cond_ff_w2, L1_cond_ff_b2)
    x = _L2_cond_ref(x, cond_1024, L2_cond_norm1_g, L2_cond_norm1_b, L2_cond_Wq, L2_cond_Wk, L2_cond_Wv, L2_cond_Wo, L2_cond_norm2_g, L2_cond_norm2_b, L2_cond_W1, L2_cond_W2, L2_cond_ada_W, L2_cond_ada_b)
    x = _L3_cond_ref(x, cond_1024, fside_1x1xSxS_0, L3_cond_qkv_w, L3_cond_q_bias, L3_cond_v_bias, L3_cond_scale_mul, L3_cond_proj_w, L3_cond_proj_b, L3_cond_fc1_w, L3_cond_fc1_b, L3_cond_fc2_w, L3_cond_fc2_b, L3_cond_ada_w, L3_cond_ada_b)
    return x

_drawn_inputs = setup_inputs


def setup_inputs(seed=0):
    import zlib

    import numpy as np

    out = dict(_drawn_inputs(seed))
    spreads = {'L0_cond_norm_g': (1.0, 0.6),
     'L0_cond_norm_b': (0.0, 0.275),
     'L0_cond_bq': (0.0, 0.8),
     'L0_cond_bk': (0.0, 2.0),
     'L0_cond_bv': (0.0, 0.1),
     'L0_cond_emb_b': (0.0, 0.354),
     'L0_cond_sn_g': (1.0, 0.6),
     'L0_cond_sn_b': (0.0, 0.554),
     'L0_cond_out_b': (0.0, 0.1),
     'L1_cond_ada_b': (0.0, 0.1),
     'L1_cond_ssm_b1': (0.0, 0.298),
     'L1_cond_ssm_b2': (0.0, 0.1),
     'L1_cond_ff_b1': (0.0, 0.333),
     'L1_cond_ff_b2': (0.0, 0.1),
     'L2_cond_norm1_g': (1.0, 0.2),
     'L2_cond_norm1_b': (0.0, 0.1),
     'L2_cond_norm2_g': (1.0, 0.2),
     'L2_cond_norm2_b': (0.0, 0.297),
     'L2_cond_ada_b': (0.0, 0.1),
     'L3_cond_q_bias': (0.0, 0.8),
     'L3_cond_v_bias': (0.0, 0.8),
     'L3_cond_scale_mul': (1.3862943649291992, 0.6),
     'L3_cond_proj_b': (0.0, 0.646),
     'L3_cond_fc1_b': (0.0, 0.8),
     'L3_cond_fc2_b': (0.0, 0.75),
     'L3_cond_ada_b': (0.0, 0.756)}
    factors = {'fside_1x1xSxS_0': 8.0,
     'L0_cond_Wq': 8.0,
     'L0_cond_Wk': 8.0,
     'L3_cond_qkv_w': 8.0,
     'L3_cond_proj_w': 8.0,
     'L3_cond_fc1_w': 8.0,
     'L3_cond_fc2_w': 8.0,
     'L3_cond_ada_w': 3.592}
    for name, (base, spread) in spreads.items():
        noise = np.random.default_rng([zlib.crc32(name.encode()), seed]).standard_normal(out[name].shape)
        drawn = base * np.exp(spread * noise) if base else spread * noise
        out[name] = jnp.asarray(drawn.astype(out[name].dtype))
    for name, factor in factors.items():
        out[name] = (out[name] * factor).astype(out[name].dtype)
    return out
```

```python
from contextlib import ExitStack

import numpy as np

import concourse.bass as bass
from concourse import mybir

ALU = mybir.AluOpType
ACT = mybir.ActivationFunctionType
AX = mybir.AxisListType
F32 = mybir.dt.float32
F32R = mybir.dt.float32r

P = 128
B, T, H, DH = 2, 512, 16, 8
TT = T // P
HG = 4
NG = B * H // HG
GB = H // HG
SP = 32
SPLIT = 3 * DH
SHIFT = SPLIT + 2
RING = 3
LAG = 24

LN_EPS = [1e-5, 1e-5, 1e-6, 1e-6, 1e-5, 1e-5, 1e-6, 1e-6]
NLN = len(LN_EPS)
LN_STATE = [0, None, 1, 2, 3, 4, 5, 6]
NMOD = 20
NUP = 7
NO_BIAS = (3, 4)

W_LOADS = [
    [("ones", 128), ("cond", 2), ("vec", 200), ("mod0", 256), ("ident", 128), ("blocks", 128), ("l0_q", 128),
     ("l0_k", 128), ("l0_v", 128), ("l0_bq", 128), ("l0_bv", 128), ("l0_o", 128)],
    [("mod", 18 * 128), ("l1_a", 128), ("l1_b", 128), ("l1_c", 256), ("l1_d", 256)],
    [("cos", 512), ("sin", 512), ("qcos", 512), ("qsin", 512), ("l2_q", 128), ("l2_qr", 128), ("l2_k", 128),
     ("l2_kr", 128), ("l2_v", 128), ("l2_o", 512), ("sumsel", 128), ("l2_a", 512), ("l2_b", 512)],
    [("l3_q", 128), ("l3_k", 128), ("l3_v", 128), ("l3_bv", 128), ("l3_o", 512), ("l3_a", 512), ("l3_b", 512)],
]
VEC = {}
_at = 0
for _name, _n in [("modb", NMOD), ("g", 2 * NLN), ("b", 2 * NLN), ("outb", 2 * NUP), ("eps", NLN), ("bk", 1),
                  ("l1_a", 1), ("l1_c", 2), ("l2_a", 0), ("l3_a", 4), ("l3_bq", 1), ("scale", 1)]:
    VEC[_name] = _at
    _at += _n
NVEC = 200

MLPS = [
    (2, 1, "l1_a", "l1_b", "l1_a", ACT.Gelu, 1),
    (3, 2, "l1_c", "l1_d", "l1_c", ACT.Gelu_apprx_tanh, 2),
    (5, 4, "l2_a", "l2_b", None, ACT.Gelu, 4),
    (7, 4, "l3_a", "l3_b", "l3_a", ACT.Gelu_apprx_tanh, 6),
]


def build(nc, xT, loads, bias_q, bias_k, const_rows, out):
    ctx = ExitStack()
    with ctx:
        def sb(name, shape, dt=F32):
            return ctx.enter_context(nc.sbuf_tensor(name, shape, dt))

        def sem(name):
            return ctx.enter_context(nc.semaphore(name))

        wt, load_of = {}, {}
        tiles = []
        for n, cols in enumerate(W_LOADS):
            tile = sb(f"weights{n}", [P, sum(c for _, c in cols)])
            tiles.append(tile)
            at = 0
            for name, c in cols:
                wt[name] = tile[:, at:at + c]
                load_of[name] = n
                at += c
        vec = wt["vec"]
        ones, ident, blocks, sumsel = wt["ones"], wt["ident"], wt["blocks"], wt["sumsel"]
        state = [sb(f"state{k}", [P, B, T]) for k in range(2)]
        state_b = sb("state_b", [P, B, T])
        xc = sb("xc", [P, B, T])
        sq = sb("sq", [P, B, T])
        lnv = sb("lnv", [P, B, T])
        rstd = sb("rstd", [P, B, T])
        xn = sb("xn", [P, B, T])
        xm = sb("xm", [P, B, T])
        hid = sb("hid", [P, 4, B, T])
        silc = sb("silc", [P, 2])
        mods = sb("mods", [P, NMOD, B])
        scale1 = sb("scale1", [P, NLN - 1, B])
        ln_a = sb("ln_a", [P, NLN, B])
        ln_t = sb("ln_t", [P, NLN - 1, B])
        ln_b = sb("ln_b", [P, NLN, B])
        gate = sb("gate", [P, NUP, B])
        gate_b = sb("gate_b", [P, NUP, B])
        qs = sb("qs", [P, B, T])
        qd = hid[:, 0]
        qe = hid[:, 1]
        qp = hid[:, 2]
        qmx = sb("qmx", [P, B, TT * H])
        qsum = sb("qsum", [P, B, TT * H])
        qrec = sb("qrec", [P, B, TT * H])
        kmx = sb("kmx", [P, B, 4])
        ke = hid[:, 3]
        ktok = lnv
        vtok = sq
        qT = rstd
        ctxm = sb("ctxm", [P, B, P])
        ysb = qs
        silh = xc
        qh = [hid[:, t].bitcast(F32R) for t in range(2)]
        ql = [hid[:, 2 + t].bitcast(F32R) for t in range(2)]
        vx = sb("vx", [P, NG, TT, HG, SP])
        qg = [sb(f"qg{u}", [P, T], F32R) for u in range(RING)]
        kg = [sb(f"kg{u}", [P, HG, T], F32R) for u in range(RING)]
        vg = [sb(f"vg{u}", [P, TT, HG, SP]) for u in range(2)]
        mx = [sb(f"mx{u}", [P, TT * HG]) for u in range(2)]
        nmx = [sb(f"nmx{u}", [P, TT, 2, HG], F32R) for u in range(2)]
        mrow = [sb(f"mrow{u}", [HG * 2, T], F32R) for u in range(2)]
        prob = [sb(f"prob{n}", [P, 2, T]) for n in range(4)]
        osb = [sb(f"osb{u}", [P, T]) for u in range(2)]
        orec = [sb(f"orec{u}", [P, T]) for u in range(2)]
        onorm = hid[:, :, :, :].rearrange("p a b t -> p (a b) t")
        junk = [sb(f"junk{n}", [P, T]) for n in range(2)]
        bq_sb = wt["mod"][:, 0:TT * T].rearrange("p (q n) -> p q n", q=TT)
        bk_hi = sb("bias_k_hi", [P, TT, T], F32R)
        bk_lo = sb("bias_k_lo", [P, TT, T], F32R)
        bk_sb = prob
        identr = sb("identr", [P, P], F32R)
        qmul = sb("qmul", [P, 2])
        scratch = {(a, t): nc.dram_tensor(f"split_{t}{a}", [NG, HG, SHIFT, T], F32).ap() for a in range(2) for t in "qk"}

        ps = ctx.enter_context(nc.psum_tensor("ps", [P, 8, T], F32))

        ld_x = [sem(f"ld_x{b}") for b in range(B)]
        ld_w = [sem(f"ld_w{n}") for n in range(len(W_LOADS))]
        ld_bq, ld_bk = sem("ld_bias_q"), sem("ld_bias_k")
        s_silc, s_modmm, s_mod, s_modok = sem("silu_cond"), sem("mod_products"), sem("mod_steps"), sem("mods_ready")
        s_x, s_xb = sem("x_ready"), sem("x_plus_bias")
        s_mean, s_xc, s_sq, s_var, s_lnv, s_rstd, s_xnn, s_ln = (
            sem(n) for n in ("ln_mean", "ln_centered", "ln_square", "ln_var", "ln_log", "ln_rstd", "ln_scaled", "ln_out"))
        s_m1, s_hid, s_m2 = sem("mlp_first"), sem("mlp_hidden"), sem("mlp_second")
        s_q0, s_k0, s_v0 = sem("l0_q"), sem("l0_k"), sem("l0_v")
        s_qstep, s_qd, s_qe, s_qp = sem("l0_q_steps"), sem("l0_q_shifted"), sem("l0_q_exp"), sem("l0_q_probs")
        s_kstep, s_kb, s_ke = sem("l0_k_steps"), sem("l0_k_shift"), sem("l0_k_exp")
        s_vtok, s_ktT, s_ktok, s_ctx, s_ctxm, s_qTp, s_qT, s_y, s_ysb, s_silh, s_o0 = (
            sem(n) for n in ("l0_v_ready", "l0_k_turned", "l0_k_tokens", "l0_ctx", "l0_ctx_ready", "l0_q_turned",
                             "l0_q_features", "l0_y", "l0_y_ready", "l0_silu", "l0_out"))
        s_rows = sem("rows_written")
        s_ones, s_idr, s_bks = sem("ones_rows"), sem("ident_rounded"), sem("bias_split")
        att = []
        for a in range(2):
            att.append({n: sem(f"{n}{a}") for n in (
                "qkv", "rot", "qsum", "hi", "lo", "split_w0", "split_w1", "v_mm", "v_ready", "stage0", "stage1", "stage2",
                "mrow_in0", "mrow_in1", "a_score", "a_max", "nm_hi", "nm_lo", "m_turned", "m_row", "b_score", "b_exp", "pv", "o_copied",
                "o_sum", "o_log", "o_rec", "o_norm", "v_group", "proj", "t1", "t2", "qf", "nrm")})
        s_out = sem("out_written")

        def w(name, a=0, n=P):
            return wt[name][:, a:a + n]

        def v1(name, k=0):
            return vec[:, VEC[name] + k:VEC[name] + k + 1]

        def x_ready(eng, k, b):
            if k == 0:
                eng.wait_ge(ld_x[b], 16)
            else:
                eng.wait_ge(s_x, 2 * (k - 1) + b + 1)

        def loaded(eng, name):
            eng.wait_ge(ld_w[load_of[name]], 16)

        def nth(n, b):
            return 2 * n + b + 1

        mlp_base, at = [], 0
        for m in MLPS:
            mlp_base.append(at)
            at += 2 * m[1]
        up_of_mlp = {m[6]: n for n, m in enumerate(MLPS)}

        block = ctx.enter_context(nc.Block())

        @block.sync
        def _(sp):
            sp.dma_start(state[0][:, 0, :], xT[:, 0, :]).then_inc(ld_x[0], 16)
            sp.dma_start(tiles[0][:], loads[0]).then_inc(ld_w[0], 16)
            sp.dma_start(state[0][:, 1, :], xT[:, 1, :]).then_inc(ld_x[1], 16)
            for n in range(1, len(W_LOADS)):
                sp.dma_start(tiles[n][:], loads[n]).then_inc(ld_w[n], 16)
            for t in range(TT):
                sp.dma_start(bk_sb[t][:, 0, :], bias_k[:, t, :]).then_inc(ld_bk, 16)
            sp.wait_ge(s_modmm, 1)
            sp.dma_start(bq_sb, bias_q).then_inc(ld_bq, 16)
            for a in range(2):
                for t, value in enumerate("qk"):
                    sp.dma_start(scratch[a, value][:, :, SPLIT:SHIFT, :].rearrange("i j r n -> (i j) r n"),
                                 const_rows[t]).then_inc(s_rows, 16)
            for a in range(2):
                s = att[a]
                for b in range(B):
                    for t in range(2):
                        sp.wait_ge(s["lo"], 2 * b + t + 1)
                        rows = [(qh, 0), (qh, 1), (ql, 2)] if t == 0 else [(qh, 0), (ql, 1), (qh, 2)]
                        for half, r in rows:
                            dst = scratch[a, "qk"[t]][b * GB:(b + 1) * GB, :, r * DH:(r + 1) * DH, :]
                            sp.dma_start(dst.rearrange("g j d n -> (g j) d n"),
                                         half[t][:, b, :].bitcast(F32)).then_inc(s[f"split_w{b}"], 16)

                def stage(i):
                    if i >= RING:
                        sp.wait_ge(s["b_score"], 8 * (i - RING + 1))
                    for j in range(HG):
                        rows = slice(SP * j, SP * j + SHIFT)
                        sp.dma_start(qg[i % RING][rows, :].bitcast(F32), scratch[a, "q"][i, j]).then_inc(s[f"stage{i % RING}"], 16)
                        sp.dma_start(kg[i % RING][rows, j, :].bitcast(F32), scratch[a, "k"][i, j]).then_inc(s[f"stage{i % RING}"], 16)

                def stage_m(i):
                    sp.wait_ge(s["m_row"], i + 1)
                    for t in range(2):
                        sp.dma_start(qg[i % RING][SPLIT + t::SP, :].bitcast(F32),
                                     mrow[i % 2][t * HG:(t + 1) * HG, :].bitcast(F32)).then_inc(s[f"mrow_in{i % 2}"], 16)

                sp.wait_ge(s["split_w0"], 16 * 6)
                sp.wait_ge(s_rows, 64)
                if a == 0:
                    sp.wait_ge(s_ones, 6)
                stage(0)
                stage(1)
                stage_m(0)
                for i in range(NG):
                    if i == 0:
                        sp.wait_ge(s["split_w1"], 16 * 6)
                    if i + 2 < NG:
                        stage(i + 2)
                    if i + 1 < NG:
                        stage_m(i + 1)
            for b in range(B):
                x_ready(sp, NUP, b)
                sp.dma_start(out[:, b, :], state[NUP % 2][:, b, :]).then_inc(s_out, 16)
            sp.wait_ge(s_out, 16 * B)

        @block.tensor
        def _(pe):
            mm = nc.tensor.matmul

            def norm(n):
                for b in range(B):
                    if LN_STATE[n] is None:
                        pe.wait_ge(s_ysb, b + 1)
                        src = ysb
                    else:
                        x_ready(pe, LN_STATE[n], b)
                        src = state[LN_STATE[n] % 2]
                    mm(ps[:, b, :], ones, src[:, b, :], start=True, stop=True).then_inc(s_mean, 1)
                for b in range(B):
                    pe.wait_ge(s_sq, nth(n, b))
                    mm(ps[:, 2 + b, :], ones, sq[:, b, :], start=True, stop=True).then_inc(s_var, 1)

            def mlp(m):
                n, nb, w1, w2, _, _, _ = MLPS[m]
                base = mlp_base[m]
                for b in range(B):
                    pe.wait_ge(s_ln, nth(n, b))
                    for j in range(nb):
                        c = b * nb + j
                        if c >= 4:
                            pe.wait_ge(s_hid, base + c - 3)
                        mm(ps[:, 4 + c % 4, :], w(w1, j * P), xm[:, b, :], start=True, stop=True).then_inc(s_m1, 1)
                for b in range(B):
                    for j in range(nb):
                        pe.wait_ge(s_hid, base + b * nb + j + 1)
                        last = mm(ps[:, b, :], w(w2, j * P), hid[:, j, b, :], start=(j == 0), stop=(j == nb - 1))
                    last.then_inc(s_m2, 1)

            def attention(a):
                s = att[a]

                def a_pair(k):
                    for n in range(2 * k, 2 * k + 2):
                        i, qt, j = n // 16, n % 16 // 4, n % 4
                        if n % 16 == 0:
                            pe.wait_ge(s[f"stage{i % RING}"], 2 * HG * 16 * (i // RING + 1))
                        if n >= 2:
                            pe.wait_ge(s["a_max"], n - 1)
                        mm(ps[:, 4 + n % 2, :], qg[i % RING][:, qt * P:(qt + 1) * P], kg[i % RING][:, j, :],
                           start=True, stop=True).then_inc(s["a_score"], 1)

                def turn_max(i):
                    pe.wait_ge(s["nm_lo"], i + 1)
                    if i >= 3:
                        pe.wait_ge(s["o_log"], i - 2)
                    for qt in range(TT):
                        last = nc.tensor.transpose(ps[0:2 * HG, 7, qt * P:(qt + 1) * P],
                                                   nmx[i % 2][:, qt, :, :].rearrange("p t j -> p (t j)").bitcast(F32),
                                                   ident)
                    last.then_inc(s["m_turned"], 1)

                def scores(c):
                    i, kt, p = c // 8, c % 8 // 2, c % 2
                    if c % 8 == 0:
                        pe.wait_ge(s[f"mrow_in{i % 2}"], 32 * (i // 2 + 1))
                    if c >= 2:
                        pe.wait_ge(s["b_exp"], c - 1)
                    for j in (2 * p, 2 * p + 1):
                        last = mm(ps[:, 2 * (c % 2) + j % 2, :], kg[i % RING][:, j, kt * P:(kt + 1) * P], qg[i % RING][:],
                                  start=True, stop=(a == 0))
                    if a == 1:
                        for j in range(2):
                            for half in (bk_hi, bk_lo):
                                last = mm(ps[:, 2 * (c % 2) + j, :], identr[:], half[:, kt, :], start=False,
                                          stop=(half is bk_lo))
                    last.then_inc(s["b_score"], 1)

                def values(n):
                    i, kt = n // TT, n % TT
                    pe.wait_ge(s["b_exp"], 2 * n + 2)
                    if kt == 0:
                        pe.wait_ge(s["v_group"], i + 1)
                        if i >= 1:
                            pe.wait_ge(s["o_copied"], i)
                    for j in range(HG):
                        last = mm(ps[SP * j:SP * (j + 1), 6, :], vg[i % 2][:, kt, j, :],
                                  prob[(2 * n + j // 2) % 4][:, j % 2, :], start=(kt == 0), stop=(kt == TT - 1))
                    last.then_inc(s["pv"], 1)

                def sums(i):
                    pe.wait_ge(s["o_copied"], i + 1)
                    pe.wait_ge(s["m_row"], min(i + 3, NG))
                    mm(ps[:, 7, :], sumsel, osb[i % 2][:], start=True, stop=True).then_inc(s["o_sum"], 1)

                if a == 0:
                    for b in range(B):
                        pe.wait_ge(s_ln, nth(4, b))
                        if b == 0:
                            loaded(pe, "l2_q")
                        for n, name in enumerate(("l2_q", "l2_qr", "l2_k", "l2_kr")):
                            if b:
                                pe.wait_ge(s["rot"], n + 1)
                            mm(ps[:, 4 + n, :], w(name), xm[:, b, :], start=True, stop=True).then_inc(s["qkv"], 1)
                        for t in range(TT):
                            last = mm(ps[:, b, t * P:(t + 1) * P], xm[:, b, t * P:(t + 1) * P], w("l2_v"),
                                      start=True, stop=True)
                        last.then_inc(s["v_mm"], 1)
                else:
                    for b in range(B):
                        pe.wait_ge(s_ln, nth(6, b))
                        for n, name in enumerate(("l3_q", "l3_k")):
                            mm(ps[:, 4 + 2 * b + n, :], w(name), xm[:, b, :], start=True, stop=True).then_inc(s["qkv"], 1)
                        for t in range(TT):
                            last = mm(ps[:, b, t * P:(t + 1) * P], xm[:, b, t * P:(t + 1) * P], w("l3_v"),
                                      start=True, stop=True)
                        last.then_inc(s["v_mm"], 1)
                    for n in range(4):
                        pe.wait_ge(s["t1"], n + 1)
                        mm(ps[:, 4 + n, :], blocks, (xc, sq)[n % 2][:, n // 2, :], start=True, stop=True).then_inc(s["qsum"], 1)

                for k in range(LAG // 2):
                    if k == 10:
                        turn_max(0)
                    a_pair(k)
                for c in range(8 * NG + 3):
                    i = c // 8
                    if c < 8 * NG:
                        scores(c)
                        if 2 * c + LAG < 16 * NG:
                            a_pair(c + LAG // 2)
                    if c % 2 == 1 and c >= 3:
                        values((c - 3) // 2)
                    if c % 8 == 5 and i + 1 < NG:
                        turn_max(i + 1)
                    if c % 8 == 3 and i >= 1 and c < 8 * NG:
                        pass
                    if c % 8 == 7 and i >= 1:
                        sums(i - 1)
                sums(NG - 1)
                for b in range(B):
                    for g in range(GB):
                        pe.wait_ge(s["o_norm"], b * GB + g + 1)
                        last = mm(ps[:, b, :], w(("l2_o", "l3_o")[a], g * P), onorm[:, b * GB + g, :],
                                  start=(g == 0), stop=(g == GB - 1))
                    last.then_inc(s["proj"], 1)

            loaded(pe, "ones")
            pe.wait_ge(s_silc, 1)
            norm(0)
            for j in range(NMOD):
                if j == 2:
                    loaded(pe, "mod")
                wj = w("mod0", j * P) if j < 2 else w("mod", (j - 2) * P)
                last = mm(ps[:, 7, 2 * j:2 * j + 2], wj, silc[:], start=True, stop=True)
            last.then_inc(s_modmm, 1)
            for b in range(B):
                pe.wait_ge(s_ln, nth(0, b))
                for t in range(TT):
                    last = mm(ps[:, 4 + b, t * P:(t + 1) * P], xm[:, b, t * P:(t + 1) * P], w("l0_q"), start=True, stop=True)
                last.then_inc(s_q0, 1)
                for t in range(TT):
                    last = mm(ps[:, b, t * P:(t + 1) * P], xm[:, b, t * P:(t + 1) * P], w("l0_v"), start=True, stop=True)
                last.then_inc(s_v0, 1)
                mm(ps[:, 2 + b, :], w("l0_k"), xm[:, b, :], start=True, stop=True).then_inc(s_k0, 1)
            pe.wait_ge(s_mod, 1)
            for b in range(B):
                pe.wait_ge(s_ke, b + 1)
                for t in range(TT):
                    last = nc.tensor.transpose(ps[:, 6 + b, t * P:(t + 1) * P], ke[:, b, t * P:(t + 1) * P], ident)
                last.then_inc(s_ktT, 1)
            for b in range(B):
                pe.wait_ge(s_ktok, b + 1)
                pe.wait_ge(s_vtok, b + 1)
                for t in range(TT):
                    last = mm(ps[:, b, 0:P], ktok[:, b, t * P:(t + 1) * P], vtok[:, b, t * P:(t + 1) * P],
                              start=(t == 0), stop=(t == TT - 1))
                last.then_inc(s_ctx, 1)
            for b in range(B):
                pe.wait_ge(s_qp, b + 1)
                for t in range(TT):
                    last = nc.tensor.transpose(ps[:, 4 + b, t * P:(t + 1) * P], qp[:, b, t * P:(t + 1) * P], ident)
                last.then_inc(s_qTp, 1)
            for b in range(B):
                pe.wait_ge(s_qT, b + 1)
                pe.wait_ge(s_ctxm, b + 1)
                mm(ps[:, 2 + b, :], ctxm[:, b, :], qT[:, b, :], start=True, stop=True).then_inc(s_y, 1)
            norm(1)
            for b in range(B):
                pe.wait_ge(s_silh, b + 1)
                mm(ps[:, b, :], w("l0_o"), silh[:, b, :], start=True, stop=True).then_inc(s_o0, 1)
            norm(2)
            mlp(0)
            norm(3)
            mlp(1)
            norm(4)
            attention(0)
            norm(5)
            mlp(2)
            norm(6)
            loaded(pe, "l3_q")
            attention(1)
            norm(7)
            mlp(3)

        @block.vector
        def _(dv):
            V = nc.vector

            def norm(n):
                for b in range(B):
                    dv.wait_ge(s_mean, nth(n, b))
                    src = ysb if LN_STATE[n] is None else state[LN_STATE[n] % 2]
                    if LN_STATE[n] is None:
                        dv.wait_ge(s_ysb, b + 1)
                    else:
                        x_ready(dv, LN_STATE[n], b)
                    V.tensor_tensor(xc[:, b, :], src[:, b, :], ps[:, b, :], ALU.subtract).then_inc(s_xc, 1)
                for b in range(B):
                    dv.wait_ge(s_rstd, nth(n, b))
                    dv.wait_ge(s_xc, nth(n, b))
                    V.tensor_tensor(xn[:, b, :], xc[:, b, :], rstd[:, b, :], ALU.mult).then_inc(s_xnn, 1)
                    dv.wait_ge(s_xnn, nth(n, b))
                    V.tensor_scalar(xm[:, b, :], xn[:, b, :], ln_a[:, n, b:b + 1], ln_b[:, n, b:b + 1],
                                    ALU.mult, ALU.add).then_inc(s_ln, 1)

            def update(k, ready, base):
                for b in range(B):
                    dv.wait_ge(ready, base + b + 1)
                    if k in NO_BIAS:
                        x_ready(dv, k, b)
                        src = state[k % 2]
                    else:
                        dv.wait_ge(s_xb, [0, 1, 2, None, None, 3, 4][k] * 2 + b + 1)
                        src = state_b
                    V.scalar_tensor_tensor(out=state[(k + 1) % 2][:, b, :], in0=ps[:, b, :], scalar=gate[:, k, b:b + 1],
                                           in1=src[:, b, :], op0=ALU.mult, op1=ALU.add).then_inc(s_x, 1)

            def split_pair(s, b, t, src, ready, count):
                dv.wait_ge(ready, count)
                dv.wait_ge(s["hi"], 2 * b + t + 1)
                V.tensor_tensor(ql[t][:, b, :], src, qh[t][:, b, :].bitcast(F32), ALU.subtract).then_inc(s["lo"], 1)

            def attention(a):
                s = att[a]
                if a == 0:
                    for b in range(B):
                        for n, (name, dst) in enumerate((("qcos", xc), ("qsin", sq), ("cos", lnv), ("sin", rstd))):
                            dv.wait_ge(s["qkv"], 4 * b + n + 1)
                            V.tensor_tensor(dst[:, b, :], ps[:, 4 + n, :], wt[name], ALU.mult).then_inc(s["rot"], 1)
                        for t in range(2):
                            src = (xn, junk[b])[t]
                            dst = xn[:, b, :] if t == 0 else junk[b][:]
                            dv.wait_ge(s["rot"], 4 * b + 2 * t + 2)
                            x1, x2 = ((xc, sq), (lnv, rstd))[t]
                            V.tensor_tensor(dst, x1[:, b, :], x2[:, b, :], ALU.add).then_inc(s["qf"], 1)
                            split_pair(s, b, t, dst, s["qf"], 2 * b + t + 1)
                        dv.wait_ge(s["v_mm"], b + 1)
                        if b == 0:
                            dv.wait_ge(s_ones, 8)
                        for t in range(TT):
                            V.tensor_copy(vx[:, b * GB:(b + 1) * GB, t, :, 0:DH],
                                          ps[:, b, t * P:(t + 1) * P].rearrange("p (g j d) -> p g j d", g=GB, j=HG)
                                          ).then_inc(s["v_ready"], 1)
                else:
                    for b in range(B):
                        dv.wait_ge(s["v_mm"], b + 1)
                        if b == 0:
                            dv.wait_ge(att[0]["v_group"], NG)
                        for t in range(TT):
                            V.tensor_tensor(vx[:, b * GB:(b + 1) * GB, t, :, 0:DH],
                                            ps[:, b, t * P:(t + 1) * P].rearrange("p (g j d) -> p g j d", g=GB, j=HG),
                                            wt["l3_bv"].rearrange("p (g j d) -> p g j d", g=GB, j=HG),
                                            ALU.add).then_inc(s["v_ready"], 1)
                    for n in range(4):
                        b, t = n // 2, n % 2
                        dv.wait_ge(s["qsum"], n + 1)
                        V.tensor_scalar((lnv, rstd)[t][:, b, :], ps[:, 4 + n, :], 1e-24, None, ALU.max).then_inc(s["t2"], 1)
                    for n in range(4):
                        b, t = n // 2, n % 2
                        dv.wait_ge(s["nrm"], n + 1)
                        src = (xn, qs)[t][:, b, :]
                        dv.wait_ge(s["rot"], n + 1)
                        V.scalar_tensor_tensor(out=src, in0=src, scalar=(qmul[:, 1:2], 1.0)[t], in1=(lnv, rstd)[t][:, b, :],
                                               op0=ALU.mult, op1=ALU.mult).then_inc(s["qf"], 1)
                        split_pair(s, b, t, src, s["qf"], n + 1)

                def maxima(k):
                    for n in range(2 * k, 2 * k + 2):
                        i, c = n // 16, n % 16
                        if c == 0 and i >= 2:
                            dv.wait_ge(s["nm_lo"], i - 1)
                        dv.wait_ge(s["a_score"], n + 1)
                        dst = mx[i % 2][:, c:c + 1]
                        if a == 0:
                            V.tensor_reduce(dst, ps[:, 4 + n % 2, :], AX.X, ALU.max).then_inc(s["a_max"], 1)
                        else:
                            if n >= 2:
                                dv.wait_ge(s["a_max"], n - 1)
                            V.tensor_tensor_reduce(junk[n % 2][:], ps[:, 4 + n % 2, :], bq_sb[:, c // 4, :], 1.0, -3e38,
                                                   ALU.add, ALU.max, dst).then_inc(s["a_max"], 1)
                        if c == 15:
                            dv.wait_ge(s["a_max"], n + 1)
                            if i >= 2:
                                dv.wait_ge(s["m_turned"], i - 1)
                            m = mx[i % 2][:].rearrange("p (q j) -> p q j", q=TT)
                            V.tensor_scalar(nmx[i % 2][:, :, 0, :], m, -1.0, None, ALU.mult).then_inc(s["nm_hi"], 1)
                            dv.wait_ge(s["nm_hi"], i + 1)
                            V.scalar_tensor_tensor(out=nmx[i % 2][:, :, 1, :], in0=m, scalar=-1.0,
                                                   in1=nmx[i % 2][:, :, 0, :].bitcast(F32), op0=ALU.mult,
                                                   op1=ALU.subtract).then_inc(s["nm_lo"], 1)

                if a == 1:
                    dv.wait_ge(ld_bq, 16)
                for k in range(8 * NG):
                    maxima(k)

            dv.wait_ge(ld_w[0], 16)
            V.tensor_copy(ln_a[:, 0, :], vec[:, VEC["g"]:VEC["g"] + 2]).then_inc(s_modok, 1)
            V.tensor_copy(ln_b[:, 0, :], vec[:, VEC["b"]:VEC["b"] + 2]).then_inc(s_modok, 1)
            V.tensor_copy(gate[:, 0, :], wt["cond"]).then_inc(s_modok, 1)
            V.tensor_copy(identr[:], ident).then_inc(s_idr, 1)
            dv.wait_ge(s_modok, 2)
            norm(0)
            dv.wait_ge(s_modmm, 1)
            V.tensor_tensor(mods[:], ps[:, 7, 0:2 * NMOD].rearrange("p (m b) -> p m b", b=B),
                            vec[:, VEC["modb"]:VEC["modb"] + NMOD].unsqueeze(2).to_broadcast([P, NMOD, B]),
                            ALU.add).then_inc(s_mod, 1)
            dv.wait_ge(s_mod, 1)
            V.tensor_scalar(scale1[:], mods[:, 0:7, :], 1.0, None, ALU.add).then_inc(s_mod, 1)
            V.tensor_copy(gate[:, 1:NUP, :], mods[:, 14:20, :]).then_inc(s_mod, 1)
            dv.wait_ge(s_mod, 3)
            V.tensor_tensor(ln_a[:, 1:NLN, :], scale1[:],
                            vec[:, VEC["g"] + 2:VEC["g"] + 2 * NLN].rearrange("p (n b) -> p n b", b=B),
                            ALU.mult).then_inc(s_modok, 1)
            V.tensor_tensor(ln_t[:], scale1[:], vec[:, VEC["b"] + 2:VEC["b"] + 2 * NLN].rearrange("p (n b) -> p n b", b=B),
                            ALU.mult).then_inc(s_mod, 1)
            dv.wait_ge(s_modok, 3)
            V.tensor_tensor(gate_b[:], gate[:], vec[:, VEC["outb"]:VEC["outb"] + 2 * NUP].rearrange("p (n b) -> p n b", b=B),
                            ALU.mult).then_inc(s_modok, 1)
            dv.wait_ge(s_mod, 4)
            V.tensor_tensor(ln_b[:, 1:NLN, :], ln_t[:], mods[:, 7:14, :], ALU.add).then_inc(s_modok, 1)

            for b in range(B):
                dv.wait_ge(s_k0, b + 1)
                V.tensor_reduce(kmx[:, b, 0:1], ps[:, 2 + b, :], AX.X, ALU.max).then_inc(s_kstep, 1)
                dv.wait_ge(s_kstep, 2 * b + 1)
                V.tensor_tensor(kmx[:, b, 1:2], kmx[:, b, 0:1], v1("bk"), ALU.add).then_inc(s_kstep, 1)
                dv.wait_ge(s_kstep, 2 * b + 2)
                V.tensor_tensor(kmx[:, b, 2:3], v1("bk"), kmx[:, b, 1:2], ALU.subtract).then_inc(s_kb, 1)
            h8 = "p (h d) -> p h d"
            for b in range(B):
                dv.wait_ge(s_q0, b + 1)
                V.tensor_tensor(qs[:, b, :].rearrange("p (t n) -> p t n", t=TT),
                                ps[:, 4 + b, :].rearrange("p (t n) -> p t n", t=TT),
                                wt["l0_bq"].unsqueeze(1).to_broadcast([P, TT, P]), ALU.add).then_inc(s_qstep, 1)
                dv.wait_ge(s_qstep, 2 * b + 1)
                V.tensor_reduce(qmx[:, b, :], qs[:, b, :].rearrange(h8, d=DH), AX.X, ALU.max).then_inc(s_qstep, 1)
                dv.wait_ge(s_qstep, 2 * b + 2)
                V.tensor_tensor(qd[:, b, :].rearrange(h8, d=DH), qs[:, b, :].rearrange(h8, d=DH),
                                qmx[:, b, :].unsqueeze(2).to_broadcast([P, TT * H, DH]), ALU.subtract).then_inc(s_qd, 1)
            for b in range(B):
                dv.wait_ge(s_v0, b + 1)
                dv.wait_ge(s_var, nth(0, b))
                V.tensor_tensor(vtok[:, b, :].rearrange("p (t n) -> p t n", t=TT),
                                ps[:, b, :].rearrange("p (t n) -> p t n", t=TT),
                                wt["l0_bv"].unsqueeze(1).to_broadcast([P, TT, P]), ALU.add).then_inc(s_vtok, 1)
            for b in range(B):
                dv.wait_ge(s_qe, b + 1)
                V.tensor_reduce(qsum[:, b, :], qe[:, b, :].rearrange(h8, d=DH), AX.X, ALU.add).then_inc(s_qstep, 1)
                dv.wait_ge(s_qstep, 2 * b + 5)
                V.reciprocal(qrec[:, b, :], qsum[:, b, :]).then_inc(s_qstep, 1)
                dv.wait_ge(s_qstep, 2 * b + 6)
                V.tensor_tensor(qp[:, b, :].rearrange(h8, d=DH), qe[:, b, :].rearrange(h8, d=DH),
                                qrec[:, b, :].unsqueeze(2).to_broadcast([P, TT * H, DH]), ALU.mult).then_inc(s_qp, 1)
            for b in range(B):
                dv.wait_ge(s_ke, b + 1)
                V.reciprocal(kmx[:, b, 0:1], kmx[:, b, 3:4]).then_inc(s_kstep, 1)
                dv.wait_ge(s_kstep, b + 5)
                dv.wait_ge(s_ctx, b + 1)
                V.scalar_tensor_tensor(out=ctxm[:, b, :], in0=ps[:, b, 0:P], scalar=kmx[:, b, 0:1], in1=blocks,
                                       op0=ALU.mult, op1=ALU.mult).then_inc(s_ctxm, 1)
            for b in range(B):
                dv.wait_ge(s_qTp, b + 1)
                V.tensor_copy(qT[:, b, :], ps[:, 4 + b, :]).then_inc(s_qT, 1)
            dv.wait_ge(s_modok, 6)
            norm(1)
            update(0, s_o0, 0)
            norm(2)
            update(1, s_m2, 0)
            norm(3)
            update(2, s_m2, 2)
            norm(4)
            for t in range(TT):
                dv.wait_ge(ld_bk, 16 * TT)
                V.tensor_copy(bk_hi[:, t, :], bk_sb[t][:, 0, :]).then_inc(s_bks, 1)
            for t in range(TT):
                dv.wait_ge(s_bks, t + 1)
                V.tensor_tensor(bk_lo[:, t, :], bk_sb[t][:, 0, :], bk_hi[:, t, :].bitcast(F32), ALU.subtract).then_inc(s_bks, 1)
            attention(0)
            update(3, att[0]["proj"], 0)
            norm(5)
            update(4, s_m2, 4)
            norm(6)
            attention(1)
            update(5, att[1]["proj"], 0)
            norm(7)
            update(6, s_m2, 6)

        @block.scalar
        def _(act):
            A = nc.scalar.activation

            def log_exp_table():
                nc.scalar.preload_act_table_set("natural_log_exp_and_others")

            def norm(n):
                log_exp_table()
                for b in range(B):
                    act.wait_ge(s_xc, nth(n, b))
                    A(sq[:, b, :], xc[:, b, :], ACT.Square).then_inc(s_sq, 1)
                for b in range(B):
                    act.wait_ge(s_var, nth(n, b))
                    A(lnv[:, b, :], ps[:, 2 + b, :], ACT.Ln, bias=v1("eps", n)).then_inc(s_lnv, 1)
                    act.wait_ge(s_lnv, nth(n, b))
                    A(rstd[:, b, :], lnv[:, b, :], ACT.Exp, scale=-0.5).then_inc(s_rstd, 1)

            def mlp(m):
                _, nb, _, _, bias, func, _ = MLPS[m]
                base = mlp_base[m]
                for b in range(B):
                    for j in range(nb):
                        act.wait_ge(s_m1, base + b * nb + j + 1)
                        A(hid[:, j, b, :], ps[:, 4 + (b * nb + j) % 4, :], func,
                          bias=v1(bias, j) if bias else 0.0).then_inc(s_hid, 1)

            def attention(a):
                s = att[a]
                if a == 0:
                    for n in range(4):
                        b, t = n // 2, n % 2
                        act.wait_ge(s["qf"], n + 1)
                        A(qh[t][:, b, :], xn[:, b, :] if t == 0 else junk[b][:], ACT.Copy).then_inc(s["hi"], 1)
                else:
                    act.wait_ge(s_ln, nth(6, B - 1))
                    for n in range(4):
                        b, t = n // 2, n % 2
                        act.wait_ge(s["qkv"], n + 1)
                        if t == 0:
                            A((xn, qs)[t][:, b, :], ps[:, 4 + n, :], ACT.Identity, bias=v1("l3_bq")).then_inc(s["rot"], 1)
                        else:
                            A((xn, qs)[t][:, b, :], ps[:, 4 + n, :], ACT.Copy).then_inc(s["rot"], 1)
                        act.wait_ge(s["rot"], n + 1)
                        A((xc, sq)[t][:, b, :], (xn, qs)[t][:, b, :], ACT.Square).then_inc(s["t1"], 1)
                    for n in range(4):
                        b, t = n // 2, n % 2
                        act.wait_ge(s["t2"], n + 1)
                        A((xc, sq)[t][:, b, :], (lnv, rstd)[t][:, b, :], ACT.Sqrt).then_inc(s["t1"], 1)
                    log_exp_table()
                    A(qmul[:, 1:2], qmul[:, 0:1], ACT.Exp).then_inc(s["t1"], 1)
                    for n in range(4):
                        b, t = n // 2, n % 2
                        act.wait_ge(s["t1"], 5 + n)
                        A((xc, sq)[t][:, b, :], (xc, sq)[t][:, b, :], ACT.Ln).then_inc(s["t1"], 1)
                        act.wait_ge(s["t1"], 10 + n)
                        A((lnv, rstd)[t][:, b, :], (xc, sq)[t][:, b, :], ACT.Exp, scale=-1.0).then_inc(s["nrm"], 1)
                    for n in range(4):
                        b, t = n // 2, n % 2
                        act.wait_ge(s["qf"], n + 1)
                        A(qh[t][:, b, :], (xn, qs)[t][:, b, :], ACT.Copy).then_inc(s["hi"], 1)

                def m_row(i):
                    act.wait_ge(s["m_turned"], i + 1)
                    if i >= 2:
                        act.wait_ge(s[f"mrow_in{i % 2}"], 32 * (i // 2))
                    A(mrow[i % 2][:], ps[0:2 * HG, 7, :], ACT.Copy).then_inc(s["m_row"], 1)

                def copy_o(i):
                    act.wait_ge(s["pv"], TT * (i + 1))
                    if i >= 2:
                        act.wait_ge(s["o_norm"], i - 1)
                    A(osb[i % 2][:], ps[:, 6, :], ACT.Copy).then_inc(s["o_copied"], 1)

                def invert(i):
                    act.wait_ge(s["o_sum"], i + 1)
                    if i >= 2:
                        act.wait_ge(s["o_norm"], i - 1)
                    A(orec[i % 2][:], ps[:, 7, :], ACT.Ln).then_inc(s["o_log"], 1)
                    act.wait_ge(s["o_log"], i + 1)
                    A(orec[i % 2][:], orec[i % 2][:], ACT.Exp, scale=-1.0).then_inc(s["o_rec"], 1)

                m_row(0)
                for c in range(8 * NG):
                    i = c // 8
                    act.wait_ge(s["b_score"], c + 1)
                    if c >= 4:
                        act.wait_ge(s["pv"], (c - 4) // 2 + 1)
                    A(prob[c % 4][:], ps[:, 2 * (c % 2):2 * (c % 2) + 2, :], ACT.Exp).then_inc(s["b_exp"], 1)
                    if c % 8 == 1 and i >= 1:
                        copy_o(i - 1)
                    if c % 8 == 5 and i + 1 < NG:
                        m_row(i + 1)
                    if c % 8 == 7 and i >= 1:
                        invert(i - 1)
                copy_o(NG - 1)
                invert(NG - 1)

            loaded(act, "cond")
            A(silc[:], wt["cond"], ACT.Silu).then_inc(s_silc, 1)
            norm(0)
            for b in range(B):
                act.wait_ge(s_kb, b + 1)
                A(ke[:, b, :], ps[:, 2 + b, :], ACT.Exp, bias=kmx[:, b, 2:3], accum_out=kmx[:, b, 3:4]).then_inc(s_ke, 1)
            for b in range(B):
                act.wait_ge(s_qd, b + 1)
                A(qe[:, b, :], qd[:, b, :], ACT.Exp).then_inc(s_qe, 1)
            for b in range(B):
                act.wait_ge(s_ktT, b + 1)
                A(ktok[:, b, :], ps[:, 6 + b, :], ACT.Copy).then_inc(s_ktok, 1)
            for b in range(B):
                act.wait_ge(s_y, b + 1)
                act.wait_ge(s_qd, b + 1)
                A(ysb[:, b, :], ps[:, 2 + b, :], ACT.Copy).then_inc(s_ysb, 1)
            norm(1)
            for b in range(B):
                act.wait_ge(s_ln, nth(1, b))
                A(silh[:, b, :], xm[:, b, :], ACT.Silu).then_inc(s_silh, 1)
            norm(2)
            mlp(0)
            norm(3)
            mlp(1)
            norm(4)
            attention(0)
            norm(5)
            mlp(2)
            norm(6)
            act.wait_ge(s_idr, 2)
            attention(1)
            norm(7)
            mlp(3)

        @block.gpsimd
        def _(gp):
            G = nc.gpsimd
            for u in range(RING):
                G.memset(kg[u][:].bitcast(F32), 0.0).then_inc(s_ones, 1)
            for u in range(RING):
                G.memset(qg[u][:].bitcast(F32), 0.0).then_inc(s_ones, 1)
            G.memset(vx[:, :, :, :, DH:DH + 1], 1.0).then_inc(s_ones, 1)
            G.memset(vx[:, :, :, :, DH + 1:SP], 0.0).then_inc(s_ones, 1)
            gp.wait_ge(ld_w[0], 16)
            G.tensor_scalar(qmul[:, 0:1], v1("scale"), float(np.log(100.0)), None, ALU.min).then_inc(s_idr, 1)

            def biased(k):
                for b in range(B):
                    x_ready(gp, k, b)
                    G.tensor_scalar(state_b[:, b, :], state[k % 2][:, b, :], gate_b[:, k, b:b + 1], None,
                                    ALU.add).then_inc(s_xb, 1)

            def attention(a):
                s = att[a]

                def group(i):
                    gp.wait_ge(s["v_ready"], TT * (1 + i // GB))
                    if i >= 2:
                        gp.wait_ge(s["pv"], TT * (i - 1))
                    G.tensor_copy(vg[i % 2][:], vx[:, i]).then_inc(s["v_group"], 1)

                if a == 0:
                    gp.wait_ge(s_ones, 8)
                group(0)
                group(1)
                for i in range(NG):
                    gp.wait_ge(s["o_rec"], i + 1)
                    G.tensor_tensor(onorm[:, i, :], osb[i % 2][:], orec[i % 2][:], ALU.mult).then_inc(s["o_norm"], 1)
                    if i + 2 < NG:
                        group(i + 2)

            gp.wait_ge(s_modok, 6)
            biased(0)
            biased(1)
            biased(2)
            attention(0)
            biased(5)
            attention(1)
            biased(6)


def kernel(**inputs):
    import concourse.bacc as bacc
    from concourse.bass_utils import run_bass_kernel_spmd

    d = {k: np.asarray(v) for k, v in inputs.items()}
    f = np.float32

    def strips(w):
        o = np.zeros((GB, HG, SP, P), f)
        o[:, :, :DH] = w.reshape(GB, HG, DH, P)
        return o.reshape(GB, P, P).transpose(1, 0, 2).reshape(P, GB * P)

    def blocked(w):
        return w.reshape(-1, P, w.shape[1]).transpose(1, 0, 2).reshape(P, -1)

    inv = 1.0 / 10000.0 ** (np.arange(0, DH, 2, dtype=f) / f(DH))
    ang = np.outer(np.arange(T, dtype=f), inv.astype(f)).astype(f)
    ang = np.concatenate([ang, ang], -1).T
    cos, sin = np.cos(ang).astype(f), np.sin(ang).astype(f)
    sin[: DH // 2] *= -1
    cos, sin = np.tile(cos, (H, 1)), np.tile(sin, (H, 1))
    turn = np.concatenate([np.arange(1, DH, 2), np.arange(0, DH, 2)])
    turn = (np.arange(H)[:, None] * DH + turn[None]).ravel()
    root = f(DH ** -0.5)

    e0, e1 = d["L0_cond_emb_W"].reshape(P, 2, P), d["L1_cond_ada_w"].reshape(P, 6, P)
    e2, e3 = d["L2_cond_ada_W"].reshape(P, 6, P), d["L3_cond_ada_w"].T.reshape(P, 6, P)
    b0, b1 = d["L0_cond_emb_b"].reshape(2, P), d["L1_cond_ada_b"].reshape(6, P)
    b2, b3 = d["L2_cond_ada_b"].reshape(6, P), d["L3_cond_ada_b"].reshape(6, P)
    order = [(0, 0), (1, 1), (1, 4), (2, 1), (2, 4), (3, 2), (3, 3), (0, 1), (1, 0), (1, 3), (2, 0), (2, 3), (3, 4), (3, 5),
             (1, 2), (1, 5), (2, 2), (2, 5), (3, 0), (3, 1)]
    E, Bm = (e0, e1, e2, e3), (b0, b1, b2, b3)
    mod = np.stack([E[l][:, j] for l, j in order], 1)
    modb = np.stack([Bm[l][j] for l, j in order], 1)
    one, zero = np.ones(P, f), np.zeros(P, f)

    def twice(cols):
        return np.stack([c for c in cols for _ in range(B)], 1)

    vec = np.zeros((P, NVEC), f)

    def put(name, cols):
        cols = cols.reshape(P, -1)
        vec[:, VEC[name]:VEC[name] + cols.shape[1]] = cols

    put("modb", modb)
    put("g", twice([d["L0_cond_norm_g"], d["L0_cond_sn_g"], one, one, d["L2_cond_norm1_g"], d["L2_cond_norm2_g"], one, one]))
    put("b", twice([d["L0_cond_norm_b"], d["L0_cond_sn_b"], zero, zero, d["L2_cond_norm1_b"], d["L2_cond_norm2_b"], zero, zero]))
    put("outb", twice([d["L0_cond_out_b"], d["L1_cond_ssm_b2"], d["L1_cond_ff_b2"], zero, zero, d["L3_cond_proj_b"],
                       d["L3_cond_fc2_b"]]))
    put("eps", np.tile(np.array(LN_EPS, f), (P, 1)))
    put("bk", d["L0_cond_bk"])
    put("l1_a", d["L1_cond_ssm_b1"])
    put("l1_c", d["L1_cond_ff_b1"].reshape(2, P).T)
    put("l3_a", d["L3_cond_fc1_b"].reshape(4, P).T)
    put("l3_bq", d["L3_cond_q_bias"])
    put("scale", np.repeat(d["L3_cond_scale_mul"].reshape(H), DH))

    def wide(row):
        return np.tile(row[None], (P, 1))

    blk = np.kron(np.eye(H, dtype=f), np.ones((DH, DH), f))
    sel = np.zeros((P, P), f)
    for j in range(HG):
        sel[SP * j + DH, SP * j:SP * (j + 1)] = 1
    qkv = d["L3_cond_qkv_w"].T
    parts = {
        "ones": np.full((P, P), 1.0 / P, f), "cond": d["cond_1024"].T, "vec": vec, "mod0": mod[:, 0:2].reshape(P, -1),
        "mod": mod[:, 2:].reshape(P, -1), "ident": np.eye(P, dtype=f), "blocks": blk, "sumsel": sel,
        "l0_q": d["L0_cond_Wq"], "l0_k": d["L0_cond_Wk"], "l0_v": d["L0_cond_Wv"], "l0_bq": wide(d["L0_cond_bq"]),
        "l0_bv": wide(d["L0_cond_bv"]), "l0_o": d["L0_cond_out_W"],
        "l1_a": d["L1_cond_ssm_w1"], "l1_b": d["L1_cond_ssm_w2"], "l1_c": d["L1_cond_ff_w1"], "l1_d": blocked(d["L1_cond_ff_w2"]),
        "cos": cos, "sin": sin, "qcos": cos * root, "qsin": sin * root,
        "l2_q": d["L2_cond_Wq"], "l2_qr": d["L2_cond_Wq"][:, turn], "l2_k": d["L2_cond_Wk"], "l2_kr": d["L2_cond_Wk"][:, turn],
        "l2_v": d["L2_cond_Wv"], "l2_o": strips(d["L2_cond_Wo"]), "l2_a": d["L2_cond_W1"], "l2_b": blocked(d["L2_cond_W2"]),
        "l3_q": qkv[:, :P], "l3_k": qkv[:, P:2 * P], "l3_v": qkv[:, 2 * P:], "l3_bv": wide(d["L3_cond_v_bias"]),
        "l3_o": strips(d["L3_cond_proj_w"].T), "l3_a": d["L3_cond_fc1_w"].T, "l3_b": blocked(d["L3_cond_fc2_w"].T),
    }
    arrays = {"xT": np.ascontiguousarray(d["x"].transpose(2, 0, 1))}
    for n, cols in enumerate(W_LOADS):
        arrays[f"weights{n}_in"] = np.ascontiguousarray(np.concatenate([parts[name] for name, _ in cols], 1))
    bias = d["fside_1x1xSxS_0"][0, 0]
    arrays["bias_by_query"] = np.ascontiguousarray(bias.reshape(TT, P, T).transpose(1, 0, 2))
    arrays["bias_by_key"] = np.ascontiguousarray(bias.T.reshape(TT, P, T).transpose(1, 0, 2))

    arrays["const_rows"] = np.stack([np.zeros((NG * HG, 2, T), f), np.ones((NG * HG, 2, T), f)])

    nc = bacc.Bacc("TRN2", target_bir_lowering=False, num_devices=1)
    ap = {n: nc.dram_tensor(n, a.shape, F32, kind="ExternalInput").ap() for n, a in arrays.items()}
    out = nc.dram_tensor("outT", [P, B, T], F32, kind="ExternalOutput").ap()
    build(nc, ap["xT"], [ap[f"weights{n}_in"] for n in range(len(W_LOADS))], ap["bias_by_query"], ap["bias_by_key"], ap["const_rows"], out)
    r = run_bass_kernel_spmd(nc, [arrays], core_ids=[0])
    return np.ascontiguousarray(r.results[0]["outT"].transpose(1, 2, 0))
```

```python
from contextlib import ExitStack

import numpy as np

import concourse.bass as bass
from concourse import mybir

ALU = mybir.AluOpType
ACT = mybir.ActivationFunctionType
AX = mybir.AxisListType
F32 = mybir.dt.float32
F32R = mybir.dt.float32r

P = 128
B, T, H, DH = 2, 512, 16, 8
TT = T // P
HG = 4
NG = B * H // HG
NE = NG * HG * TT
GB = H // HG
SP = 32
SPLIT = 3 * DH
SHIFT = SPLIT + 2
RING = 3
LN_SCALE, ROOT_LN_SCALE = 2.0 ** 16, 2.0 ** 8
NPROB = 16
BOUND, BIAS_RANGE = 60.0, 80.0
BANKS = 3
LAG = 24

LN_EPS = [1e-5, 1e-5, 1e-6, 1e-6, 1e-5, 1e-5, 1e-6, 1e-6]
NLN = len(LN_EPS)
LN_STATE = [0, None, 1, 2, 3, 4, 5, 6]
NMOD = 20
NUP = 7
NO_BIAS = (3, 4)

W_LOADS = [
    [("ones", 128), ("cond", 2), ("scales", 16), ("vec", 100), ("mod0", 256), ("ident", 128), ("blocks", 128), ("l0_q", 128),
     ("l0_k", 128), ("l0_v", 128), ("l0_bq", 128), ("l0_bv", 128), ("l0_o", 128)],
    [("mod", 18 * 128), ("l1_a", 128), ("l1_b", 128), ("l1_c", 256), ("l1_d", 256)],
    [("cos", 512), ("sin", 512), ("qcos", 512), ("qsin", 512), ("l2_q", 128), ("l2_qr", 128), ("l2_k", 128),
     ("l2_kr", 128), ("l2_v", 128), ("l2_o", 512), ("sumsel", HG), ("l2_a", 512), ("l2_b", 512)],
    [("l3_q", 128), ("l3_k", 128), ("l3_v", 128), ("l3_bv", 128), ("l3_o", 512), ("l3_a", 512), ("l3_b", 512)],
]
VEC = {}
_at = 0
for _name, _n in [("modb", NMOD), ("g", 2 * NLN), ("b", 2 * NLN), ("outb", 2 * NUP), ("eps", NLN), ("bk", 1),
                  ("l1_a", 1), ("l1_c", 2), ("l2_a", 0), ("l3_a", 4), ("l3_bq", 1), ("scale", 1)]:
    VEC[_name] = _at
    _at += _n
NVEC = 100

MLPS = [
    (2, 1, "l1_a", "l1_b", "l1_a", ACT.Gelu, 1),
    (3, 2, "l1_c", "l1_d", "l1_c", ACT.Gelu_apprx_tanh, 2),
    (5, 4, "l2_a", "l2_b", None, ACT.Gelu, 4),
    (7, 4, "l3_a", "l3_b", "l3_a", ACT.Gelu_apprx_tanh, 6),
]


def build(nc, xT, loads, bias_q, bias_k, rows_q, rows_k, out):
    ctx = ExitStack()
    with ctx:
        def sb(name, shape, dt=F32):
            return ctx.enter_context(nc.sbuf_tensor(name, shape, dt))

        def sem(name):
            return ctx.enter_context(nc.semaphore(name))

        wt, load_of = {}, {}
        tiles = []
        for n, cols in enumerate(W_LOADS):
            tile = sb(f"weights{n}", [P, sum(c for _, c in cols)])
            tiles.append(tile)
            at = 0
            for name, c in cols:
                wt[name] = tile[:, at:at + c]
                load_of[name] = n
                at += c
        vec = wt["vec"]
        ones, ident, blocks, sumsel = wt["ones"], wt["ident"], wt["blocks"], wt["sumsel"]
        state = [sb(f"state{k}", [P, B, T]) for k in range(2)]
        state_b = sb("state_b", [P, B, T])
        xc = sb("xc", [P, B, T])
        sq = sb("sq", [P, B, T])
        lnv = sb("lnv", [P, B, T])
        rstd = sb("rstd", [P, B, T])
        xn = sb("xn", [P, B, T])
        xm = sb("xm", [P, B, T])
        hid = sb("hid", [P, 4, B, T])
        silc = sb("silc", [P, 2])
        mods = sb("mods", [P, NMOD, B])
        scale1 = sb("scale1", [P, NLN - 1, B])
        ln_a = sb("ln_a", [P, NLN, B])
        ln_t = sb("ln_t", [P, NLN - 1, B])
        ln_b = sb("ln_b", [P, NLN, B])
        gate = sb("gate", [P, NUP, B])
        gate_b = sb("gate_b", [P, NUP, B])
        qs = sb("qs", [P, B, T])
        qd = hid[:, 0]
        qe = hid[:, 1]
        qp = hid[:, 2]
        qmx = sb("qmx", [P, B, TT * H])
        qsum = sb("qsum", [P, B, TT * H])
        kmx = sb("kmx", [P, B, 4])
        ke = hid[:, 3]
        ktok = lnv
        vtok = sq
        qT = rstd
        ysb = qs
        silh = xc
        qh = [hid[:, t].bitcast(F32R) for t in range(2)]
        ql = [hid[:, 2 + t].bitcast(F32R) for t in range(2)]
        vx = sb("vx", [P, NG, TT, HG, SP])
        qg = [sb(f"qg{u}", [P, T], F32R) for u in range(RING)]
        kg = [sb(f"kg{u}", [P, HG, T], F32R) for u in range(RING)]
        diag = sb("diag", [P, T])
        mx = [sb(f"mx{u}", [P, TT * HG]) for u in range(2)]
        nmx = [sb(f"nmx{u}", [P, TT, 2, HG], F32R) for u in range(2)]
        mrow = [sb(f"mrow{u}", [HG * 2, T], F32R) for u in range(2)]
        prob = [sb(f"prob{n}", [P, 2, T]) for n in range(NPROB // 2)]
        osb = [sb(f"osb{u}", [P, T]) for u in range(2)]
        inv = [sb(f"inv{u}", [P, TT * HG]) for u in range(2)]
        onorm = hid[:, :, :, :].rearrange("p a b t -> p (a b) t")
        junk = [sb(f"junk{n}", [P, T]) for n in range(2)]
        ctxm = junk[0][:, 0:B * P].rearrange("p (b n) -> p b n", b=B)
        bq_sb = wt["mod"][:, 0:TT * T].rearrange("p (q n) -> p q n", q=TT)
        bk_all = sb("bias_k", [P, TT, T])
        bk_sb = [bk_all[:, t, :] for t in range(TT)]
        qmul = sb("qmul", [P, 3])
        flag = sb("flag", [1, 1], mybir.dt.int32)
        smax = sb("smax", [1, 3])
        bmax = sb("bmax", [P, TT])
        bmin = sb("bmin", [P, TT])
        brange = sb("brange", [P, TT])
        over = sb("over", [P, 1])
        over_all = sb("over_all", [P, 1])
        scratch = {(a, t): nc.dram_tensor(f"split_{t}{a}", [NG, HG, SP if t == "q" else SHIFT, T], F32).ap()
                   for a in range(2) for t in "qk"}

        ps = ctx.enter_context(nc.psum_tensor("ps", [P, 8, T], F32))

        ld_x = [sem(f"ld_x{b}") for b in range(B)]
        ld_w = [sem(f"ld_w{n}") for n in range(len(W_LOADS))]
        ld_bq, ld_bk = sem("ld_bias_q"), sem("ld_bias_k")
        s_silc, s_modmm, s_mod, s_modok = sem("silu_cond"), sem("mod_products"), sem("mod_steps"), sem("mods_ready")
        s_x, s_xb = sem("x_ready"), sem("x_plus_bias")
        s_mean, s_xc, s_sq, s_var, s_lnv, s_rstd, s_xnn, s_ln = (
            sem(n) for n in ("ln_mean", "ln_centered", "ln_square", "ln_var", "ln_log", "ln_rstd", "ln_scaled", "ln_out"))
        s_m1, s_hid, s_m2 = sem("mlp_first"), sem("mlp_hidden"), sem("mlp_second")
        s_q0, s_k0, s_v0 = sem("l0_q"), sem("l0_k"), sem("l0_v")
        s_qstep, s_qd, s_qe, s_qp = sem("l0_q_steps"), sem("l0_q_shifted"), sem("l0_q_exp"), sem("l0_q_probs")
        s_kstep, s_kb, s_ke = sem("l0_k_steps"), sem("l0_k_shift"), sem("l0_k_exp")
        s_vtok, s_ktT, s_ktok, s_ctx, s_ctxm, s_qTp, s_qT, s_y, s_ysb, s_silh, s_o0 = (
            sem(n) for n in ("l0_v_ready", "l0_k_turned", "l0_k_tokens", "l0_ctx", "l0_ctx_ready", "l0_q_turned",
                             "l0_q_features", "l0_y", "l0_y_ready", "l0_silu", "l0_out"))
        s_rows = sem("rows_written")
        s_ones, s_qmul = sem("ones_rows"), sem("scale_clipped")
        att = []
        for a in range(3):
            att.append({n: sem(f"{n}{a}") for n in (
                "stage0", "stage1", "stage2", "b_raw", "b_exp", "pv", "o_copied", "o_sum", "o_inv", "o_spread",
                "o_norm") + (("bias_exp", "dv_biased", "gp_biased") if a == 2 else
                             ("mrow_in0", "mrow_in1", "a_score", "a_max", "nm_hi", "nm_lo", "m_turned", "m_row"))})
            if a == 1:
                att[a]["b_score"] = sem("b_score1")
            if a < 2:
                att[a] |= {n: sem(f"{n}{a}") for n in (
                    "qkv", "rot", "qsum", "hi", "lo", "split_w0", "split_w1", "v_mm", "v_ready", "proj", "t1", "t2", "qf",
                    "nrm", "q_scale", "ln")}
        BOUNDED = 2
        s_flag0, s_over, s_flag, s_bmax, s_bshift, s_bdiag, s_bspread, s_bks = (
            sem(n) for n in ("flag_steps", "over_bounds_summed", "flag", "bias_max", "bias_shifted", "bias_diag",
                             "bias_shift_spread", "bias_k_shifted"))
        s_out = sem("out_written")

        def w(name, a=0, n=P):
            return wt[name][:, a:a + n]

        def prob_of(e):
            return prob[e % NPROB // 2][:, e % 2, :]

        def out_bank(v, i):
            return 6 + i % 2 if v == BOUNDED else 6

        def turn_bank(v, i):
            return 6 + i % 2 if v == BOUNDED else 7

        def v1(name, k=0):
            return vec[:, VEC[name] + k:VEC[name] + k + 1]

        def x_ready(eng, k, b):
            if k == 0:
                eng.wait_ge(ld_x[b], 16)
            else:
                eng.wait_ge(s_x, 2 * (k - 1) + b + 1)

        def loaded(eng, name):
            eng.wait_ge(ld_w[load_of[name]], 16)

        def nth(n, b):
            return 2 * n + b + 1

        def by_bound(eng, program):
            eng.wait_ge(s_flag, 1)
            unbounded = eng.value_load(flag[0:1, 0:1], min_val=0, max_val=1)
            with eng.If(unbounded == 0):
                program(BOUNDED)
            with eng.Else():
                program(1)

        mlp_base, at = [], 0
        for m in MLPS:
            mlp_base.append(at)
            at += 2 * m[1]
        up_of_mlp = {m[6]: n for n, m in enumerate(MLPS)}

        block = ctx.enter_context(nc.Block())

        @block.sync
        def _(sp):
            sp.dma_start(state[0][:, 0, :], xT[:, 0, :]).then_inc(ld_x[0], 16)
            sp.dma_start(tiles[0][:], loads[0]).then_inc(ld_w[0], 16)
            sp.dma_start(state[0][:, 1, :], xT[:, 1, :]).then_inc(ld_x[1], 16)
            for n in range(1, len(W_LOADS)):
                sp.dma_start(tiles[n][:], loads[n]).then_inc(ld_w[n], 16)
            sp.dma_start(bk_all[:], bias_k).then_inc(ld_bk, 16)
            sp.wait_ge(s_modmm, 1)
            sp.dma_start(bq_sb, bias_q).then_inc(ld_bq, 16)
            for a in range(2):
                for t, rows in (("q", rows_q), ("k", rows_k)):
                    sp.dma_start(scratch[a, t][:, :, SPLIT:, :].rearrange("i j r n -> (i j) r n"), rows).then_inc(s_rows, 16)
            for a in range(2):
                s = att[a]
                def send(b):
                    for t in range(2):
                        sp.wait_ge(att[a]["lo"], 2 * b + t + 1)
                        rows = [(qh, 0), (qh, 1), (ql, 2)] if t == 0 else [(qh, 0), (ql, 1), (qh, 2)]
                        for half, r in rows:
                            dst = scratch[a, "qk"[t]][b * GB:(b + 1) * GB, :, r * DH:(r + 1) * DH, :]
                            sp.dma_start(dst.rearrange("g j d n -> (g j) d n"),
                                         half[t][:, b, :].bitcast(F32)).then_inc(att[a][f"split_w{b}"], 16)

                def groups(v):
                    s = att[v]

                    def stage(i):
                        if i >= RING:
                            sp.wait_ge(s["b_raw"], 16 * (i - RING + 1))
                        if i % GB == 0:
                            sp.wait_ge(att[a][f"split_w{i // GB}"], 16 * 6)
                        done = s[f"stage{i % RING}"]
                        sp.dma_start(qg[i % RING][:].bitcast(F32),
                                     scratch[a, "q"][i].rearrange("j r n -> (j r) n")).then_inc(done, 16)
                        for j in range(HG):
                            rows = slice(SP * j, SP * j + SHIFT)
                            sp.dma_start(kg[i % RING][rows, j, :].bitcast(F32), scratch[a, "k"][i, j]).then_inc(done, 16)

                    def stage_m(i):
                        sp.wait_ge(s["m_row"], i + 1)
                        for t in range(2):
                            sp.dma_start(qg[i % RING][SPLIT + t::SP, :].bitcast(F32),
                                         mrow[i % 2][t * HG:(t + 1) * HG, :].bitcast(F32)).then_inc(s[f"mrow_in{i % 2}"], 16)

                    stage(0)
                    send(1)
                    stage(1)
                    if v != BOUNDED:
                        stage_m(0)
                    for i in range(NG):
                        if i + 2 < NG:
                            stage(i + 2)
                        if v != BOUNDED and i + 1 < NG:
                            stage_m(i + 1)

                send(0)
                sp.wait_ge(s_rows, 64)
                if a == 0:
                    sp.wait_ge(s_ones, RING)
                    groups(0)
                else:
                    by_bound(sp, groups)
            for b in range(B):
                x_ready(sp, NUP, b)
                sp.dma_start(out[:, b, :], state[NUP % 2][:, b, :]).then_inc(s_out, 16)
            sp.wait_ge(s_out, 16 * B)

        @block.tensor
        def _(pe):
            mm = nc.tensor.matmul

            def norm(n):
                for b in range(B):
                    if LN_STATE[n] is None:
                        pe.wait_ge(s_ysb, b + 1)
                        src = ysb
                    else:
                        x_ready(pe, LN_STATE[n], b)
                        src = state[LN_STATE[n] % 2]
                    mm(ps[:, b, :], ones, src[:, b, :], start=True, stop=True).then_inc(s_mean, 1)
                for b in range(B):
                    pe.wait_ge(s_sq, nth(n, b))
                    mm(ps[:, 2 + b, :], ones, sq[:, b, :], start=True, stop=True).then_inc(s_var, 1)

            def mlp(m):
                n, nb, w1, w2, _, _, _ = MLPS[m]
                base = mlp_base[m]
                for b in range(B):
                    pe.wait_ge(s_ln, nth(n, b))
                    for j in range(nb):
                        c = b * nb + j
                        if c >= 4:
                            pe.wait_ge(s_hid, base + c - 3)
                        mm(ps[:, 4 + c % 4, :], w(w1, j * P), xm[:, b, :], start=True, stop=True).then_inc(s_m1, 1)
                for b in range(B):
                    for j in range(nb):
                        pe.wait_ge(s_hid, base + b * nb + j + 1)
                        last = mm(ps[:, b, :], w(w2, j * P), hid[:, j, b, :], start=(j == 0), stop=(j == nb - 1))
                    last.then_inc(s_m2, 1)

            def attention(a):
                s = att[a]

                def softmax(v):
                    s = att[v]
                    ring = 2 * BANKS if v == BOUNDED else BANKS

                    def a_block(n):
                        i, qt, j = n // 16, n % 16 // 4, n % 4
                        if n % 16 == 0:
                            pe.wait_ge(s[f"stage{i % RING}"], (1 + HG) * 16 * (i // RING + 1))
                        if n >= BANKS:
                            pe.wait_ge(s["a_max"], n - BANKS + 1)
                        mm(ps[:, BANKS + n % BANKS, :], qg[i % RING][:, qt * P:(qt + 1) * P], kg[i % RING][:, j, :],
                           start=True, stop=True).then_inc(s["a_score"], 1)

                    def turn_max(i):
                        pe.wait_ge(s["nm_lo"], i + 1)
                        if i >= 1:
                            pe.wait_ge(s["m_row"], i)
                        if i >= 2:
                            pe.wait_ge(s["o_inv"], i - 1)
                        for qt in range(TT):
                            last = nc.tensor.transpose(ps[0:2 * HG, 7, qt * P:(qt + 1) * P],
                                                       nmx[i % 2][:, qt, :, :].rearrange("p t j -> p (t j)").bitcast(F32),
                                                       ident)
                        last.then_inc(s["m_turned"], 1)

                    def score(e):
                        i, kt, j = e // 16, e % 16 // 4, e % 4
                        if e % 16 == 0:
                            if v == BOUNDED:
                                pe.wait_ge(s[f"stage{i % RING}"], (1 + HG) * 16 * (i // RING + 1))
                            else:
                                pe.wait_ge(s[f"mrow_in{i % 2}"], 32 * (i // 2 + 1))
                        if e >= ring:
                            pe.wait_ge(s["b_exp"], e - ring + 1)
                        mm(ps[:, e % ring, :], kg[i % RING][:, j, kt * P:(kt + 1) * P], qg[i % RING][:],
                           start=True, stop=True).then_inc(s["b_raw"], 1)

                    def values(n):
                        i, kt = n // TT, n % TT
                        if v == BOUNDED:
                            pe.wait_ge(s["dv_biased"], 3 * (n + 1))
                            pe.wait_ge(s["gp_biased"], n + 1)
                        else:
                            pe.wait_ge(s["b_exp"], 4 * n + 4)
                        if kt == 0:
                            pe.wait_ge(att[a]["v_ready"], TT * (1 + i // GB))
                            if v == BOUNDED and i >= 2:
                                pe.wait_ge(s["o_norm"], i - 1)
                            if v != BOUNDED and i >= 1:
                                pe.wait_ge(s["o_copied"], i)
                        for j in range(HG):
                            last = mm(ps[SP * j:SP * (j + 1), out_bank(v, i), :], vx[:, i, kt, j, :], prob_of(4 * n + j),
                                      start=(kt == 0), stop=(kt == TT - 1))
                        last.then_inc(s["pv"], 1)

                    def turn_sums(i):
                        pe.wait_ge(s["o_copied"], i + 1)
                        if v != BOUNDED and i >= 1:
                            pe.wait_ge(s["o_norm"], i)
                        if v != BOUNDED:
                            pe.wait_ge(s["m_row"], min(i + 2, NG))
                        for qt in range(TT):
                            last = mm(ps[:, turn_bank(v, i), qt * HG:(qt + 1) * HG], osb[i % 2][:, qt * P:(qt + 1) * P], sumsel,
                                      start=True, stop=True)
                        last.then_inc(s["o_sum"], 1)

                    def spread(i):
                        pe.wait_ge(s["o_inv"], i + 1)
                        if v != BOUNDED:
                            pe.wait_ge(s["m_row"], min(i + 3, NG))
                        for qt in range(TT):
                            for j in range(HG):
                                wide = inv[i % 2][:, qt * HG + j:qt * HG + j + 1].to_broadcast([P, SP])
                                last = mm(ps[SP * j:SP * (j + 1), turn_bank(v, i), qt * P:(qt + 1) * P], wide, ident, start=True, stop=True)
                        last.then_inc(s["o_spread"], 1)

                    pe.wait_ge(att[a]["rot"], (8, 2)[a])
                    pe.wait_ge(att[a]["qf"], 4)
                    pe.wait_ge(att[a]["v_ready"], B * TT)
                    if v != BOUNDED:
                        for n in range(LAG):
                            if n == 20:
                                turn_max(0)
                            a_block(n)
                    back = 13 if v == BOUNDED else ring + 3
                    for e in range(NE + back - 2):
                        i = e // 16
                        if e < NE:
                            score(e)
                        if v != BOUNDED and e + LAG < NE:
                            a_block(e + LAG)
                        if e >= back and (e - back) % 4 == 0:
                            values((e - back) // 4)
                        if v != BOUNDED and e % 16 == 11 and i + 1 < NG:
                            turn_max(i + 1)
                        if v == 0 and e == NE - 8:
                            pe.wait_ge(s_bdiag, TT)
                            mm(ps[:, BANKS, :], ones, diag[:], start=True, stop=True).then_inc(s_bspread, 1)
                            pe.wait_ge(s_flag0, 3)
                            mm(ps[:, BANKS + 1, 0:1], ones, over_all[:], start=True, stop=True).then_inc(s_over, 1)
                        if v != BOUNDED and e % 16 == 6 and 1 <= i < NG:
                            turn_sums(i - 1)
                        if v != BOUNDED and e % 16 == 14 and 1 <= i < NG:
                            spread(i - 1)
                        if v == BOUNDED and e % 16 == 3 and 2 <= i:
                            turn_sums(i - 2)
                        if v == BOUNDED and e % 16 == 7 and 2 <= i:
                            spread(i - 2)
                    turn_sums(NG - 1)
                    spread(NG - 1)
                    for b in range(B):
                        for g in range(GB):
                            pe.wait_ge(s["o_norm"], b * GB + g + 1)
                            last = mm(ps[:, b, :], w(("l2_o", "l3_o")[a], g * P), onorm[:, b * GB + g, :],
                                      start=(g == 0), stop=(g == GB - 1))
                        last.then_inc(att[a]["proj"], 1)

                if a == 0:
                    for b in range(B):
                        pe.wait_ge(s_ln, nth(4, b))
                        if b == 0:
                            loaded(pe, "l2_q")
                        for n, name in enumerate(("l2_q", "l2_qr", "l2_k", "l2_kr")):
                            if b:
                                pe.wait_ge(s["rot"], n + 1)
                            mm(ps[:, 4 + n, :], w(name), xm[:, b, :], start=True, stop=True).then_inc(s["qkv"], 1)
                        for t in range(TT):
                            last = mm(ps[:, b, t * P:(t + 1) * P], xm[:, b, t * P:(t + 1) * P], w("l2_v"),
                                      start=True, stop=True)
                        last.then_inc(s["v_mm"], 1)
                else:
                    for b in range(B):
                        pe.wait_ge(s_ln, nth(6, b))
                        for n, name in enumerate(("l3_q", "l3_k")):
                            mm(ps[:, 4 + 2 * b + n, :], w(name), xm[:, b, :], start=True, stop=True).then_inc(s["qkv"], 1)
                        for t in range(TT):
                            last = mm(ps[:, b, t * P:(t + 1) * P], xm[:, b, t * P:(t + 1) * P], w("l3_v"),
                                      start=True, stop=True)
                        last.then_inc(s["v_mm"], 1)
                    for n in range(4):
                        pe.wait_ge(s["t1"], n + 1)
                        if n >= 2:
                            pe.wait_ge(s["t2"], n - 1)
                        mm(ps[:, 2 + n % 2, :], blocks, (xc, sq)[n % 2][:, n // 2, :], start=True, stop=True).then_inc(s["qsum"], 1)

                if a == 0:
                    softmax(0)
                else:
                    by_bound(pe, softmax)

            loaded(pe, "ones")
            pe.wait_ge(s_silc, 1)
            norm(0)
            for b in range(B):
                pe.wait_ge(s_ln, nth(0, b))
                for t in range(TT):
                    last = mm(ps[:, 4 + b, t * P:(t + 1) * P], xm[:, b, t * P:(t + 1) * P], w("l0_q"), start=True, stop=True)
                last.then_inc(s_q0, 1)
                for t in range(TT):
                    last = mm(ps[:, b, t * P:(t + 1) * P], xm[:, b, t * P:(t + 1) * P], w("l0_v"), start=True, stop=True)
                last.then_inc(s_v0, 1)
                mm(ps[:, 2 + b, :], w("l0_k"), xm[:, b, :], start=True, stop=True).then_inc(s_k0, 1)
            for j in range(NMOD):
                if j == 2:
                    loaded(pe, "mod")
                wj = w("mod0", j * P) if j < 2 else w("mod", (j - 2) * P)
                last = mm(ps[:, 7, 2 * j:2 * j + 2], wj, silc[:], start=True, stop=True)
            last.then_inc(s_modmm, 1)
            pe.wait_ge(s_mod, 1)
            for b in range(B):
                pe.wait_ge(s_ke, b + 1)
                for t in range(TT):
                    last = nc.tensor.transpose(ps[:, 6 + b, t * P:(t + 1) * P], ke[:, b, t * P:(t + 1) * P], ident)
                last.then_inc(s_ktT, 1)
            for b in range(B):
                pe.wait_ge(s_ktok, b + 1)
                pe.wait_ge(s_vtok, b + 1)
                for t in range(TT):
                    last = mm(ps[:, b, 0:P], ktok[:, b, t * P:(t + 1) * P], vtok[:, b, t * P:(t + 1) * P],
                              start=(t == 0), stop=(t == TT - 1))
                last.then_inc(s_ctx, 1)
            for b in range(B):
                pe.wait_ge(s_qp, b + 1)
                for t in range(TT):
                    last = nc.tensor.transpose(ps[:, 4 + b, t * P:(t + 1) * P], qp[:, b, t * P:(t + 1) * P], ident)
                last.then_inc(s_qTp, 1)
            for b in range(B):
                pe.wait_ge(s_qT, b + 1)
                pe.wait_ge(s_ctxm, b + 1)
                mm(ps[:, 2 + b, :], ctxm[:, b, :], qT[:, b, :], start=True, stop=True).then_inc(s_y, 1)
            norm(1)
            for b in range(B):
                pe.wait_ge(s_silh, b + 1)
                mm(ps[:, b, :], w("l0_o"), silh[:, b, :], start=True, stop=True).then_inc(s_o0, 1)
            norm(2)
            mlp(0)
            norm(3)
            mlp(1)
            norm(4)
            attention(0)
            norm(5)
            mlp(2)
            norm(6)
            loaded(pe, "l3_q")
            attention(1)
            norm(7)
            mlp(3)

        @block.vector
        def _(dv):
            V = nc.vector

            def norm(n):
                for b in range(B):
                    dv.wait_ge(s_mean, nth(n, b))
                    src = ysb if LN_STATE[n] is None else state[LN_STATE[n] % 2]
                    if LN_STATE[n] is None:
                        dv.wait_ge(s_ysb, b + 1)
                    else:
                        x_ready(dv, LN_STATE[n], b)
                    V.tensor_tensor(xc[:, b, :], src[:, b, :], ps[:, b, :], ALU.subtract).then_inc(s_xc, 1)
                for b in range(B):
                    dv.wait_ge(s_rstd, nth(n, b))
                    dv.wait_ge(s_xc, nth(n, b))
                    V.tensor_tensor(xn[:, b, :], xc[:, b, :], rstd[:, b, :], ALU.mult).then_inc(s_xnn, 1)
                    dv.wait_ge(s_xnn, nth(n, b))
                    V.tensor_scalar(xm[:, b, :], xn[:, b, :], ln_a[:, n, b:b + 1], ln_b[:, n, b:b + 1],
                                    ALU.mult, ALU.add).then_inc(s_ln, 1)

            def update(k, ready, base):
                for b in range(B):
                    dv.wait_ge(ready, base + b + 1)
                    if k in NO_BIAS:
                        x_ready(dv, k, b)
                        src = state[k % 2]
                    else:
                        dv.wait_ge(s_xb, [0, 1, 2, None, None, 3, 4][k] * 2 + b + 1)
                        src = state_b
                    V.scalar_tensor_tensor(out=state[(k + 1) % 2][:, b, :], in0=ps[:, b, :], scalar=gate[:, k, b:b + 1],
                                           in1=src[:, b, :], op0=ALU.mult, op1=ALU.add).then_inc(s_x, 1)

            def split_pair(s, b, t, src, ready, count):
                dv.wait_ge(ready, count)
                dv.wait_ge(s["hi"], 2 * b + t + 1)
                V.tensor_tensor(ql[t][:, b, :], src, qh[t][:, b, :].bitcast(F32), ALU.subtract).then_inc(s["lo"], 1)

            def attention(a):
                s = att[a]
                if a == 0:
                    for b in range(B):
                        for n, (name, dst) in enumerate((("qcos", xc), ("qsin", sq), ("cos", lnv), ("sin", rstd))):
                            dv.wait_ge(s["qkv"], 4 * b + n + 1)
                            V.tensor_tensor(dst[:, b, :], ps[:, 4 + n, :], wt[name], ALU.mult).then_inc(s["rot"], 1)
                        for t in range(2):
                            dst = xn[:, b, :] if t == 0 else junk[b][:]
                            dv.wait_ge(s["rot"], 4 * b + 2 * t + 2)
                            x1, x2 = ((xc, sq), (lnv, rstd))[t]
                            V.tensor_tensor(dst, x1[:, b, :], x2[:, b, :], ALU.add).then_inc(s["qf"], 1)
                        for t in range(2):
                            split_pair(s, b, t, xn[:, b, :] if t == 0 else junk[b][:], s["qf"], 2 * b + t + 1)
                else:
                    def values(b):
                        dv.wait_ge(s["v_mm"], b + 1)
                        if b == 0:
                            dv.wait_ge(att[0]["pv"], NE // HG)
                        for t in range(TT):
                            V.tensor_tensor(vx[:, b * GB:(b + 1) * GB, t, :, 0:DH],
                                            ps[:, b, t * P:(t + 1) * P].rearrange("p (g j d) -> p g j d", g=GB, j=HG),
                                            wt["l3_bv"].rearrange("p (g j d) -> p g j d", g=GB, j=HG),
                                            ALU.add).then_inc(s["v_ready"], 1)

                    for b in range(B):
                        for t in range(2):
                            dv.wait_ge(s["qsum"], 2 * b + t + 1)
                            V.tensor_scalar((lnv, rstd)[t][:, b, :], ps[:, 2 + t, :], 1e-24, None,
                                            ALU.max).then_inc(s["t2"], 1)
                        if b == 0:
                            dv.wait_ge(s["q_scale"], 1)
                            V.tensor_scalar(qmul[:, 2:3], qmul[:, 1:2], ROOT_LN_SCALE, None, ALU.mult).then_inc(s["q_scale"], 1)
                            dv.wait_ge(s["q_scale"], 2)
                        for t in range(2):
                            n = 2 * b + t
                            dv.wait_ge(s["nrm"], n + 1)
                            if t == 0:
                                dv.wait_ge(s["rot"], b + 1)
                            src = xn[:, b, :] if t == 0 else ps[:, 5 + 2 * b, :]
                            V.scalar_tensor_tensor(out=(xn, qs)[t][:, b, :], in0=src,
                                                   scalar=(qmul[:, 2:3], ROOT_LN_SCALE)[t], in1=(lnv, rstd)[t][:, b, :],
                                                   op0=ALU.mult, op1=ALU.mult).then_inc(s["qf"], 1)
                        for t in range(2):
                            split_pair(s, b, t, (xn, qs)[t][:, b, :], s["qf"], 2 * b + t + 1)
                        values(b)

                def softmax(v):
                    s = att[v]

                    def maximum(n):
                        i, c = n // 16, n % 16
                        dv.wait_ge(s["a_score"], n + 1)
                        dst = mx[i % 2][:, c:c + 1]
                        bank = ps[:, BANKS + n % BANKS, :]
                        if v == 0:
                            V.tensor_reduce(dst, bank, AX.X, ALU.max).then_inc(s["a_max"], 1)
                        else:
                            if n >= 2:
                                dv.wait_ge(s["a_max"], n - 1)
                            V.tensor_tensor_reduce(junk[n % 2][:], bank, bq_sb[:, c // 4, :], 1.0, -3e38,
                                                   ALU.add, ALU.max, dst).then_inc(s["a_max"], 1)
                        if c == 15:
                            dv.wait_ge(s["a_max"], n + 1)
                            if i >= 2:
                                dv.wait_ge(s["m_turned"], i - 1)
                            m = mx[i % 2][:].rearrange("p (q j) -> p q j", q=TT)
                            V.tensor_scalar(nmx[i % 2][:, :, 0, :], m, -1.0, None, ALU.mult).then_inc(s["nm_hi"], 1)
                            dv.wait_ge(s["nm_hi"], i + 1)
                            V.scalar_tensor_tensor(out=nmx[i % 2][:, :, 1, :], in0=m, scalar=-1.0,
                                                   in1=nmx[i % 2][:, :, 0, :].bitcast(F32), op0=ALU.mult,
                                                   op1=ALU.subtract).then_inc(s["nm_lo"], 1)

                    def invert(i):
                        dv.wait_ge(s["o_sum"], i + 1)
                        if i >= 2:
                            dv.wait_ge(s["o_spread"], i - 1)
                        V.reciprocal(inv[i % 2][:], ps[:, turn_bank(v, i), 0:TT * HG]).then_inc(s["o_inv"], 1)

                    def normalise(i):
                        dv.wait_ge(s["o_spread"], i + 1)
                        V.tensor_tensor(onorm[:, i, :], osb[i % 2][:], ps[:, turn_bank(v, i), :],
                                        ALU.mult).then_inc(s["o_norm"], 1)

                    def add_bias(e):
                        bank = ps[:, e % BANKS, :]
                        dv.wait_ge(s["b_raw"], e + 1)
                        V.tensor_tensor(bank, bank, bk_sb[e % 16 // 4], ALU.add).then_inc(s["b_score"], 1)

                    if v != BOUNDED:
                        for n in range(NE):
                            maximum(n)
                            if v == 1 and n >= LAG:
                                add_bias(n - LAG)
                            if n % 16 == 2 and n // 16 >= 3:
                                invert(n // 16 - 3)
                            if n % 16 == 8 and n // 16 >= 3:
                                normalise(n // 16 - 3)
                        for e in range(NE - LAG, NE):
                            if v == 1:
                                add_bias(e)
                            if e == NE - 22:
                                invert(NG - 3)
                            if e == NE - 12:
                                if v == 0:
                                    bias_maxima()
                                    bias_range()
                                normalise(NG - 3)
                            if e == NE - 6:
                                invert(NG - 2)
                        if v == 0:
                            bias_shift()
                        normalise(NG - 2)
                        invert(NG - 1)
                        normalise(NG - 1)
                    else:
                        for n in range(NE // HG):
                            i, kt = n // TT, n % TT
                            if n == 0:
                                dv.wait_ge(s["bias_exp"], TT)
                            dv.wait_ge(s["b_exp"], 4 * n + 2)
                            pair = prob[4 * n % NPROB // 2]
                            V.tensor_tensor(pair[:], pair[:], bk_sb[kt].unsqueeze(1).to_broadcast([P, 2, T]),
                                            ALU.mult).then_inc(s["dv_biased"], 2)
                            dv.wait_ge(s["b_exp"], 4 * n + 4)
                            V.tensor_tensor(prob_of(4 * n + 2), prob_of(4 * n + 2), bk_sb[kt],
                                            ALU.mult).then_inc(s["dv_biased"], 1)
                            if kt == 3 and i >= 1:
                                invert(i - 1)
                            if kt == 0 and i >= 2:
                                normalise(i - 2)
                        normalise(NG - 2)
                        invert(NG - 1)
                        normalise(NG - 1)

                if a == 0:
                    softmax(0)
                else:
                    by_bound(dv, softmax)

            def bias_maxima():
                dv.wait_ge(ld_bq, 16)
                V.tensor_reduce(bmax[:], bq_sb, AX.X, ALU.max).then_inc(s_bmax, 1)
                dv.wait_ge(s_bmax, 1)
                for t in range(TT):
                    V.tensor_scalar(diag[:, t * P:(t + 1) * P], ident, bmax[:, t:t + 1], float(P),
                                    ALU.mult, ALU.mult).then_inc(s_bdiag, 1)

            def bias_range():
                V.tensor_reduce(bmin[:], bq_sb, AX.X, ALU.min).then_inc(s_bmax, 1)
                dv.wait_ge(s_bmax, 2)
                V.tensor_tensor(brange[:], bmax[:], bmin[:], ALU.subtract).then_inc(s_bmax, 1)
                dv.wait_ge(s_bmax, 3)
                V.tensor_reduce(over[:], brange[:], AX.X, ALU.max).then_inc(s_bmax, 1)
                dv.wait_ge(s_bmax, 4)
                V.tensor_scalar(over_all[:], over[:], BIAS_RANGE, None, ALU.is_gt).then_inc(s_flag0, 1)

            def bias_shift():
                for t in range(TT):
                    V.tensor_scalar(bq_sb[:, t, :], bq_sb[:, t, :], bmax[:, t:t + 1], None,
                                    ALU.subtract).then_inc(s_bshift, 1)
                dv.wait_ge(s_bspread, 1)
                dv.wait_ge(ld_bk, 16)
                for t in range(TT):
                    V.tensor_tensor(bk_sb[t], bk_sb[t], ps[:, BANKS, :], ALU.subtract).then_inc(s_bks, 1)
                dv.wait_ge(s_over, 1)
                V.tensor_tensor(smax[:, 2:3], ps[0:1, BANKS + 1, 0:1], smax[:, 1:2], ALU.add).then_inc(s_flag0, 1)
                dv.wait_ge(s_flag0, 4)
                V.tensor_scalar(flag[:], smax[:, 2:3], 0.0, None, ALU.is_gt).then_inc(s_flag, 1)

            dv.wait_ge(ld_w[0], 16)
            V.tensor_reduce(smax[:, 0:1], wt["scales"][0:1, :], AX.X, ALU.max).then_inc(s_flag0, 1)
            dv.wait_ge(s_flag0, 1)
            V.tensor_scalar(smax[:, 1:2], smax[:, 0:1], float(np.log(BOUND)), None, ALU.is_gt).then_inc(s_flag0, 1)
            dv.wait_ge(ld_w[0], 16)
            V.tensor_copy(ln_a[:, 0, :], vec[:, VEC["g"]:VEC["g"] + 2]).then_inc(s_modok, 1)
            V.tensor_copy(ln_b[:, 0, :], vec[:, VEC["b"]:VEC["b"] + 2]).then_inc(s_modok, 1)
            V.tensor_copy(gate[:, 0, :], wt["cond"]).then_inc(s_modok, 1)
            dv.wait_ge(s_modok, 2)
            norm(0)
            for b in range(B):
                dv.wait_ge(s_k0, b + 1)
                V.tensor_reduce(kmx[:, b, 0:1], ps[:, 2 + b, :], AX.X, ALU.max).then_inc(s_kstep, 1)
                dv.wait_ge(s_kstep, 2 * b + 1)
                V.tensor_tensor(kmx[:, b, 1:2], kmx[:, b, 0:1], v1("bk"), ALU.add).then_inc(s_kstep, 1)
                dv.wait_ge(s_kstep, 2 * b + 2)
                V.tensor_tensor(kmx[:, b, 2:3], v1("bk"), kmx[:, b, 1:2], ALU.subtract).then_inc(s_kb, 1)
            h8 = "p (h d) -> p h d"
            for b in range(B):
                dv.wait_ge(s_q0, b + 1)
                V.tensor_tensor(qs[:, b, :].rearrange("p (t n) -> p t n", t=TT),
                                ps[:, 4 + b, :].rearrange("p (t n) -> p t n", t=TT),
                                wt["l0_bq"].unsqueeze(1).to_broadcast([P, TT, P]), ALU.add).then_inc(s_qstep, 1)
                dv.wait_ge(s_qstep, 2 * b + 1)
                V.tensor_reduce(qmx[:, b, :], qs[:, b, :].rearrange(h8, d=DH), AX.X, ALU.max).then_inc(s_qstep, 1)
                dv.wait_ge(s_qstep, 2 * b + 2)
                V.tensor_tensor(qd[:, b, :].rearrange(h8, d=DH), qs[:, b, :].rearrange(h8, d=DH),
                                qmx[:, b, :].unsqueeze(2).to_broadcast([P, TT * H, DH]), ALU.subtract).then_inc(s_qd, 1)
            dv.wait_ge(s_modmm, 1)
            V.tensor_tensor(mods[:], ps[:, 7, 0:2 * NMOD].rearrange("p (m b) -> p m b", b=B),
                            vec[:, VEC["modb"]:VEC["modb"] + NMOD].unsqueeze(2).to_broadcast([P, NMOD, B]),
                            ALU.add).then_inc(s_mod, 1)
            dv.wait_ge(s_mod, 1)
            V.tensor_scalar(scale1[:], mods[:, 0:7, :], 1.0, None, ALU.add).then_inc(s_mod, 1)
            V.tensor_copy(gate[:, 1:NUP, :], mods[:, 14:20, :]).then_inc(s_mod, 1)
            dv.wait_ge(s_mod, 3)
            V.tensor_tensor(ln_a[:, 1:NLN, :], scale1[:],
                            vec[:, VEC["g"] + 2:VEC["g"] + 2 * NLN].rearrange("p (n b) -> p n b", b=B),
                            ALU.mult).then_inc(s_modok, 1)
            V.tensor_tensor(ln_t[:], scale1[:], vec[:, VEC["b"] + 2:VEC["b"] + 2 * NLN].rearrange("p (n b) -> p n b", b=B),
                            ALU.mult).then_inc(s_mod, 1)
            dv.wait_ge(s_modok, 3)
            V.tensor_tensor(gate_b[:], gate[:], vec[:, VEC["outb"]:VEC["outb"] + 2 * NUP].rearrange("p (n b) -> p n b", b=B),
                            ALU.mult).then_inc(s_modok, 1)
            dv.wait_ge(s_mod, 4)
            V.tensor_tensor(ln_b[:, 1:NLN, :], ln_t[:], mods[:, 7:14, :], ALU.add).then_inc(s_modok, 1)
            for b in range(B):
                dv.wait_ge(s_v0, b + 1)
                dv.wait_ge(s_var, nth(0, b))
                V.tensor_tensor(vtok[:, b, :].rearrange("p (t n) -> p t n", t=TT),
                                ps[:, b, :].rearrange("p (t n) -> p t n", t=TT),
                                wt["l0_bv"].unsqueeze(1).to_broadcast([P, TT, P]), ALU.add).then_inc(s_vtok, 1)
            for b in range(B):
                dv.wait_ge(s_qe, b + 1)
                V.tensor_reduce(qsum[:, b, :], qe[:, b, :].rearrange(h8, d=DH), AX.X, ALU.add).then_inc(s_qstep, 1)
                dv.wait_ge(s_qstep, 2 * b + 5)
                V.reciprocal(qsum[:, b, :], qsum[:, b, :]).then_inc(s_qstep, 1)
                dv.wait_ge(s_qstep, 2 * b + 6)
                V.tensor_tensor(qp[:, b, :].rearrange(h8, d=DH), qe[:, b, :].rearrange(h8, d=DH),
                                qsum[:, b, :].unsqueeze(2).to_broadcast([P, TT * H, DH]), ALU.mult).then_inc(s_qp, 1)
            for b in range(B):
                dv.wait_ge(s_ke, b + 1)
                V.reciprocal(kmx[:, b, 0:1], kmx[:, b, 3:4]).then_inc(s_kstep, 1)
                dv.wait_ge(s_kstep, b + 5)
                dv.wait_ge(s_ctx, b + 1)
                V.scalar_tensor_tensor(out=ctxm[:, b, :], in0=ps[:, b, 0:P], scalar=kmx[:, b, 0:1], in1=blocks,
                                       op0=ALU.mult, op1=ALU.mult).then_inc(s_ctxm, 1)
            for b in range(B):
                dv.wait_ge(s_qTp, b + 1)
                V.tensor_copy(qT[:, b, :], ps[:, 4 + b, :]).then_inc(s_qT, 1)
            dv.wait_ge(s_modok, 6)
            norm(1)
            update(0, s_o0, 0)
            norm(2)
            update(1, s_m2, 0)
            norm(3)
            update(2, s_m2, 2)
            norm(4)
            attention(0)
            update(3, att[0]["proj"], 0)
            norm(5)
            update(4, s_m2, 4)
            norm(6)
            attention(1)
            update(5, att[1]["proj"], 0)
            norm(7)
            update(6, s_m2, 6)

        @block.scalar
        def _(act):
            A = nc.scalar.activation

            def log_exp_table():
                nc.scalar.preload_act_table_set("natural_log_exp_and_others")

            def norm(n):
                log_exp_table()
                for b in range(B):
                    act.wait_ge(s_xc, nth(n, b))
                    A(sq[:, b, :], xc[:, b, :], ACT.Square).then_inc(s_sq, 1)
                for b in range(B):
                    act.wait_ge(s_var, nth(n, b))
                    A(lnv[:, b, :], ps[:, 2 + b, :], ACT.Ln, bias=v1("eps", n)).then_inc(s_lnv, 1)
                    act.wait_ge(s_lnv, nth(n, b))
                    A(rstd[:, b, :], lnv[:, b, :], ACT.Exp, scale=-0.5).then_inc(s_rstd, 1)

            def mlp(m):
                _, nb, _, _, bias, func, _ = MLPS[m]
                base = mlp_base[m]
                for b in range(B):
                    for j in range(nb):
                        act.wait_ge(s_m1, base + b * nb + j + 1)
                        A(hid[:, j, b, :], ps[:, 4 + (b * nb + j) % 4, :], func,
                          bias=v1(bias, j) if bias else 0.0).then_inc(s_hid, 1)

            def attention(a):
                s = att[a]
                if a == 0:
                    for n in range(4):
                        b, t = n // 2, n % 2
                        act.wait_ge(s["qf"], n + 1)
                        A(qh[t][:, b, :], xn[:, b, :] if t == 0 else junk[b][:], ACT.Copy).then_inc(s["hi"], 1)
                        if t == 1:
                            act.wait_ge(s["v_mm"], b + 1)
                            act.wait_ge(s_ones, RING + 2)
                            for tile in range(TT):
                                A(vx[:, b * GB:(b + 1) * GB, tile, :, 0:DH],
                                  ps[:, b, tile * P:(tile + 1) * P].rearrange("p (g j d) -> p g j d", g=GB, j=HG),
                                  ACT.Copy).then_inc(s["v_ready"], 1)
                else:
                    act.wait_ge(s_ln, nth(6, B - 1))
                    A(qmul[:, 1:2], qmul[:, 0:1], ACT.Exp).then_inc(s["q_scale"], 1)
                    for b in range(B):
                        for t in range(2):
                            act.wait_ge(s["qkv"], 2 * b + t + 1)
                            A((xc, sq)[t][:, b, :], ps[:, 4 + 2 * b + t, :], ACT.Square,
                              bias=v1("l3_bq") if t == 0 else 0.0).then_inc(s["t1"], 1)
                        A(xn[:, b, :], ps[:, 4 + 2 * b, :], ACT.Identity, bias=v1("l3_bq")).then_inc(s["rot"], 1)
                        for t in range(2):
                            n = 2 * b + t
                            act.wait_ge(s["t2"], n + 1)
                            A((xc, sq)[t][:, b, :], (lnv, rstd)[t][:, b, :], ACT.Ln, scale=LN_SCALE).then_inc(s["ln"], 1)
                            act.wait_ge(s["ln"], n + 1)
                            A((lnv, rstd)[t][:, b, :], (xc, sq)[t][:, b, :], ACT.Exp, scale=-0.5).then_inc(s["nrm"], 1)
                        for t in range(2):
                            act.wait_ge(s["qf"], 2 * b + t + 1)
                            A(qh[t][:, b, :], (xn, qs)[t][:, b, :], ACT.Copy).then_inc(s["hi"], 1)

                def softmax(v):
                    s = att[v]
                    ring = 2 * BANKS if v == BOUNDED else BANKS

                    def m_row(i):
                        act.wait_ge(s["m_turned"], i + 1)
                        if i >= 2:
                            act.wait_ge(s[f"mrow_in{i % 2}"], 32 * (i // 2))
                        A(mrow[i % 2][:], ps[0:2 * HG, 7, :], ACT.Copy).then_inc(s["m_row"], 1)

                    def copy_o(i):
                        act.wait_ge(s["pv"], TT * (i + 1))
                        if i >= 2:
                            act.wait_ge(s["o_norm"], i - 1)
                        A(osb[i % 2][:], ps[:, out_bank(v, i), :], ACT.Copy).then_inc(s["o_copied"], 1)

                    if v != BOUNDED:
                        m_row(0)
                    if v == BOUNDED:
                        for t in range(TT):
                            act.wait_ge(s_bks, t + 1)
                            A(bk_sb[t], bk_sb[t], ACT.Exp).then_inc(s["bias_exp"], 1)
                        for n in range(NE // 2):
                            i, c = n // 8, n % 8
                            act.wait_ge(s["b_raw"], 2 * n + 2)
                            if 2 * n >= NPROB:
                                act.wait_ge(s["pv"], (2 * n - NPROB) // 4 + 1)
                            A(prob[n % (NPROB // 2)][:], ps[:, 2 * n % ring:2 * n % ring + 2, :],
                              ACT.Exp).then_inc(s["b_exp"], 2)
                            if c == 5 and i >= 1:
                                copy_o(i - 1)
                    else:
                        for e in range(NE):
                            i = e // 16
                            if v == 1:
                                act.wait_ge(s["b_score"], e + 1)
                            else:
                                act.wait_ge(s["b_raw"], e + 1)
                            if e >= NPROB:
                                act.wait_ge(s["pv"], (e - NPROB) // 4 + 1)
                            A(prob_of(e), ps[:, e % ring, :], ACT.Exp).then_inc(s["b_exp"], 1)
                            if e % 16 == 4 and i >= 1:
                                copy_o(i - 1)
                            if e % 16 == 12 and i + 1 < NG:
                                m_row(i + 1)
                    copy_o(NG - 1)

                if a == 0:
                    softmax(0)
                else:
                    by_bound(act, softmax)

            loaded(act, "cond")
            A(silc[:], wt["cond"], ACT.Silu).then_inc(s_silc, 1)
            norm(0)
            for b in range(B):
                act.wait_ge(s_kb, b + 1)
                A(ke[:, b, :], ps[:, 2 + b, :], ACT.Exp, bias=kmx[:, b, 2:3], accum_out=kmx[:, b, 3:4]).then_inc(s_ke, 1)
            for b in range(B):
                act.wait_ge(s_qd, b + 1)
                A(qe[:, b, :], qd[:, b, :], ACT.Exp).then_inc(s_qe, 1)
            for b in range(B):
                act.wait_ge(s_ktT, b + 1)
                A(ktok[:, b, :], ps[:, 6 + b, :], ACT.Copy).then_inc(s_ktok, 1)
            for b in range(B):
                act.wait_ge(s_y, b + 1)
                act.wait_ge(s_qd, b + 1)
                A(ysb[:, b, :], ps[:, 2 + b, :], ACT.Copy).then_inc(s_ysb, 1)
            norm(1)
            for b in range(B):
                act.wait_ge(s_ln, nth(1, b))
                A(silh[:, b, :], xm[:, b, :], ACT.Silu).then_inc(s_silh, 1)
            norm(2)
            mlp(0)
            norm(3)
            mlp(1)
            norm(4)
            attention(0)
            norm(5)
            mlp(2)
            norm(6)
            act.wait_ge(s_qmul, 1)
            attention(1)
            norm(7)
            mlp(3)

        @block.gpsimd
        def _(gp):
            G = nc.gpsimd
            for u in range(RING):
                G.memset(kg[u][:].bitcast(F32), 0.0).then_inc(s_ones, 1)
            G.memset(vx[:, :, :, :, DH:DH + 1], 1.0).then_inc(s_ones, 1)
            G.memset(vx[:, :, :, :, DH + 1:SP], 0.0).then_inc(s_ones, 1)
            gp.wait_ge(ld_w[0], 16)
            G.tensor_scalar(qmul[:, 0:1], v1("scale"), float(np.log(100.0)), None, ALU.min).then_inc(s_qmul, 1)

            def biased(k):
                for b in range(B):
                    x_ready(gp, k, b)
                    G.tensor_scalar(state_b[:, b, :], state[k % 2][:, b, :], gate_b[:, k, b:b + 1], None,
                                    ALU.add).then_inc(s_xb, 1)

            def attention(a):
                s = att[a]

                def softmax(v):
                    s = att[v]

                    if v == BOUNDED:
                        gp.wait_ge(s["bias_exp"], TT)
                        for n in range(NE // HG):
                            i, kt = n // TT, n % TT
                            gp.wait_ge(s["b_exp"], 4 * n + 4)
                            G.tensor_tensor(prob_of(4 * n + 3), prob_of(4 * n + 3), bk_sb[kt],
                                            ALU.mult).then_inc(s["gp_biased"], 1)
                if a == 1:
                    by_bound(gp, softmax)

            gp.wait_ge(s_modok, 6)
            biased(0)
            biased(1)
            biased(2)
            attention(0)
            biased(5)
            attention(1)
            biased(6)


def kernel(**inputs):
    import concourse.bacc as bacc
    from concourse.bass_utils import run_bass_kernel_spmd

    d = {k: np.asarray(v) for k, v in inputs.items()}
    f = np.float32

    def strips(w):
        o = np.zeros((GB, HG, SP, P), f)
        o[:, :, :DH] = w.reshape(GB, HG, DH, P)
        return o.reshape(GB, P, P).transpose(1, 0, 2).reshape(P, GB * P)

    def blocked(w):
        return w.reshape(-1, P, w.shape[1]).transpose(1, 0, 2).reshape(P, -1)

    inv = 1.0 / 10000.0 ** (np.arange(0, DH, 2, dtype=f) / f(DH))
    ang = np.outer(np.arange(T, dtype=f), inv.astype(f)).astype(f)
    ang = np.concatenate([ang, ang], -1).T
    cos, sin = np.cos(ang).astype(f), np.sin(ang).astype(f)
    sin[: DH // 2] *= -1
    cos, sin = np.tile(cos, (H, 1)), np.tile(sin, (H, 1))
    turn = np.concatenate([np.arange(1, DH, 2), np.arange(0, DH, 2)])
    turn = (np.arange(H)[:, None] * DH + turn[None]).ravel()
    root = f(DH ** -0.5)

    e0, e1 = d["L0_cond_emb_W"].reshape(P, 2, P), d["L1_cond_ada_w"].reshape(P, 6, P)
    e2, e3 = d["L2_cond_ada_W"].reshape(P, 6, P), d["L3_cond_ada_w"].T.reshape(P, 6, P)
    b0, b1 = d["L0_cond_emb_b"].reshape(2, P), d["L1_cond_ada_b"].reshape(6, P)
    b2, b3 = d["L2_cond_ada_b"].reshape(6, P), d["L3_cond_ada_b"].reshape(6, P)
    order = [(0, 0), (1, 1), (1, 4), (2, 1), (2, 4), (3, 2), (3, 3), (0, 1), (1, 0), (1, 3), (2, 0), (2, 3), (3, 4), (3, 5),
             (1, 2), (1, 5), (2, 2), (2, 5), (3, 0), (3, 1)]
    E, Bm = (e0, e1, e2, e3), (b0, b1, b2, b3)
    mod = np.stack([E[l][:, j] for l, j in order], 1)
    modb = np.stack([Bm[l][j] for l, j in order], 1)
    one, zero = np.ones(P, f), np.zeros(P, f)

    def twice(cols):
        return np.stack([c for c in cols for _ in range(B)], 1)

    vec = np.zeros((P, NVEC), f)

    def put(name, cols):
        cols = cols.reshape(P, -1)
        vec[:, VEC[name]:VEC[name] + cols.shape[1]] = cols

    put("modb", modb)
    put("g", twice([d["L0_cond_norm_g"], d["L0_cond_sn_g"], one, one, d["L2_cond_norm1_g"], d["L2_cond_norm2_g"], one, one]))
    put("b", twice([d["L0_cond_norm_b"], d["L0_cond_sn_b"], zero, zero, d["L2_cond_norm1_b"], d["L2_cond_norm2_b"], zero, zero]))
    put("outb", twice([d["L0_cond_out_b"], d["L1_cond_ssm_b2"], d["L1_cond_ff_b2"], zero, zero, d["L3_cond_proj_b"],
                       d["L3_cond_fc2_b"]]))
    put("eps", np.tile(np.array(LN_EPS, f), (P, 1)))
    put("bk", d["L0_cond_bk"])
    put("l1_a", d["L1_cond_ssm_b1"])
    put("l1_c", d["L1_cond_ff_b1"].reshape(2, P).T)
    put("l3_a", d["L3_cond_fc1_b"].reshape(4, P).T)
    put("l3_bq", d["L3_cond_q_bias"])
    put("scale", np.repeat(d["L3_cond_scale_mul"].reshape(H), DH))

    def wide(row):
        return np.tile(row[None], (P, 1))

    blk = np.kron(np.eye(H, dtype=f), np.ones((DH, DH), f))
    sel = np.zeros((P, HG), f)
    for j in range(HG):
        sel[SP * j + DH, j] = 1
    qkv = d["L3_cond_qkv_w"].T
    parts = {
        "ones": np.full((P, P), 1.0 / P, f), "cond": d["cond_1024"].T, "scales": wide(d["L3_cond_scale_mul"].reshape(H)), "vec": vec, "mod0": mod[:, 0:2].reshape(P, -1),
        "mod": mod[:, 2:].reshape(P, -1), "ident": np.eye(P, dtype=f), "blocks": blk, "sumsel": sel,
        "l0_q": d["L0_cond_Wq"], "l0_k": d["L0_cond_Wk"], "l0_v": d["L0_cond_Wv"], "l0_bq": wide(d["L0_cond_bq"]),
        "l0_bv": wide(d["L0_cond_bv"]), "l0_o": d["L0_cond_out_W"],
        "l1_a": d["L1_cond_ssm_w1"], "l1_b": d["L1_cond_ssm_w2"], "l1_c": d["L1_cond_ff_w1"], "l1_d": blocked(d["L1_cond_ff_w2"]),
        "cos": cos, "sin": sin, "qcos": cos * root, "qsin": sin * root,
        "l2_q": d["L2_cond_Wq"], "l2_qr": d["L2_cond_Wq"][:, turn], "l2_k": d["L2_cond_Wk"], "l2_kr": d["L2_cond_Wk"][:, turn],
        "l2_v": d["L2_cond_Wv"], "l2_o": strips(d["L2_cond_Wo"]), "l2_a": d["L2_cond_W1"], "l2_b": blocked(d["L2_cond_W2"]),
        "l3_q": qkv[:, :P], "l3_k": qkv[:, P:2 * P], "l3_v": qkv[:, 2 * P:], "l3_bv": wide(d["L3_cond_v_bias"]),
        "l3_o": strips(d["L3_cond_proj_w"].T), "l3_a": d["L3_cond_fc1_w"].T, "l3_b": blocked(d["L3_cond_fc2_w"].T),
    }
    arrays = {"xT": np.ascontiguousarray(d["x"].transpose(2, 0, 1))}
    for n, cols in enumerate(W_LOADS):
        arrays[f"weights{n}_in"] = np.ascontiguousarray(np.concatenate([parts[name] for name, _ in cols], 1))
    bias = d["fside_1x1xSxS_0"][0, 0]
    arrays["bias_by_query"] = np.ascontiguousarray(bias.reshape(TT, P, T).transpose(1, 0, 2))
    arrays["bias_by_key"] = np.ascontiguousarray(bias.T.reshape(TT, P, T).transpose(1, 0, 2))

    arrays["rows_q"] = np.zeros((NG * HG, SP - SPLIT, T), f)
    arrays["rows_k"] = np.ones((NG * HG, SHIFT - SPLIT, T), f)

    nc = bacc.Bacc("TRN2", target_bir_lowering=False, num_devices=1)
    ap = {n: nc.dram_tensor(n, a.shape, F32, kind="ExternalInput").ap() for n, a in arrays.items()}
    out = nc.dram_tensor("outT", [P, B, T], F32, kind="ExternalOutput").ap()
    build(nc, ap["xT"], [ap[f"weights{n}_in"] for n in range(len(W_LOADS))], ap["bias_by_query"], ap["bias_by_key"], ap["rows_q"],
          ap["rows_k"], out)
    r = run_bass_kernel_spmd(nc, [arrays], core_ids=[0])
    return np.ascontiguousarray(r.results[0]["outT"].transpose(1, 2, 0))
```

```python
from contextlib import ExitStack

import numpy as np

import concourse.bass as bass
from concourse import mybir

ALU = mybir.AluOpType
ACT = mybir.ActivationFunctionType
AX = mybir.AxisListType
F32 = mybir.dt.float32
F32R = mybir.dt.float32r

P = 128
B, T, H, DH = 2, 512, 16, 8
TT = T // P
HG = 4
NG = B * H // HG
NE = NG * HG * TT
GB = H // HG
SP = 32
ROLES = 4
SHIFT_ROLE = 3
RING = 3
LN_SCALE, ROOT_LN_SCALE = 2.0 ** 16, 2.0 ** 8
WARM = (8, 5)
NPROB = 16
BOUND, BIAS_RANGE = 60.0, 80.0
BANKS = 3
LAG = 26

LN_EPS = [1e-5, 1e-5, 1e-6, 1e-6, 1e-5, 1e-5, 1e-6, 1e-6]
NLN = len(LN_EPS)
LN_STATE = [0, None, 1, 2, 3, 4, 5, 6]
SHIFTED = (0, 4, 6)
NMOD = 20
NUP = 7
NO_BIAS = (3, 4)

W_LOADS = [
    [("ones", 128), ("center", 128), ("cond", 2), ("scales", 16), ("vec", 100)],
    [("mod0", 256), ("ident", 128), ("blocks", 128), ("l0_q", 128),
     ("l0_k", 128), ("l0_v", 128), ("l0_bq", 128), ("l0_bv", 128), ("l0_o", 128)],
    [("mod", 18 * 128), ("l1_a", 128), ("l1_b", 128), ("l1_c", 256), ("l1_d", 256)],
    [("cos", 512), ("sin", 512), ("qcos", 512), ("qsin", 512), ("l2_q", 128), ("l2_qr", 128), ("l2_k", 128),
     ("l2_kr", 128), ("l2_v", 128), ("l2_o", 512), ("sumsel", HG), ("sumwide", 128), ("l2_a", 512), ("l2_b", 512)],
    [("l3_q", 128), ("l3_k", 128), ("l3_v", 128), ("l3_bv", 128), ("l3_o", 512), ("l3_a", 512), ("l3_b", 512)],
]
NHID = 11
VEC = {}
_at = 0
for _name, _n in [("modb", NMOD), ("g", 2 * NLN), ("b", 2 * NLN), ("outb", 2 * NUP), ("eps", NLN), ("bk", 1),
                  ("hidden", NHID), ("l3_bq", 1), ("scale", 1)]:
    VEC[_name] = _at
    _at += _n
NVEC = 100

MLPS = [
    (2, 1, "l1_a", "l1_b", 0, ACT.Gelu, 1),
    (3, 2, "l1_c", "l1_d", 1, ACT.Gelu_apprx_tanh, 2),
    (5, 4, "l2_a", "l2_b", 3, ACT.Gelu, 4),
    (7, 4, "l3_a", "l3_b", 7, ACT.Gelu_apprx_tanh, 6),
]

MLPS_BLOCKS = {m[2]: m[1] for m in MLPS}


def build(nc, xT, loads, bias_q, bias_k, rows_q, rows_k, out):
    ctx = ExitStack()
    with ctx:
        def sb(name, shape, dt=F32):
            return ctx.enter_context(nc.sbuf_tensor(name, shape, dt))

        def sem(name):
            return ctx.enter_context(nc.semaphore(name))

        wt, load_of = {}, {}
        tiles = []
        for n, cols in enumerate(W_LOADS):
            tile = sb(f"weights{n}", [P, sum(c for _, c in cols)])
            tiles.append(tile)
            at = 0
            for name, c in cols:
                wt[name] = tile[:, at:at + c]
                load_of[name] = n
                at += c
        vec = wt["vec"]
        ones, center_w, ident, blocks, sumsel = wt["ones"], wt["center"], wt["ident"], wt["blocks"], wt["sumsel"]
        state = [sb(f"state{k}", [P, B, T]) for k in range(2)]
        state_b = sb("state_b", [P, B, T])
        xc = sb("xc", [P, B, T])
        sq = sb("sq", [P, B, T])
        lnv = sb("lnv", [P, B, T])
        rstd = sb("rstd", [P, B, T])
        xn = sb("xn", [P, B, T])
        xm = sb("xm", [P, B, T])
        hid = sb("hid", [P, 4, B, T])
        silc = sb("silc", [P, 2])
        mods = sb("mods", [P, NMOD, B])
        scale1 = sb("scale1", [P, NLN - 1, B])
        ln_a = sb("ln_a", [P, NLN, B])
        ln_t = sb("ln_t", [P, NLN - 1, B])
        ln_b = sb("ln_b", [P, NLN, B])
        hid_b = sb("hid_b", [P, NHID, B])
        gate = sb("gate", [P, NUP, B])
        gate_b = sb("gate_b", [P, NUP, B])
        qs = sb("qs", [P, B, T])
        qd = hid[:, 0]
        qe = hid[:, 1]
        qp = hid[:, 2]
        qmx = sb("qmx", [P, B, TT * H])
        qsum = sb("qsum", [P, B, TT * H])
        kmx = sb("kmx", [P, B, 4])
        ke = hid[:, 3]
        ktok = lnv
        vtok = sq
        qT = rstd
        ysb = qs
        silh = xc
        qh = [hid[:, t].bitcast(F32R) for t in range(2)]
        ql = [hid[:, 2 + t].bitcast(F32R) for t in range(2)]
        vx = sb("vx", [P, NG, TT, HG, SP])
        qg = [sb(f"qg{u}", [P, T], F32R) for u in range(RING)]
        kg = [sb(f"kg{u}", [P, HG, T], F32R) for u in range(RING)]
        diag = sb("diag", [P, T])
        mx = [sb(f"mx{u}", [P, TT * HG]) for u in range(2)]
        nmx = [sb(f"nmx{u}", [P, TT, 2, HG], F32R) for u in range(2)]
        mrow = [sb(f"mrow{u}", [HG * 2, T], F32R) for u in range(2)]
        prob = [sb(f"prob{n}", [P, 2, T]) for n in range(NPROB // 2)]
        osb = [sb(f"osb{u}", [P, T]) for u in range(2)]
        inv = [sb(f"inv{u}", [P, TT * HG]) for u in range(2)]
        onorm = hid[:, :, :, :].rearrange("p a b t -> p (a b) t")
        junk = [sb(f"junk{n}", [P, T]) for n in range(2)]
        ctxm = junk[0][:, 0:B * P].rearrange("p (b n) -> p b n", b=B)
        bq_sb = wt["mod"][:, 0:TT * T].rearrange("p (q n) -> p q n", q=TT)
        bk_all = sb("bias_k", [P, TT, T])
        bk_sb = [bk_all[:, t, :] for t in range(TT)]
        qmul = sb("qmul", [P, 3])
        warm = sb("warm", [P, T], mybir.dt.bfloat16)
        flag = sb("flag", [1, 1], mybir.dt.int32)
        smax = sb("smax", [1, 3])
        bmax = sb("bmax", [P, TT])
        bmin = sb("bmin", [P, TT])
        brange = sb("brange", [P, TT])
        over = sb("over", [P, 1])
        over_all = sb("over_all", [P, 1])
        scratch = {(a, t): nc.dram_tensor(f"split_{t}{a}", [NG * HG * DH, ROLES, T], F32).ap()
                   for a in range(2) for t in "qk"}

        ps = ctx.enter_context(nc.psum_tensor("ps", [P, 8, T], F32))

        ld_x = [sem(f"ld_x{b}") for b in range(B)]
        ld_w = [sem(f"ld_w{n}") for n in range(len(W_LOADS))]
        ld_bq, ld_bk = sem("ld_bias_q"), sem("ld_bias_k")
        s_silc, s_modmm, s_mod, s_modok = sem("silu_cond"), sem("mod_products"), sem("mod_steps"), sem("mods_ready")
        s_x, s_xb = sem("x_ready"), sem("x_plus_bias")
        s_xc, s_sq, s_var, s_lnv, s_rstd, s_xnn, s_ln = (
            sem(n) for n in ("ln_centered", "ln_square", "ln_var", "ln_log", "ln_rstd", "ln_scaled", "ln_out"))
        s_hbmm, s_hb = sem("hidden_bias_products"), sem("hidden_bias")
        s_m1, s_hid, s_m2 = sem("mlp_first"), sem("mlp_hidden"), sem("mlp_second")
        s_q0, s_k0, s_v0 = sem("l0_q"), sem("l0_k"), sem("l0_v")
        s_qstep, s_qd, s_qe, s_qp = sem("l0_q_steps"), sem("l0_q_shifted"), sem("l0_q_exp"), sem("l0_q_probs")
        s_kstep, s_kb, s_ke = sem("l0_k_steps"), sem("l0_k_shift"), sem("l0_k_exp")
        s_vtok, s_ktT, s_ktok, s_ctx, s_ctxm, s_qTp, s_qT, s_y, s_ysb, s_silh, s_o0 = (
            sem(n) for n in ("l0_v_ready", "l0_k_turned", "l0_k_tokens", "l0_ctx", "l0_ctx_ready", "l0_q_turned",
                             "l0_q_features", "l0_y", "l0_y_ready", "l0_silu", "l0_out"))
        s_rows = sem("rows_written")
        s_warm = sem("warm_zeros")
        s_ones, s_qmul = sem("ones_rows"), sem("scale_clipped")
        att = []
        for a in range(3):
            att.append({n: sem(f"{n}{a}") for n in (
                "stage0", "stage1", "stage2", "b_raw", "b_exp", "pv", "o_copied", "o_spread",
                "o_norm") + (("bias_exp", "dv_biased", "gp_biased", "o_sum", "o_inv", "o_wide") if a == 2 else
                             ("mrow_in0", "mrow_in1", "a_score", "a_max", "nm_hi", "nm_lo", "m_turned", "m_row", "o_log", "o_rec"))})
            if a == 1:
                att[a]["b_score"] = sem("b_score1")
            if a < 2:
                att[a] |= {n: sem(f"{n}{a}") for n in (
                    "qkv", "rot", "qsum", "hi", "lo", "split_w0", "split_w1", "split_w2", "v_mm", "v_ready", "proj", "t1", "t2", "qf",
                    "nrm", "q_scale", "ln")}
        BOUNDED = 2
        s_flag0, s_over, s_flag, s_bmax, s_bshift, s_bdiag, s_bspread, s_bks = (
            sem(n) for n in ("flag_steps", "over_bounds_summed", "flag", "bias_max", "bias_shifted", "bias_diag",
                             "bias_shift_spread", "bias_k_shifted"))
        s_out = sem("out_written")

        def w(name, a=0, n=P):
            return wt[name][:, a:a + n]

        def prob_of(e):
            return prob[e % NPROB // 2][:, e % 2, :]

        def out_bank(v, i):
            return 6 + i % 2 if v == BOUNDED else 6

        def turn_bank(v, i):
            return 6 + i % 2 if v == BOUNDED else 7

        def v1(name, k=0):
            return vec[:, VEC[name] + k:VEC[name] + k + 1]

        def x_ready(eng, k, b):
            if k == 0:
                eng.wait_ge(ld_x[b], 16)
            else:
                eng.wait_ge(s_x, 2 * (k - 1) + b + 1)

        def loaded(eng, name):
            eng.wait_ge(ld_w[load_of[name]], 16)

        def nth(n, b):
            return 2 * n + b + 1

        def by_bound(eng, program):
            eng.wait_ge(s_flag, 1)
            unbounded = eng.value_load(flag[0:1, 0:1], min_val=0, max_val=1)
            with eng.If(unbounded == 0):
                program(BOUNDED)
            with eng.Else():
                program(1)

        mlp_base, at = [], 0
        for m in MLPS:
            mlp_base.append(at)
            at += 2 * m[1]

        block = ctx.enter_context(nc.Block())

        @block.sync
        def _(sp):
            sp.dma_start(state[0][:, 0, :], xT[:, 0, :]).then_inc(ld_x[0], 16)
            sp.dma_start(tiles[0][:], loads[0]).then_inc(ld_w[0], 16)
            sp.dma_start(state[0][:, 1, :], xT[:, 1, :]).then_inc(ld_x[1], 16)
            for n in range(1, len(W_LOADS)):
                sp.dma_start(tiles[n][:], loads[n]).then_inc(ld_w[n], 16)
            sp.dma_start(bk_all[:], bias_k).then_inc(ld_bk, 16)
            sp.wait_ge(s_modmm, 1)
            sp.dma_start(bq_sb, bias_q).then_inc(ld_bq, 16)
            for a in range(2):
                for t, rows in (("q", rows_q), ("k", rows_k)):
                    sp.dma_start(scratch[a, t][:, SHIFT_ROLE, :], rows).then_inc(s_rows, 16)
            for a in range(2):
                s = att[a]

                def send(piece):
                    b, rows = ((0, slice(0, SP)), (0, slice(SP, P)), (1, slice(0, P)))[piece]
                    count = rows.stop - rows.start
                    done = att[a][f"split_w{piece}"]
                    for t in range(2):
                        dst = scratch[a, "qk"[t]][b * P + rows.start:b * P + rows.stop]
                        sp.wait_ge(att[a]["hi"], 2 * b + t + 1)
                        sp.dma_start((dst[:, 0:2, :], dst[:, 0:3:2, :])[t],
                                     qh[t][rows, b, :].bitcast(F32).unsqueeze(1).to_broadcast([count, 2, T])
                                     ).then_inc(done, 16)
                        sp.wait_ge(att[a]["lo"], 2 * b + t + 1)
                        sp.dma_start(dst[:, 2 - t, :], ql[t][rows, b, :].bitcast(F32)).then_inc(done, 16)

                def groups(v):
                    s = att[v]

                    def stage(i):
                        if i >= RING:
                            sp.wait_ge(s["b_raw"], 16 * (i - RING + 1))
                        if i in (0, 1, GB):
                            sp.wait_ge(att[a][f"split_w{(0, 1, GB).index(i)}"], 16 * 4)
                        done = s[f"stage{i % RING}"]
                        sp.dma_start(qg[i % RING][:].bitcast(F32),
                                     scratch[a, "q"][i * SP:(i + 1) * SP].rearrange("d r n -> (d r) n")).then_inc(done, 16)
                        for j in range(HG):
                            rows = slice(SP * j, SP * (j + 1))
                            head = slice((i * HG + j) * DH, (i * HG + j + 1) * DH)
                            sp.dma_start(kg[i % RING][rows, j, :].bitcast(F32),
                                         scratch[a, "k"][head].rearrange("d r n -> (d r) n")).then_inc(done, 16)

                    def stage_m(i):
                        sp.wait_ge(s["m_row"], i + 1)
                        for t in range(2):
                            sp.dma_start(qg[i % RING][SHIFT_ROLE + ROLES * t::SP, :].bitcast(F32),
                                         mrow[i % 2][t * HG:(t + 1) * HG, :].bitcast(F32)).then_inc(s[f"mrow_in{i % 2}"], 16)

                    stage(0)
                    send(1)
                    stage(1)
                    send(2)
                    if v != BOUNDED:
                        stage_m(0)
                    for i in range(NG):
                        if i + 2 < NG:
                            stage(i + 2)
                        if v != BOUNDED and i + 1 < NG:
                            stage_m(i + 1)

                send(0)
                sp.wait_ge(s_rows, 64)
                if a == 0:
                    sp.wait_ge(s_ones, RING)
                    groups(0)
                else:
                    by_bound(sp, groups)
            for b in range(B):
                x_ready(sp, NUP, b)
                sp.dma_start(out[:, b, :], state[NUP % 2][:, b, :]).then_inc(s_out, 16)
            sp.wait_ge(s_out, 16 * B)

        @block.tensor
        def _(pe):
            mm = nc.tensor.matmul

            def keep_warm(count, bank):
                for _ in range(count):
                    mm(ps[:, bank, :], warm[:, 0:P], warm[:], start=True, stop=True)

            def center(n, b):
                if LN_STATE[n] is None:
                    pe.wait_ge(s_ysb, b + 1)
                    src = ysb
                else:
                    x_ready(pe, LN_STATE[n], b)
                    src = state[LN_STATE[n] % 2]
                mm(ps[:, b, :], center_w, src[:, b, :], start=True, stop=True).then_inc(s_xc, 1)

            def variance(n, b):
                pe.wait_ge(s_sq, nth(n, b))
                mm(ps[:, 2 + b, :], ones, sq[:, b, :], start=True, stop=True).then_inc(s_var, 1)

            def norm(n):
                for b in range(B):
                    center(n, b)
                for b in range(B):
                    variance(n, b)

            def mlp_first(m, b, j):
                n, nb, w1 = MLPS[m][0:3]
                c = b * nb + j
                if j == 0:
                    pe.wait_ge(s_ln, nth(n, b))
                if c >= 4:
                    pe.wait_ge(s_hid, mlp_base[m] + c - 3)
                mm(ps[:, 4 + c % 4, :], w(w1, j * P), xm[:, b, :], start=True, stop=True).then_inc(s_m1, 1)

            def mlp_second(m):
                _, nb, _, w2, _, _, _ = MLPS[m]

                def term(b, j):
                    pe.wait_ge(s_hid, mlp_base[m] + b * nb + j + 1)
                    return mm(ps[:, b, :], w(w2, j * P), hid[:, j, b, :], start=(j == 0), stop=(j == nb - 1))

                return term

            def branch_and_norm(terms, term, done, n, following=None):
                for j in range(terms):
                    last = term(0, j)
                last.then_inc(done, 1)
                for j in range(terms):
                    if j == 1 and n is not None:
                        center(n, 0)
                    if j == 2 and n is not None:
                        variance(n, 0)
                    last = term(1, j)
                last.then_inc(done, 1)
                if n is None:
                    return
                if terms == 1:
                    center(n, 0)
                if terms == 2:
                    variance(n, 0)
                center(n, 1)
                if terms == 1:
                    variance(n, 0)
                if following is not None:
                    mlp_first(following, 0, 0)
                variance(n, 1)

            def mlp(m, n, begun=0, following=None):
                nb = MLPS[m][1]
                for c in range(begun, 2 * nb):
                    mlp_first(m, c // nb, c % nb)
                branch_and_norm(nb, mlp_second(m), s_m2, n, following)

            def attention(a):
                s = att[a]

                def softmax(v):
                    s = att[v]
                    ring = 2 * BANKS if v == BOUNDED else BANKS

                    def a_block(n):
                        i, qt, j = n // 16, n % 16 // 4, n % 4
                        if n % 16 == 0:
                            pe.wait_ge(s[f"stage{i % RING}"], (1 + HG) * 16 * (i // RING + 1))
                        if n >= BANKS:
                            pe.wait_ge(s["a_max"], n - BANKS + 1)
                        mm(ps[:, BANKS + n % BANKS, :], qg[i % RING][:, qt * P:(qt + 1) * P], kg[i % RING][:, j, :],
                           start=True, stop=True).then_inc(s["a_score"], 1)

                    def turn_max(i):
                        pe.wait_ge(s["nm_lo"], i + 1)
                        if i >= 1:
                            pe.wait_ge(s["m_row"], i)
                        if i >= 3:
                            pe.wait_ge(s["o_log"], i - 2)
                        for qt in range(TT):
                            last = nc.tensor.transpose(ps[0:2 * HG, 7, qt * P:(qt + 1) * P],
                                                       nmx[i % 2][:, qt, :, :].rearrange("p t j -> p (t j)").bitcast(F32),
                                                       ident)
                        last.then_inc(s["m_turned"], 1)

                    def score(e):
                        i, kt, j = e // 16, e % 16 // 4, e % 4
                        if e % 16 == 0:
                            if v == BOUNDED:
                                pe.wait_ge(s[f"stage{i % RING}"], (1 + HG) * 16 * (i // RING + 1))
                            else:
                                pe.wait_ge(s[f"mrow_in{i % 2}"], 32 * (i // 2 + 1))
                        if e >= ring:
                            pe.wait_ge(s["b_exp"], e - ring + 1)
                        mm(ps[:, e % ring, :], kg[i % RING][:, j, kt * P:(kt + 1) * P], qg[i % RING][:],
                           start=True, stop=True).then_inc(s["b_raw"], 1)

                    def values(n):
                        i, kt = n // TT, n % TT
                        if v == BOUNDED:
                            pe.wait_ge(s["dv_biased"], 3 * (n + 1))
                            pe.wait_ge(s["gp_biased"], n + 1)
                        else:
                            pe.wait_ge(s["b_exp"], 4 * n + 4)
                        if kt == 0:
                            pe.wait_ge(att[a]["v_ready"], TT * (1 + i // GB))
                            if v == BOUNDED and i >= 2:
                                pe.wait_ge(s["o_norm"], i - 1)
                            if v != BOUNDED and i >= 1:
                                pe.wait_ge(s["o_copied"], i)
                        for j in range(HG):
                            last = mm(ps[SP * j:SP * (j + 1), out_bank(v, i), :], vx[:, i, kt, j, :], prob_of(4 * n + j),
                                      start=(kt == 0), stop=(kt == TT - 1))
                        last.then_inc(s["pv"], 1)

                    def turn_sums(i):
                        pe.wait_ge(s["o_copied"], i + 1)
                        for qt in range(TT):
                            last = mm(ps[:, turn_bank(v, i), qt * HG:(qt + 1) * HG], osb[i % 2][:, qt * P:(qt + 1) * P], sumsel,
                                      start=True, stop=True)
                        last.then_inc(s["o_sum"], 1)

                    def spread_sums(i):
                        pe.wait_ge(s["o_copied"], i + 1)
                        if i >= 1:
                            pe.wait_ge(s["o_log"], i)
                        pe.wait_ge(s["m_row"], min(i + 3, NG))
                        mm(ps[:, 7, :], wt["sumwide"], osb[i % 2][:], start=True, stop=True).then_inc(s["o_spread"], 1)

                    def spread(i):
                        pe.wait_ge(s["o_wide"], i + 1)
                        for qt in range(TT):
                            last = mm(ps[:, turn_bank(v, i), qt * P:(qt + 1) * P], diag[:, qt * P:(qt + 1) * P], ident,
                                      start=True, stop=True)
                        last.then_inc(s["o_spread"], 1)

                    pe.wait_ge(att[a]["rot"], (8, 2)[a])
                    pe.wait_ge(att[a]["qf"], 4)
                    pe.wait_ge(att[a]["v_ready"], B * TT)
                    if v != BOUNDED:
                        for n in range(LAG):
                            if n == 20:
                                turn_max(0)
                            a_block(n)
                    back = 13 if v == BOUNDED else ring + 3
                    for e in range(NE + back - 2):
                        i = e // 16
                        if e < NE:
                            score(e)
                        if v != BOUNDED and e + LAG < NE:
                            a_block(e + LAG)
                        if e >= back and (e - back) % 4 == 0:
                            values((e - back) // 4)
                        if v != BOUNDED and e % 16 == 9 and i + 1 < NG:
                            turn_max(i + 1)
                        if v == 0 and e == NE - 8:
                            pe.wait_ge(s_bdiag, TT)
                            mm(ps[:, BANKS, :], ones, diag[:], start=True, stop=True).then_inc(s_bspread, 1)
                            pe.wait_ge(s_flag0, 3)
                            mm(ps[:, BANKS + 1, 0:1], ones, over_all[:], start=True, stop=True).then_inc(s_over, 1)
                        if v != BOUNDED and e % 16 == 13 and 1 <= i < NG:
                            spread_sums(i - 1)
                        if v == BOUNDED and e % 16 == 3 and 2 <= i:
                            turn_sums(i - 2)
                        if v == BOUNDED and e % 16 == 7 and 2 <= i:
                            spread(i - 2)
                    if v == BOUNDED:
                        turn_sums(NG - 1)
                        spread(NG - 1)
                    else:
                        spread_sums(NG - 1)
                    def project(b, g):
                        pe.wait_ge(s["o_norm"], b * GB + g + 1)
                        return mm(ps[:, b, :], w(("l2_o", "l3_o")[a], g * P), onorm[:, b * GB + g, :],
                                  start=(g == 0), stop=(g == GB - 1))

                    branch_and_norm(GB, project, att[a]["proj"], (5, 7)[a], following=(2, 3)[a])

                if a == 0:
                    for b in range(B):
                        pe.wait_ge(s_ln, nth(4, b))
                        if b == 0:
                            loaded(pe, "l2_q")
                        for n, name in enumerate(("l2_q", "l2_qr", "l2_k", "l2_kr")):
                            if b:
                                pe.wait_ge(s["rot"], n + 1)
                            mm(ps[:, 4 + n, :], w(name), xm[:, b, :], start=True, stop=True).then_inc(s["qkv"], 1)
                        for t in range(TT):
                            last = mm(ps[:, b, t * P:(t + 1) * P], xm[:, b, t * P:(t + 1) * P], w("l2_v"),
                                      start=True, stop=True)
                        last.then_inc(s["v_mm"], 1)
                else:
                    for b in range(B):
                        pe.wait_ge(s_ln, nth(6, b))
                        for n, name in enumerate(("l3_q", "l3_k")):
                            mm(ps[:, 4 + 2 * b + n, :], w(name), xm[:, b, :], start=True, stop=True).then_inc(s["qkv"], 1)
                        for t in range(TT):
                            last = mm(ps[:, b, t * P:(t + 1) * P], xm[:, b, t * P:(t + 1) * P], w("l3_v"),
                                      start=True, stop=True)
                        last.then_inc(s["v_mm"], 1)
                        for n in range(2 * b, 2 * b + 2):
                            pe.wait_ge(s["t1"], n + 1)
                            if n >= 2:
                                pe.wait_ge(s["t2"], n - 1)
                            mm(ps[:, 2 + n % 2, :], blocks, (xc, sq)[n % 2][:, n // 2, :],
                               start=True, stop=True).then_inc(s["qsum"], 1)

                if a == 0:
                    softmax(0)
                else:
                    by_bound(pe, softmax)

            pe.wait_ge(s_warm, 1)
            keep_warm(WARM[0], 7)
            loaded(pe, "ones")
            pe.wait_ge(s_silc, 1)
            norm(0)
            loaded(pe, "l0_q")
            for b in range(B):
                pe.wait_ge(s_ln, nth(0, b))
                for t in range(TT):
                    last = mm(ps[:, 4 + b, t * P:(t + 1) * P], xm[:, b, t * P:(t + 1) * P], w("l0_q"), start=True, stop=True)
                last.then_inc(s_q0, 1)
                for t in range(TT):
                    last = mm(ps[:, b, t * P:(t + 1) * P], xm[:, b, t * P:(t + 1) * P], w("l0_v"), start=True, stop=True)
                last.then_inc(s_v0, 1)
                mm(ps[:, 2 + b, :], w("l0_k"), xm[:, b, :], start=True, stop=True).then_inc(s_k0, 1)
            for j in range(NMOD):
                if j == 2:
                    loaded(pe, "mod")
                wj = w("mod0", j * P) if j < 2 else w("mod", (j - 2) * P)
                last = mm(ps[:, 7, 2 * j:2 * j + 2], wj, silc[:], start=True, stop=True)
            last.then_inc(s_modmm, 1)
            pe.wait_ge(s_mod, 1)
            for b in range(B):
                pe.wait_ge(s_ke, b + 1)
                for t in range(TT):
                    last = nc.tensor.transpose(ps[:, 6 + b, t * P:(t + 1) * P], ke[:, b, t * P:(t + 1) * P], ident)
                last.then_inc(s_ktT, 1)
            for b in range(B):
                pe.wait_ge(s_ktok, b + 1)
                pe.wait_ge(s_vtok, b + 1)
                for t in range(TT):
                    last = mm(ps[:, b, 0:P], ktok[:, b, t * P:(t + 1) * P], vtok[:, b, t * P:(t + 1) * P],
                              start=(t == 0), stop=(t == TT - 1))
                last.then_inc(s_ctx, 1)
            for b in range(B):
                pe.wait_ge(s_qp, b + 1)
                for t in range(TT):
                    last = nc.tensor.transpose(ps[:, 4 + b, t * P:(t + 1) * P], qp[:, b, t * P:(t + 1) * P], ident)
                last.then_inc(s_qTp, 1)
            for b in range(B):
                pe.wait_ge(s_qT, b + 1)
                pe.wait_ge(s_ctxm, b + 1)
                mm(ps[:, 2 + b, :], ctxm[:, b, :], qT[:, b, :], start=True, stop=True).then_inc(s_y, 1)
            norm(1)
            pe.wait_ge(s_modok, 6)
            for n, _, w1, _, first, _, _ in MLPS:
                loaded(pe, w1)
                for j in range(MLPS_BLOCKS[w1]):
                    c = first + j
                    last = mm(ps[:, 7, 2 * c:2 * c + 2], w(w1, j * P), ln_b[:, n, :], start=True, stop=True)
            last.then_inc(s_hbmm, 1)

            def l0_out(b, _):
                pe.wait_ge(s_silh, b + 1)
                return mm(ps[:, b, :], w("l0_o"), silh[:, b, :], start=True, stop=True)

            keep_warm(WARM[1], 6)
            branch_and_norm(1, l0_out, s_o0, 2)
            mlp(0, 3)
            mlp(1, 4)
            attention(0)
            mlp(2, 6, begun=1)
            loaded(pe, "l3_q")
            attention(1)
            mlp(3, None, begun=1)

        @block.vector
        def _(dv):
            V = nc.vector
            V.memset(warm[:], 0.0).then_inc(s_warm, 1)

            def norm(n, b):
                dv.wait_ge(s_rstd, nth(n, b))
                dv.wait_ge(s_xc, nth(n, b))
                if n in SHIFTED:
                    V.scalar_tensor_tensor(out=xn[:, b, :], in0=ps[:, b, :], scalar=ln_a[:, n, b:b + 1],
                                           in1=rstd[:, b, :], op0=ALU.mult, op1=ALU.mult).then_inc(s_xnn, 1)
                    dv.wait_ge(s_xnn, nth(SHIFTED.index(n), b))
                    V.tensor_scalar(xm[:, b, :], xn[:, b, :], ln_b[:, n, b:b + 1], None, ALU.add).then_inc(s_ln, 1)
                else:
                    V.scalar_tensor_tensor(out=xm[:, b, :], in0=ps[:, b, :], scalar=ln_a[:, n, b:b + 1],
                                           in1=rstd[:, b, :], op0=ALU.mult, op1=ALU.mult).then_inc(s_ln, 1)

            def update(k, b, ready, base):
                dv.wait_ge(ready, base + b + 1)
                if k in NO_BIAS:
                    x_ready(dv, k, b)
                    src = state[k % 2]
                else:
                    dv.wait_ge(s_xb, [0, 1, 2, None, None, 3, 4][k] * 2 + b + 1)
                    src = state_b
                V.scalar_tensor_tensor(out=state[(k + 1) % 2][:, b, :], in0=ps[:, b, :], scalar=gate[:, k, b:b + 1],
                                       in1=src[:, b, :], op0=ALU.mult, op1=ALU.add).then_inc(s_x, 1)

            def update_and_norm(k, ready, base, n):
                for b in range(B):
                    update(k, b, ready, base)
                for b in range(B):
                    if n is not None:
                        norm(n, b)

            def split_pair(s, b, t, src, ready, count):
                dv.wait_ge(ready, count)
                dv.wait_ge(s["hi"], 2 * b + t + 1)
                V.tensor_tensor(ql[t][:, b, :], src, qh[t][:, b, :].bitcast(F32), ALU.subtract).then_inc(s["lo"], 1)

            def attention(a):
                s = att[a]
                if a == 0:
                    for b in range(B):
                        for t in range(2):
                            dst = xn[:, b, :] if t == 0 else junk[b][:]
                            for n in range(2 * t, 2 * t + 2):
                                name, turned = (("qcos", xc), ("qsin", sq), ("cos", lnv), ("sin", rstd))[n]
                                dv.wait_ge(s["qkv"], 4 * b + n + 1)
                                V.tensor_tensor(turned[:, b, :], ps[:, 4 + n, :], wt[name], ALU.mult).then_inc(s["rot"], 1)
                            dv.wait_ge(s["rot"], 4 * b + 2 * t + 2)
                            x1, x2 = ((xc, sq), (lnv, rstd))[t]
                            V.tensor_tensor(dst, x1[:, b, :], x2[:, b, :], ALU.add).then_inc(s["qf"], 1)
                        for t in range(2):
                            split_pair(s, b, t, xn[:, b, :] if t == 0 else junk[b][:], s["qf"], 2 * b + t + 1)
                else:
                    def values(b):
                        dv.wait_ge(s["v_mm"], b + 1)
                        if b == 0:
                            dv.wait_ge(att[0]["pv"], NE // HG)
                        for t in range(TT):
                            V.tensor_tensor(vx[:, b * GB:(b + 1) * GB, t, :, 0:DH],
                                            ps[:, b, t * P:(t + 1) * P].rearrange("p (g j d) -> p g j d", g=GB, j=HG),
                                            wt["l3_bv"].rearrange("p (g j d) -> p g j d", g=GB, j=HG),
                                            ALU.add).then_inc(s["v_ready"], 1)

                    for b in range(B):
                        for t in range(2):
                            dv.wait_ge(s["qsum"], 2 * b + t + 1)
                            V.tensor_scalar((lnv, rstd)[t][:, b, :], ps[:, 2 + t, :], 1e-24, None,
                                            ALU.max).then_inc(s["t2"], 1)
                        if b == 0:
                            dv.wait_ge(s["q_scale"], 1)
                            V.tensor_scalar(qmul[:, 2:3], qmul[:, 1:2], ROOT_LN_SCALE, None, ALU.mult).then_inc(s["q_scale"], 1)
                            dv.wait_ge(s["q_scale"], 2)
                        for t in range(2):
                            n = 2 * b + t
                            dv.wait_ge(s["nrm"], n + 1)
                            if t == 0:
                                dv.wait_ge(s["rot"], b + 1)
                            src = xn[:, b, :] if t == 0 else ps[:, 5 + 2 * b, :]
                            V.scalar_tensor_tensor(out=(xn, qs)[t][:, b, :], in0=src,
                                                   scalar=(qmul[:, 2:3], ROOT_LN_SCALE)[t], in1=(lnv, rstd)[t][:, b, :],
                                                   op0=ALU.mult, op1=ALU.mult).then_inc(s["qf"], 1)
                        for t in range(2):
                            split_pair(s, b, t, (xn, qs)[t][:, b, :], s["qf"], 2 * b + t + 1)
                        values(b)

                def softmax(v):
                    s = att[v]

                    def maximum(n):
                        i, c = n // 16, n % 16
                        dv.wait_ge(s["a_score"], n + 1)
                        dst = mx[i % 2][:, c:c + 1]
                        bank = ps[:, BANKS + n % BANKS, :]
                        if v == 0:
                            V.tensor_reduce(dst, bank, AX.X, ALU.max).then_inc(s["a_max"], 1)
                        else:
                            if n >= 2:
                                dv.wait_ge(s["a_max"], n - 1)
                            V.tensor_tensor_reduce(junk[n % 2][:], bank, bq_sb[:, c // 4, :], 1.0, -3e38,
                                                   ALU.add, ALU.max, dst).then_inc(s["a_max"], 1)
                        if c == 15:
                            dv.wait_ge(s["a_max"], n + 1)
                            if i >= 2:
                                dv.wait_ge(s["m_turned"], i - 1)
                            m = mx[i % 2][:].rearrange("p (q j) -> p q j", q=TT)
                            V.tensor_scalar(nmx[i % 2][:, :, 0, :], m, -1.0, None, ALU.mult).then_inc(s["nm_hi"], 1)
                            dv.wait_ge(s["nm_hi"], i + 1)
                            V.scalar_tensor_tensor(out=nmx[i % 2][:, :, 1, :], in0=m, scalar=-1.0,
                                                   in1=nmx[i % 2][:, :, 0, :].bitcast(F32), op0=ALU.mult,
                                                   op1=ALU.subtract).then_inc(s["nm_lo"], 1)

                    def invert(i):
                        dv.wait_ge(s["o_sum"], i + 1)
                        if i >= 2:
                            dv.wait_ge(s["o_spread"], i - 1)
                        V.reciprocal(inv[i % 2][:], ps[:, turn_bank(v, i), 0:TT * HG]).then_inc(s["o_inv"], 1)
                        dv.wait_ge(s["o_inv"], i + 1)
                        if i >= 1:
                            dv.wait_ge(s["o_spread"], i)
                        V.tensor_copy(diag[:].rearrange("p (c n) -> p c n", n=SP),
                                      inv[i % 2][:].unsqueeze(2).to_broadcast([P, TT * HG, SP])).then_inc(s["o_wide"], 1)

                    def normalise(i):
                        if v == BOUNDED:
                            dv.wait_ge(s["o_spread"], i + 1)
                            by = ps[:, turn_bank(v, i), :]
                        else:
                            dv.wait_ge(s["o_rec"], i + 1)
                            by = rstd[:, i % 2, :]
                        V.tensor_tensor(onorm[:, i, :], osb[i % 2][:], by, ALU.mult).then_inc(s["o_norm"], 1)

                    def add_bias(e):
                        bank = ps[:, e % BANKS, :]
                        dv.wait_ge(s["b_raw"], e + 1)
                        V.tensor_tensor(bank, bank, bk_sb[e % 16 // 4], ALU.add).then_inc(s["b_score"], 1)

                    if v != BOUNDED:
                        for n in range(NE):
                            maximum(n)
                            if v == 1 and n >= LAG:
                                add_bias(n - LAG)
                            if n % 16 == 8 and n // 16 >= 3:
                                normalise(n // 16 - 3)
                        for e in range(NE - LAG, NE):
                            if v == 1:
                                add_bias(e)
                            if e == NE - 12:
                                if v == 0:
                                    bias_maxima()
                                    bias_range()
                                normalise(NG - 3)
                        if v == 0:
                            bias_shift()
                        normalise(NG - 2)
                        normalise(NG - 1)
                    else:
                        for n in range(NE // HG):
                            i, kt = n // TT, n % TT
                            if n == 0:
                                dv.wait_ge(s["bias_exp"], TT)
                            dv.wait_ge(s["b_exp"], 4 * n + 2)
                            pair = prob[4 * n % NPROB // 2]
                            V.tensor_tensor(pair[:], pair[:], bk_sb[kt].unsqueeze(1).to_broadcast([P, 2, T]),
                                            ALU.mult).then_inc(s["dv_biased"], 2)
                            dv.wait_ge(s["b_exp"], 4 * n + 4)
                            V.tensor_tensor(prob_of(4 * n + 2), prob_of(4 * n + 2), bk_sb[kt],
                                            ALU.mult).then_inc(s["dv_biased"], 1)
                            if kt == 3 and i >= 1:
                                invert(i - 1)
                            if kt == 0 and i >= 2:
                                normalise(i - 2)
                        normalise(NG - 2)
                        invert(NG - 1)
                        normalise(NG - 1)

                if a == 0:
                    softmax(0)
                else:
                    by_bound(dv, softmax)

            def bias_maxima():
                dv.wait_ge(ld_bq, 16)
                V.tensor_reduce(bmax[:], bq_sb, AX.X, ALU.max).then_inc(s_bmax, 1)
                dv.wait_ge(s_bmax, 1)
                for t in range(TT):
                    V.tensor_scalar(diag[:, t * P:(t + 1) * P], ident, bmax[:, t:t + 1], float(P),
                                    ALU.mult, ALU.mult).then_inc(s_bdiag, 1)

            def bias_range():
                V.tensor_reduce(bmin[:], bq_sb, AX.X, ALU.min).then_inc(s_bmax, 1)
                dv.wait_ge(s_bmax, 2)
                V.tensor_tensor(brange[:], bmax[:], bmin[:], ALU.subtract).then_inc(s_bmax, 1)
                dv.wait_ge(s_bmax, 3)
                V.tensor_reduce(over[:], brange[:], AX.X, ALU.max).then_inc(s_bmax, 1)
                dv.wait_ge(s_bmax, 4)
                V.tensor_scalar(over_all[:], over[:], BIAS_RANGE, None, ALU.is_gt).then_inc(s_flag0, 1)

            def bias_shift():
                for t in range(TT):
                    V.tensor_scalar(bq_sb[:, t, :], bq_sb[:, t, :], bmax[:, t:t + 1], None,
                                    ALU.subtract).then_inc(s_bshift, 1)
                dv.wait_ge(s_bspread, 1)
                dv.wait_ge(ld_bk, 16)
                for t in range(TT):
                    V.tensor_tensor(bk_sb[t], bk_sb[t], ps[:, BANKS, :], ALU.subtract).then_inc(s_bks, 1)
                dv.wait_ge(s_over, 1)
                V.tensor_tensor(smax[:, 2:3], ps[0:1, BANKS + 1, 0:1], smax[:, 1:2], ALU.add).then_inc(s_flag0, 1)
                dv.wait_ge(s_flag0, 4)
                V.tensor_scalar(flag[:], smax[:, 2:3], 0.0, None, ALU.is_gt).then_inc(s_flag, 1)

            dv.wait_ge(ld_w[0], 16)
            V.tensor_reduce(smax[:, 0:1], wt["scales"][0:1, :], AX.X, ALU.max).then_inc(s_flag0, 1)
            dv.wait_ge(s_flag0, 1)
            V.tensor_scalar(smax[:, 1:2], smax[:, 0:1], float(np.log(BOUND)), None, ALU.is_gt).then_inc(s_flag0, 1)
            dv.wait_ge(ld_w[0], 16)
            V.tensor_copy(ln_a[:, 0, :], vec[:, VEC["g"]:VEC["g"] + 2]).then_inc(s_modok, 1)
            V.tensor_copy(ln_b[:, 0, :], vec[:, VEC["b"]:VEC["b"] + 2]).then_inc(s_modok, 1)
            V.tensor_copy(gate[:, 0, :], wt["cond"]).then_inc(s_modok, 1)
            dv.wait_ge(s_modok, 2)
            for b in range(B):
                norm(0, b)
            loaded(dv, "l0_bq")
            for b in range(B):
                dv.wait_ge(s_k0, b + 1)
                V.tensor_reduce(kmx[:, b, 0:1], ps[:, 2 + b, :], AX.X, ALU.max).then_inc(s_kstep, 1)
                dv.wait_ge(s_kstep, 2 * b + 1)
                V.tensor_tensor(kmx[:, b, 1:2], kmx[:, b, 0:1], v1("bk"), ALU.add).then_inc(s_kstep, 1)
                dv.wait_ge(s_kstep, 2 * b + 2)
                V.tensor_tensor(kmx[:, b, 2:3], v1("bk"), kmx[:, b, 1:2], ALU.subtract).then_inc(s_kb, 1)
            h8 = "p (h d) -> p h d"
            for b in range(B):
                dv.wait_ge(s_q0, b + 1)
                V.tensor_tensor(qs[:, b, :].rearrange("p (t n) -> p t n", t=TT),
                                ps[:, 4 + b, :].rearrange("p (t n) -> p t n", t=TT),
                                wt["l0_bq"].unsqueeze(1).to_broadcast([P, TT, P]), ALU.add).then_inc(s_qstep, 1)
                dv.wait_ge(s_qstep, 2 * b + 1)
                V.tensor_reduce(qmx[:, b, :], qs[:, b, :].rearrange(h8, d=DH), AX.X, ALU.max).then_inc(s_qstep, 1)
                dv.wait_ge(s_qstep, 2 * b + 2)
                V.tensor_tensor(qd[:, b, :].rearrange(h8, d=DH), qs[:, b, :].rearrange(h8, d=DH),
                                qmx[:, b, :].unsqueeze(2).to_broadcast([P, TT * H, DH]), ALU.subtract).then_inc(s_qd, 1)
            dv.wait_ge(s_modmm, 1)
            V.tensor_tensor(mods[:], ps[:, 7, 0:2 * NMOD].rearrange("p (m b) -> p m b", b=B),
                            vec[:, VEC["modb"]:VEC["modb"] + NMOD].unsqueeze(2).to_broadcast([P, NMOD, B]),
                            ALU.add).then_inc(s_mod, 1)
            dv.wait_ge(s_mod, 1)
            V.tensor_scalar(scale1[:], mods[:, 0:7, :], 1.0, None, ALU.add).then_inc(s_mod, 1)
            V.tensor_copy(gate[:, 1:NUP, :], mods[:, 14:20, :]).then_inc(s_mod, 1)
            dv.wait_ge(s_mod, 3)
            V.tensor_tensor(ln_a[:, 1:NLN, :], scale1[:],
                            vec[:, VEC["g"] + 2:VEC["g"] + 2 * NLN].rearrange("p (n b) -> p n b", b=B),
                            ALU.mult).then_inc(s_modok, 1)
            V.tensor_tensor(ln_t[:], scale1[:], vec[:, VEC["b"] + 2:VEC["b"] + 2 * NLN].rearrange("p (n b) -> p n b", b=B),
                            ALU.mult).then_inc(s_mod, 1)
            dv.wait_ge(s_modok, 3)
            V.tensor_tensor(gate_b[:], gate[:], vec[:, VEC["outb"]:VEC["outb"] + 2 * NUP].rearrange("p (n b) -> p n b", b=B),
                            ALU.mult).then_inc(s_modok, 1)
            dv.wait_ge(s_mod, 4)
            V.tensor_tensor(ln_b[:, 1:NLN, :], ln_t[:], mods[:, 7:14, :], ALU.add).then_inc(s_modok, 1)
            for b in range(B):
                dv.wait_ge(s_v0, b + 1)
                dv.wait_ge(s_var, nth(0, b))
                V.tensor_tensor(vtok[:, b, :].rearrange("p (t n) -> p t n", t=TT),
                                ps[:, b, :].rearrange("p (t n) -> p t n", t=TT),
                                wt["l0_bv"].unsqueeze(1).to_broadcast([P, TT, P]), ALU.add).then_inc(s_vtok, 1)
            for b in range(B):
                dv.wait_ge(s_qe, b + 1)
                V.tensor_reduce(qsum[:, b, :], qe[:, b, :].rearrange(h8, d=DH), AX.X, ALU.add).then_inc(s_qstep, 1)
                dv.wait_ge(s_qstep, 2 * b + 5)
                V.reciprocal(qsum[:, b, :], qsum[:, b, :]).then_inc(s_qstep, 1)
                dv.wait_ge(s_qstep, 2 * b + 6)
                V.tensor_tensor(qp[:, b, :].rearrange(h8, d=DH), qe[:, b, :].rearrange(h8, d=DH),
                                qsum[:, b, :].unsqueeze(2).to_broadcast([P, TT * H, DH]), ALU.mult).then_inc(s_qp, 1)
            for b in range(B):
                dv.wait_ge(s_ke, b + 1)
                V.reciprocal(kmx[:, b, 0:1], kmx[:, b, 3:4]).then_inc(s_kstep, 1)
                dv.wait_ge(s_kstep, b + 5)
                dv.wait_ge(s_ctx, b + 1)
                V.scalar_tensor_tensor(out=ctxm[:, b, :], in0=ps[:, b, 0:P], scalar=kmx[:, b, 0:1], in1=blocks,
                                       op0=ALU.mult, op1=ALU.mult).then_inc(s_ctxm, 1)
            for b in range(B):
                dv.wait_ge(s_qTp, b + 1)
                V.tensor_copy(qT[:, b, :], ps[:, 4 + b, :]).then_inc(s_qT, 1)
            dv.wait_ge(s_modok, 6)
            for b in range(B):
                norm(1, b)
            dv.wait_ge(s_hbmm, 1)
            V.tensor_tensor(hid_b[:], ps[:, 7, 0:2 * NHID].rearrange("p (c b) -> p c b", b=B),
                            vec[:, VEC["hidden"]:VEC["hidden"] + NHID].unsqueeze(2).to_broadcast([P, NHID, B]),
                            ALU.add).then_inc(s_hb, 1)
            update_and_norm(0, s_o0, 0, 2)
            update_and_norm(1, s_m2, 0, 3)
            update_and_norm(2, s_m2, 2, 4)
            attention(0)
            update_and_norm(3, att[0]["proj"], 0, 5)
            update_and_norm(4, s_m2, 4, 6)
            attention(1)
            update_and_norm(5, att[1]["proj"], 0, 7)
            update_and_norm(6, s_m2, 6, None)

        @block.scalar
        def _(act):
            A = nc.scalar.activation

            def log_exp_table():
                nc.scalar.preload_act_table_set("natural_log_exp_and_others")

            def norm(n, terms=1):
                log_exp_table()

                def square(b):
                    act.wait_ge(s_xc, nth(n, b))
                    A(sq[:, b, :], ps[:, b, :], ACT.Square).then_inc(s_sq, 1)

                square(0)
                if terms == 1:
                    square(1)
                for b in range(B):
                    if terms > 1 and b == 1:
                        square(1)
                    act.wait_ge(s_var, nth(n, b))
                    A(lnv[:, b, :], ps[:, 2 + b, :], ACT.Ln, bias=v1("eps", n)).then_inc(s_lnv, 1)
                    act.wait_ge(s_lnv, nth(n, b))
                    A(rstd[:, b, :], lnv[:, b, :], ACT.Exp, scale=-0.5).then_inc(s_rstd, 1)

            def mlp(m):
                _, nb, _, _, bias, func, _ = MLPS[m]
                base = mlp_base[m]
                if m == 0:
                    act.wait_ge(s_hb, 1)
                for b in range(B):
                    for j in range(nb):
                        act.wait_ge(s_m1, base + b * nb + j + 1)
                        A(hid[:, j, b, :], ps[:, 4 + (b * nb + j) % 4, :], func,
                          bias=hid_b[:, bias + j, b:b + 1]).then_inc(s_hid, 1)

            def attention(a):
                s = att[a]
                if a == 0:
                    for n in range(4):
                        b, t = n // 2, n % 2
                        act.wait_ge(s["qf"], n + 1)
                        A(qh[t][:, b, :], xn[:, b, :] if t == 0 else junk[b][:], ACT.Copy).then_inc(s["hi"], 1)
                        if t == 1:
                            act.wait_ge(s["v_mm"], b + 1)
                            act.wait_ge(s_ones, RING + 2)
                            for tile in range(TT):
                                A(vx[:, b * GB:(b + 1) * GB, tile, :, 0:DH],
                                  ps[:, b, tile * P:(tile + 1) * P].rearrange("p (g j d) -> p g j d", g=GB, j=HG),
                                  ACT.Copy).then_inc(s["v_ready"], 1)
                else:
                    A(qmul[:, 1:2], qmul[:, 0:1], ACT.Exp).then_inc(s["q_scale"], 1)
                    for b in range(B):
                        act.wait_ge(s_ln, nth(6, b))
                        for t in range(2):
                            act.wait_ge(s["qkv"], 2 * b + t + 1)
                            A((xc, sq)[t][:, b, :], ps[:, 4 + 2 * b + t, :], ACT.Square,
                              bias=v1("l3_bq") if t == 0 else 0.0).then_inc(s["t1"], 1)
                        A(xn[:, b, :], ps[:, 4 + 2 * b, :], ACT.Identity, bias=v1("l3_bq")).then_inc(s["rot"], 1)
                        for t in range(2):
                            n = 2 * b + t
                            act.wait_ge(s["t2"], n + 1)
                            A((xc, sq)[t][:, b, :], (lnv, rstd)[t][:, b, :], ACT.Ln, scale=LN_SCALE).then_inc(s["ln"], 1)
                            act.wait_ge(s["ln"], n + 1)
                            A((lnv, rstd)[t][:, b, :], (xc, sq)[t][:, b, :], ACT.Exp, scale=-0.5).then_inc(s["nrm"], 1)
                        for t in range(2):
                            act.wait_ge(s["qf"], 2 * b + t + 1)
                            A(qh[t][:, b, :], (xn, qs)[t][:, b, :], ACT.Copy).then_inc(s["hi"], 1)

                def softmax(v):
                    s = att[v]
                    ring = 2 * BANKS if v == BOUNDED else BANKS

                    def m_row(i):
                        act.wait_ge(s["m_turned"], i + 1)
                        if i >= 2:
                            act.wait_ge(s[f"mrow_in{i % 2}"], 32 * (i // 2))
                        A(mrow[i % 2][:], ps[0:2 * HG, 7, :], ACT.Copy).then_inc(s["m_row"], 1)

                    def copy_o(i):
                        act.wait_ge(s["pv"], TT * (i + 1))
                        if i >= 2:
                            act.wait_ge(s["o_norm"], i - 1)
                        A(osb[i % 2][:], ps[:, out_bank(v, i), :], ACT.Copy).then_inc(s["o_copied"], 1)

                    def invert(i):
                        act.wait_ge(s["o_spread"], i + 1)
                        A(lnv[:, i % 2, :], ps[:, 7, :], ACT.Ln).then_inc(s["o_log"], 1)
                        act.wait_ge(s["o_log"], i + 1)
                        if i >= 2:
                            act.wait_ge(s["o_norm"], i - 1)
                        A(rstd[:, i % 2, :], lnv[:, i % 2, :], ACT.Exp, scale=-1.0).then_inc(s["o_rec"], 1)

                    if v != BOUNDED:
                        m_row(0)
                    if v == BOUNDED:
                        for t in range(TT):
                            act.wait_ge(s_bks, t + 1)
                            A(bk_sb[t], bk_sb[t], ACT.Exp).then_inc(s["bias_exp"], 1)
                        for n in range(NE // 2):
                            i, c = n // 8, n % 8
                            act.wait_ge(s["b_raw"], 2 * n + 2)
                            if 2 * n >= NPROB:
                                act.wait_ge(s["pv"], (2 * n - NPROB) // 4 + 1)
                            A(prob[n % (NPROB // 2)][:], ps[:, 2 * n % ring:2 * n % ring + 2, :],
                              ACT.Exp).then_inc(s["b_exp"], 2)
                            if c == 5 and i >= 1:
                                copy_o(i - 1)
                    else:
                        for e in range(NE):
                            i = e // 16
                            if v == 1:
                                act.wait_ge(s["b_score"], e + 1)
                            else:
                                act.wait_ge(s["b_raw"], e + 1)
                            if e >= NPROB:
                                act.wait_ge(s["pv"], (e - NPROB) // 4 + 1)
                            A(prob_of(e), ps[:, e % ring, :], ACT.Exp).then_inc(s["b_exp"], 1)
                            if e % 16 == 4 and i >= 1:
                                copy_o(i - 1)
                            if e % 16 == 8 and i + 1 < NG:
                                m_row(i + 1)
                            if e % 16 == 13 and i >= 1:
                                invert(i - 1)
                    copy_o(NG - 1)
                    if v != BOUNDED:
                        invert(NG - 1)

                if a == 0:
                    softmax(0)
                else:
                    by_bound(act, softmax)

            loaded(act, "cond")
            A(silc[:], wt["cond"], ACT.Silu).then_inc(s_silc, 1)
            norm(0)
            for b in range(B):
                act.wait_ge(s_kb, b + 1)
                A(ke[:, b, :], ps[:, 2 + b, :], ACT.Exp, bias=kmx[:, b, 2:3], accum_out=kmx[:, b, 3:4]).then_inc(s_ke, 1)
            for b in range(B):
                act.wait_ge(s_qd, b + 1)
                A(qe[:, b, :], qd[:, b, :], ACT.Exp).then_inc(s_qe, 1)
            for b in range(B):
                act.wait_ge(s_ktT, b + 1)
                A(ktok[:, b, :], ps[:, 6 + b, :], ACT.Copy).then_inc(s_ktok, 1)
            for b in range(B):
                act.wait_ge(s_y, b + 1)
                act.wait_ge(s_qd, b + 1)
                A(ysb[:, b, :], ps[:, 2 + b, :], ACT.Copy).then_inc(s_ysb, 1)
            norm(1)
            for b in range(B):
                act.wait_ge(s_ln, nth(1, b))
                A(silh[:, b, :], xm[:, b, :], ACT.Silu, bias=ln_b[:, 1, b:b + 1]).then_inc(s_silh, 1)
            norm(2)
            mlp(0)
            norm(3)
            mlp(1)
            norm(4, 2)
            attention(0)
            norm(5, 4)
            mlp(2)
            norm(6, 4)
            act.wait_ge(s_qmul, 1)
            attention(1)
            norm(7, 4)
            mlp(3)

        @block.gpsimd
        def _(gp):
            G = nc.gpsimd
            for u in range(RING):
                G.memset(kg[u][:].bitcast(F32), 0.0).then_inc(s_ones, 1)
            G.memset(vx[:, :, :, :, DH:DH + 1], 1.0).then_inc(s_ones, 1)
            G.memset(vx[:, :, :, :, DH + 1:SP], 0.0).then_inc(s_ones, 1)
            gp.wait_ge(ld_w[0], 16)
            G.tensor_scalar(qmul[:, 0:1], v1("scale"), float(np.log(100.0)), None, ALU.min).then_inc(s_qmul, 1)

            def biased(k):
                for b in range(B):
                    x_ready(gp, k, b)
                    G.tensor_scalar(state_b[:, b, :], state[k % 2][:, b, :], gate_b[:, k, b:b + 1], None,
                                    ALU.add).then_inc(s_xb, 1)

            def attention(a):
                s = att[a]

                def softmax(v):
                    s = att[v]

                    if v == BOUNDED:
                        gp.wait_ge(s["bias_exp"], TT)
                        for n in range(NE // HG):
                            i, kt = n // TT, n % TT
                            gp.wait_ge(s["b_exp"], 4 * n + 4)
                            G.tensor_tensor(prob_of(4 * n + 3), prob_of(4 * n + 3), bk_sb[kt],
                                            ALU.mult).then_inc(s["gp_biased"], 1)
                if a == 1:
                    by_bound(gp, softmax)

            gp.wait_ge(s_modok, 6)
            biased(0)
            biased(1)
            biased(2)
            attention(0)
            biased(5)
            attention(1)
            biased(6)


def kernel(**inputs):
    import concourse.bacc as bacc
    from concourse.bass_utils import run_bass_kernel_spmd

    d = {k: np.asarray(v) for k, v in inputs.items()}
    f = np.float32

    def strips(w):
        o = np.zeros((GB, HG, SP, P), f)
        o[:, :, :DH] = w.reshape(GB, HG, DH, P)
        return o.reshape(GB, P, P).transpose(1, 0, 2).reshape(P, GB * P)

    def blocked(w):
        return w.reshape(-1, P, w.shape[1]).transpose(1, 0, 2).reshape(P, -1)

    inv = 1.0 / 10000.0 ** (np.arange(0, DH, 2, dtype=f) / f(DH))
    ang = np.outer(np.arange(T, dtype=f), inv.astype(f)).astype(f)
    ang = np.concatenate([ang, ang], -1).T
    cos, sin = np.cos(ang).astype(f), np.sin(ang).astype(f)
    sin[: DH // 2] *= -1
    cos, sin = np.tile(cos, (H, 1)), np.tile(sin, (H, 1))
    turn = np.concatenate([np.arange(1, DH, 2), np.arange(0, DH, 2)])
    turn = (np.arange(H)[:, None] * DH + turn[None]).ravel()
    root = f(DH ** -0.5)

    e0, e1 = d["L0_cond_emb_W"].reshape(P, 2, P), d["L1_cond_ada_w"].reshape(P, 6, P)
    e2, e3 = d["L2_cond_ada_W"].reshape(P, 6, P), d["L3_cond_ada_w"].T.reshape(P, 6, P)
    b0, b1 = d["L0_cond_emb_b"].reshape(2, P), d["L1_cond_ada_b"].reshape(6, P)
    b2, b3 = d["L2_cond_ada_b"].reshape(6, P), d["L3_cond_ada_b"].reshape(6, P)
    order = [(0, 0), (1, 1), (1, 4), (2, 1), (2, 4), (3, 2), (3, 3), (0, 1), (1, 0), (1, 3), (2, 0), (2, 3), (3, 4), (3, 5),
             (1, 2), (1, 5), (2, 2), (2, 5), (3, 0), (3, 1)]
    E, Bm = (e0, e1, e2, e3), (b0, b1, b2, b3)
    mod = np.stack([E[l][:, j] for l, j in order], 1)
    modb = np.stack([Bm[l][j] for l, j in order], 1)
    one, zero = np.ones(P, f), np.zeros(P, f)

    def twice(cols):
        return np.stack([c for c in cols for _ in range(B)], 1)

    vec = np.zeros((P, NVEC), f)

    def put(name, cols):
        cols = cols.reshape(P, -1)
        vec[:, VEC[name]:VEC[name] + cols.shape[1]] = cols

    put("modb", modb)
    put("g", twice([d["L0_cond_norm_g"], d["L0_cond_sn_g"], one, one, d["L2_cond_norm1_g"], d["L2_cond_norm2_g"], one, one]))
    put("b", twice([d["L0_cond_norm_b"], d["L0_cond_sn_b"], zero, zero, d["L2_cond_norm1_b"], d["L2_cond_norm2_b"], zero, zero]))
    put("outb", twice([d["L0_cond_out_b"], d["L1_cond_ssm_b2"], d["L1_cond_ff_b2"], zero, zero, d["L3_cond_proj_b"],
                       d["L3_cond_fc2_b"]]))
    put("eps", np.tile(np.array(LN_EPS, f), (P, 1)))
    put("bk", d["L0_cond_bk"])
    put("hidden", np.concatenate([d["L1_cond_ssm_b1"], d["L1_cond_ff_b1"], np.zeros(4 * P, f), d["L3_cond_fc1_b"]])
        .reshape(NHID, P).T)
    put("l3_bq", d["L3_cond_q_bias"])
    put("scale", np.repeat(d["L3_cond_scale_mul"].reshape(H), DH))

    def wide(row):
        return np.tile(row[None], (P, 1))

    blk = np.kron(np.eye(H, dtype=f), np.ones((DH, DH), f))
    sel = np.zeros((P, HG), f)
    for j in range(HG):
        sel[SP * j + DH, j] = 1
    qkv = d["L3_cond_qkv_w"].T
    parts = {
        "ones": np.full((P, P), 1.0 / P, f),
        "center": np.eye(P, dtype=f) - f(1.0 / P), "cond": d["cond_1024"].T, "scales": wide(d["L3_cond_scale_mul"].reshape(H)),
        "vec": vec, "mod0": mod[:, 0:2].reshape(P, -1),
        "mod": mod[:, 2:].reshape(P, -1), "ident": np.eye(P, dtype=f), "blocks": blk, "sumsel": sel, "sumwide": np.repeat(sel, SP, 1),
        "l0_q": d["L0_cond_Wq"], "l0_k": d["L0_cond_Wk"], "l0_v": d["L0_cond_Wv"], "l0_bq": wide(d["L0_cond_bq"]),
        "l0_bv": wide(d["L0_cond_bv"]), "l0_o": d["L0_cond_out_W"],
        "l1_a": d["L1_cond_ssm_w1"], "l1_b": d["L1_cond_ssm_w2"], "l1_c": d["L1_cond_ff_w1"], "l1_d": blocked(d["L1_cond_ff_w2"]),
        "cos": cos, "sin": sin, "qcos": cos * root, "qsin": sin * root,
        "l2_q": d["L2_cond_Wq"], "l2_qr": d["L2_cond_Wq"][:, turn], "l2_k": d["L2_cond_Wk"], "l2_kr": d["L2_cond_Wk"][:, turn],
        "l2_v": d["L2_cond_Wv"], "l2_o": strips(d["L2_cond_Wo"]), "l2_a": d["L2_cond_W1"], "l2_b": blocked(d["L2_cond_W2"]),
        "l3_q": qkv[:, :P], "l3_k": qkv[:, P:2 * P], "l3_v": qkv[:, 2 * P:], "l3_bv": wide(d["L3_cond_v_bias"]),
        "l3_o": strips(d["L3_cond_proj_w"].T), "l3_a": d["L3_cond_fc1_w"].T, "l3_b": blocked(d["L3_cond_fc2_w"].T),
    }
    arrays = {"xT": np.ascontiguousarray(d["x"].transpose(2, 0, 1))}
    for n, cols in enumerate(W_LOADS):
        arrays[f"weights{n}_in"] = np.ascontiguousarray(np.concatenate([parts[name] for name, _ in cols], 1))
    bias = d["fside_1x1xSxS_0"][0, 0]
    arrays["bias_by_query"] = np.ascontiguousarray(bias.reshape(TT, P, T).transpose(1, 0, 2))
    arrays["bias_by_key"] = np.ascontiguousarray(bias.T.reshape(TT, P, T).transpose(1, 0, 2))

    arrays["rows_q"] = np.zeros((NG * HG * DH, T), f)
    arrays["rows_k"] = np.tile((np.arange(DH) < 2).astype(f)[None, :, None], (NG * HG, 1, T)).reshape(-1, T)

    nc = bacc.Bacc("TRN2", target_bir_lowering=False, num_devices=1)
    ap = {n: nc.dram_tensor(n, a.shape, F32, kind="ExternalInput").ap() for n, a in arrays.items()}
    out = nc.dram_tensor("outT", [P, B, T], F32, kind="ExternalOutput").ap()
    build(nc, ap["xT"], [ap[f"weights{n}_in"] for n in range(len(W_LOADS))], ap["bias_by_query"], ap["bias_by_key"], ap["rows_q"],
          ap["rows_k"], out)
    r = run_bass_kernel_spmd(nc, [arrays], core_ids=[0])
    return np.ascontiguousarray(r.results[0]["outT"].transpose(1, 2, 0))
```
